# Optimizing a Trainium2 kernel written in Bass

```python
import numpy as np
import jax
import jax.numpy as jnp

def _softmax(x, axis=-1):
    return jax.nn.softmax(x, axis=axis)

def _gelu(x):
    return jax.nn.gelu(x, approximate=True)

def _silu(x):
    return jax.nn.silu(x)

def _sigmoid(x):
    return jax.nn.sigmoid(x)

def _layernorm(x, axis=-1, eps=1e-05):
    m = jnp.mean(x, axis=axis, keepdims=True)
    v = jnp.var(x, axis=axis, keepdims=True)
    return (x - m) / jnp.sqrt(v + eps)

def _scatter_add(tgt, idx, src, axis=0):
    return tgt.at[idx].add(src)

def _segment_sum(src, seg, n):
    return jax.ops.segment_sum(src, seg, n)
kernel_name = 'mk_pixart_seq_d4_seqx_r8_3ad432'

def setup_inputs(seed: int=0):
    np.random.seed(seed)
    _w = jnp.asarray

    def _rec_inputs():
        import jax
        import jax.numpy as jnp
        _rk = jax.random.key(seed)
        x = -0.0003929 + 0.9999 * jax.random.normal(jax.random.fold_in(_rk, 1), (128, 64, 128), jnp.float32)
        _lenS = 64 - jax.random.randint(jax.random.fold_in(_rk, 7), (128,), 0, max(1, 64 // 4) + 1, jnp.int32)
        _lenS2 = 64 - jax.random.randint(jax.random.fold_in(_rk, 8), (128,), 0, max(1, 64 // 4) + 1, jnp.int32)
        cond_1024 = 0.00782532 + 1.00527 * jax.random.normal(jax.random.fold_in(_rk, 11), (128, 128), jnp.float32)
        _ctx_1024P = jax.random.normal(jax.random.fold_in(_rk, 12), (128, 16, 128), jnp.float32)
        _ctx_1024c = jax.random.dirichlet(jax.random.fold_in(_rk, 512), 0.3 * jnp.ones((16,), jnp.float32), (128, 64))
        _ctx_1024t = jnp.einsum('bsk,bkd->bsd', _ctx_1024c, _ctx_1024P)
        _ctx_1024t = _ctx_1024t * jax.lax.rsqrt(jnp.mean(jnp.square(_ctx_1024t)) + 1e-12) * 0.953939
        ctx_1024 = -0.000761806 + 0.999296 * (_ctx_1024t + 0.3 * jax.random.normal(jax.random.fold_in(_rk, 612), (128, 64, 128), jnp.float32))
        _validS = jnp.arange(64)[None, :] < _lenS[:, None]
        _validS2 = jnp.arange(64)[None, :] < _lenS2[:, None]
        _causal = jnp.tril(jnp.ones((64, 64), dtype=bool))
        mask_BxS2_bf0 = jnp.logical_not(jnp.ones((128, 64), dtype=bool))
        return (x, cond_1024, ctx_1024, mask_BxS2_bf0)
    x, cond_1024, ctx_1024, mask_BxS2_bf0 = _rec_inputs()

    def _L0_xcond_setup():
        import jax, jax.numpy as jnp
        import numpy as np
        H = 128
        RH = 2 * H
        E = 3
        B, T, P = (8, 256, 64)
        LN_EPS = 1e-05

        def _layer_norm(x, gamma, beta):
            mu = jnp.mean(x, axis=-1, keepdims=True)
            var = jnp.mean(jnp.square(x - mu), axis=-1, keepdims=True)
            return (x - mu) * jax.lax.rsqrt(var + LN_EPS) * gamma + beta
        key = jax.random.key(seed)
        ks = jax.random.split(key, 24)
        s = lambda fan_in: 1.0 / np.sqrt(fan_in)
        inp = {'mix_hidden_states': jax.random.normal(ks[0], (B, T, H), jnp.float32), 'global_anchor': jax.random.normal(ks[1], (B, H), jnp.float32), 'prototype_bank': jax.random.normal(ks[2], (B, P, H), jnp.float32), 'ln_gamma': jnp.ones((H,), jnp.float32), 'ln_beta': jnp.zeros((H,), jnp.float32), 'Wq': jax.random.normal(ks[3], (H, H), jnp.float32) * s(H), 'Wk': jax.random.normal(ks[4], (H, H), jnp.float32) * s(H), 'Wv': jax.random.normal(ks[5], (H, H), jnp.float32) * s(H), 'router_W': jax.random.normal(ks[6], (3 * H, E), jnp.float32) * s(3 * H), 'router_b': jnp.zeros((E,), jnp.float32), 'e_w1': jax.random.normal(ks[7], (E, 3 * H, RH), jnp.float32) * s(3 * H), 'e_b1': jnp.zeros((E, RH), jnp.float32), 'e_w2': jax.random.normal(ks[8], (E, RH, H), jnp.float32) * s(RH), 'e_b2': jnp.zeros((E, H), jnp.float32), 'gate_w1': jax.random.normal(ks[9], (3 * H, H), jnp.float32) * s(3 * H), 'gate_b1': jnp.zeros((H,), jnp.float32), 'gate_w2': jax.random.normal(ks[10], (H, H), jnp.float32) * s(H), 'gate_b2': jnp.zeros((H,), jnp.float32), 'out_w': jax.random.normal(ks[11], (H, H), jnp.float32) * s(H), 'out_b': jnp.zeros((H,), jnp.float32)}
        return inp
    _L0_xcond_all = _L0_xcond_setup()
    _L0_xcond_in = {k: v for k, v in _L0_xcond_all.items() if k in ('ln_gamma', 'ln_beta', 'Wq', 'Wk', 'Wv', 'router_W', 'router_b', 'e_w1', 'e_b1', 'e_w2', 'e_b2', 'gate_w1', 'gate_b1', 'gate_w2', 'gate_b2', 'out_w', 'out_b')}
    del _L0_xcond_all

    def _L1_xcond_setup():
        import jax, jax.numpy as jnp
        import numpy as np
        D, H, B, N, S = (128, 16, 4, 128, 77)
        HD = D // H
        DF = 4 * D
        EPS = 1e-06
        SCALE = HD ** (-0.5)

        def _ln(x):
            m = jnp.mean(x, axis=-1, keepdims=True)
            v = jnp.mean((x - m) ** 2, axis=-1, keepdims=True)
            return (x - m) / jnp.sqrt(v + EPS)
        key = jax.random.key(seed)
        ks = jax.random.split(key, 24)
        s = 0.02
        inp = {'x': jax.random.normal(ks[0], (B, N, D), jnp.float32), 't_emb': jax.random.normal(ks[1], (B, D), jnp.float32), 'context': jax.random.normal(ks[2], (B, S, D), jnp.float32), 'context_mask': jnp.zeros((B, S), jnp.bool_), 'ada_w': jax.random.normal(ks[3], (D, 6 * D), jnp.float32) * s, 'ada_b': jnp.zeros((6 * D,), jnp.float32), 'qkv_w': jax.random.normal(ks[4], (D, 3 * D), jnp.float32) * s, 'qkv_b': jnp.zeros((3 * D,), jnp.float32), 'sa_proj_w': jax.random.normal(ks[5], (D, D), jnp.float32) * s, 'sa_proj_b': jnp.zeros((D,), jnp.float32), 'q_w': jax.random.normal(ks[6], (D, D), jnp.float32) * s, 'q_b': jnp.zeros((D,), jnp.float32), 'kv_w': jax.random.normal(ks[7], (D, 2 * D), jnp.float32) * s, 'kv_b': jnp.zeros((2 * D,), jnp.float32), 'ca_proj_w': jax.random.normal(ks[8], (D, D), jnp.float32) * s, 'ca_proj_b': jnp.zeros((D,), jnp.float32), 'fc1_w': jax.random.normal(ks[9], (D, DF), jnp.float32) * s, 'fc1_b': jnp.zeros((DF,), jnp.float32), 'fc2_w': jax.random.normal(ks[10], (DF, D), jnp.float32) * s, 'fc2_b': jnp.zeros((D,), jnp.float32)}
        return inp
    _L1_xcond_all = _L1_xcond_setup()
    _L1_xcond_in = {k: v for k, v in _L1_xcond_all.items() if k in ('ada_w', 'ada_b', 'qkv_w', 'qkv_b', 'sa_proj_w', 'sa_proj_b', 'q_w', 'q_b', 'kv_w', 'kv_b', 'ca_proj_w', 'ca_proj_b', 'fc1_w', 'fc1_b', 'fc2_w', 'fc2_b')}
    del _L1_xcond_all

    def _L2_xcond_setup():
        import jax, jax.numpy as jnp
        import numpy as np
        LN_EPS = 1e-06

        def _ln(x):
            mu = jnp.mean(x, axis=-1, keepdims=True)
            var = jnp.var(x, axis=-1, keepdims=True)
            return (x - mu) * jax.lax.rsqrt(var + LN_EPS)
        key = jax.random.key(seed)
        H, NH = (128, 16)
        B, N, S = (4, 128, 77)
        MLP = int(H * 4.0)
        ks = jax.random.split(key, 20)
        s = 1.0 / np.sqrt(H)
        return {'x': jax.random.normal(ks[0], (B, N, H), jnp.float32), 'c': jax.random.normal(ks[1], (B, H), jnp.float32), 'context': jax.random.normal(ks[2], (B, S, H), jnp.float32), 'W_mod': jax.random.normal(ks[3], (H, 6 * H), jnp.float32) * s, 'b_mod': jnp.zeros((6 * H,), jnp.float32), 'W_qkv': jax.random.normal(ks[4], (H, 3 * H), jnp.float32) * s, 'b_qkv': jnp.zeros((3 * H,), jnp.float32), 'W_proj': jax.random.normal(ks[5], (H, H), jnp.float32) * s, 'b_proj': jnp.zeros((H,), jnp.float32), 'W_qc': jax.random.normal(ks[6], (H, H), jnp.float32) * s, 'b_qc': jnp.zeros((H,), jnp.float32), 'W_kvc': jax.random.normal(ks[7], (H, 2 * H), jnp.float32) * s, 'b_kvc': jnp.zeros((2 * H,), jnp.float32), 'W_cproj': jax.random.normal(ks[8], (H, H), jnp.float32) * s, 'b_cproj': jnp.zeros((H,), jnp.float32), 'W_mlp1': jax.random.normal(ks[9], (H, MLP), jnp.float32) * s, 'b_mlp1': jnp.zeros((MLP,), jnp.float32), 'W_mlp2': jax.random.normal(ks[10], (MLP, H), jnp.float32) * (1.0 / np.sqrt(MLP)), 'b_mlp2': jnp.zeros((H,), jnp.float32)}
    _L2_xcond_all = _L2_xcond_setup()
    _L2_xcond_in = {k: v for k, v in _L2_xcond_all.items() if k in ('W_mod', 'b_mod', 'W_qkv', 'b_qkv', 'W_proj', 'b_proj', 'W_qc', 'b_qc', 'W_kvc', 'b_kvc', 'W_cproj', 'b_cproj', 'W_mlp1', 'b_mlp1', 'W_mlp2', 'b_mlp2')}
    del _L2_xcond_all

    def _L3_xcond_setup():
        import jax, jax.numpy as jnp
        import numpy as np
        import math
        D_MODEL = 128
        N_HEADS = 16
        HEAD_DIM = D_MODEL // N_HEADS
        D_FF = 512
        EPS = 1e-05
        ROPE_BASE = 10000.0

        def _rope(t):
            L, Dh = (t.shape[1], t.shape[-1])
            half = Dh // 2
            inv_freq = 1.0 / ROPE_BASE ** (jnp.arange(half, dtype=t.dtype) / half)
            ang = jnp.arange(L, dtype=t.dtype)[:, None] * inv_freq[None, :]
            cos = jnp.cos(ang)[None, :, None, :]
            sin = jnp.sin(ang)[None, :, None, :]
            t1, t2 = (t[..., :half], t[..., half:])
            return jnp.concatenate([t1 * cos - t2 * sin, t2 * cos + t1 * sin], axis=-1)

        def _adaln(x, emb, w, b):
            e = emb[:, 0, :]
            gb = e @ w.T + b
            gamma, beta = jnp.split(gb, 2, axis=-1)
            mu = x.mean(-1, keepdims=True)
            var = x.var(-1, keepdims=True)
            xn = (x - mu) * jax.lax.rsqrt(var + EPS)
            return xn * (1.0 + gamma[:, None, :]) + beta[:, None, :]

        def _attn(q, k, v):
            scale = 1.0 / math.sqrt(HEAD_DIM)
            scores = jnp.einsum('bqhd,bkhd->bhqk', q, k) * scale
            w = jax.nn.softmax(scores, axis=-1)
            out = jnp.einsum('bhqk,bkhd->bqhd', w, v)
            B, Lq = (out.shape[0], out.shape[1])
            return out.reshape(B, Lq, D_MODEL)
        key = jax.random.key(seed)
        ks = jax.random.split(key, 24)
        s = 0.02
        inp = {'x': jax.random.normal(ks[0], (2, 256, D_MODEL), jnp.float32), 'noise_emb': jax.random.normal(ks[1], (2, 1, D_MODEL), jnp.float32), 'context': jax.random.normal(ks[2], (2, 128, D_MODEL), jnp.float32), 'ln1_w': jax.random.normal(ks[3], (2 * D_MODEL, D_MODEL), jnp.float32) * s, 'ln1_b': jax.random.normal(ks[4], (2 * D_MODEL,), jnp.float32) * s, 'ln2_w': jax.random.normal(ks[5], (2 * D_MODEL, D_MODEL), jnp.float32) * s, 'ln2_b': jax.random.normal(ks[6], (2 * D_MODEL,), jnp.float32) * s, 'ln3_w': jax.random.normal(ks[7], (2 * D_MODEL, D_MODEL), jnp.float32) * s, 'ln3_b': jax.random.normal(ks[8], (2 * D_MODEL,), jnp.float32) * s, 'qkv_w': jax.random.normal(ks[9], (3 * D_MODEL, D_MODEL), jnp.float32) * s, 'sa_out_w': jax.random.normal(ks[10], (D_MODEL, D_MODEL), jnp.float32) * s, 'q_w': jax.random.normal(ks[11], (D_MODEL, D_MODEL), jnp.float32) * s, 'k_w': jax.random.normal(ks[12], (D_MODEL, D_MODEL), jnp.float32) * s, 'v_w': jax.random.normal(ks[13], (D_MODEL, D_MODEL), jnp.float32) * s, 'ca_out_w': jax.random.normal(ks[14], (D_MODEL, D_MODEL), jnp.float32) * s, 'ffn_w1': jax.random.normal(ks[15], (D_FF, D_MODEL), jnp.float32) * s, 'ffn_b1': jax.random.normal(ks[16], (D_FF,), jnp.float32) * s, 'ffn_w2': jax.random.normal(ks[17], (D_MODEL, D_FF), jnp.float32) * s, 'ffn_b2': jax.random.normal(ks[18], (D_MODEL,), jnp.float32) * s}
        return inp
    _L3_xcond_all = _L3_xcond_setup()
    _L3_xcond_in = {k: v for k, v in _L3_xcond_all.items() if k in ('ln1_w', 'ln1_b', 'ln2_w', 'ln2_b', 'ln3_w', 'ln3_b', 'qkv_w', 'sa_out_w', 'q_w', 'k_w', 'v_w', 'ca_out_w', 'ffn_w1', 'ffn_b1', 'ffn_w2', 'ffn_b2')}
    del _L3_xcond_all
    return {'x': x, 'cond_1024': cond_1024, 'ctx_1024': ctx_1024, 'mask_BxS2_bf0': mask_BxS2_bf0, 'L0_xcond_ln_gamma': _L0_xcond_in['ln_gamma'], 'L0_xcond_ln_beta': _L0_xcond_in['ln_beta'], 'L0_xcond_Wq': _L0_xcond_in['Wq'], 'L0_xcond_Wk': _L0_xcond_in['Wk'], 'L0_xcond_Wv': _L0_xcond_in['Wv'], 'L0_xcond_router_W': _L0_xcond_in['router_W'], 'L0_xcond_router_b': _L0_xcond_in['router_b'], 'L0_xcond_e_w1': _L0_xcond_in['e_w1'], 'L0_xcond_e_b1': _L0_xcond_in['e_b1'], 'L0_xcond_e_w2': _L0_xcond_in['e_w2'], 'L0_xcond_e_b2': _L0_xcond_in['e_b2'], 'L0_xcond_gate_w1': _L0_xcond_in['gate_w1'], 'L0_xcond_gate_b1': _L0_xcond_in['gate_b1'], 'L0_xcond_gate_w2': _L0_xcond_in['gate_w2'], 'L0_xcond_gate_b2': _L0_xcond_in['gate_b2'], 'L0_xcond_out_w': _L0_xcond_in['out_w'], 'L0_xcond_out_b': _L0_xcond_in['out_b'], 'L1_xcond_ada_w': _L1_xcond_in['ada_w'], 'L1_xcond_ada_b': _L1_xcond_in['ada_b'], 'L1_xcond_qkv_w': _L1_xcond_in['qkv_w'], 'L1_xcond_qkv_b': _L1_xcond_in['qkv_b'], 'L1_xcond_sa_proj_w': _L1_xcond_in['sa_proj_w'], 'L1_xcond_sa_proj_b': _L1_xcond_in['sa_proj_b'], 'L1_xcond_q_w': _L1_xcond_in['q_w'], 'L1_xcond_q_b': _L1_xcond_in['q_b'], 'L1_xcond_kv_w': _L1_xcond_in['kv_w'], 'L1_xcond_kv_b': _L1_xcond_in['kv_b'], 'L1_xcond_ca_proj_w': _L1_xcond_in['ca_proj_w'], 'L1_xcond_ca_proj_b': _L1_xcond_in['ca_proj_b'], 'L1_xcond_fc1_w': _L1_xcond_in['fc1_w'], 'L1_xcond_fc1_b': _L1_xcond_in['fc1_b'], 'L1_xcond_fc2_w': _L1_xcond_in['fc2_w'], 'L1_xcond_fc2_b': _L1_xcond_in['fc2_b'], 'L2_xcond_W_mod': _L2_xcond_in['W_mod'], 'L2_xcond_b_mod': _L2_xcond_in['b_mod'], 'L2_xcond_W_qkv': _L2_xcond_in['W_qkv'], 'L2_xcond_b_qkv': _L2_xcond_in['b_qkv'], 'L2_xcond_W_proj': _L2_xcond_in['W_proj'], 'L2_xcond_b_proj': _L2_xcond_in['b_proj'], 'L2_xcond_W_qc': _L2_xcond_in['W_qc'], 'L2_xcond_b_qc': _L2_xcond_in['b_qc'], 'L2_xcond_W_kvc': _L2_xcond_in['W_kvc'], 'L2_xcond_b_kvc': _L2_xcond_in['b_kvc'], 'L2_xcond_W_cproj': _L2_xcond_in['W_cproj'], 'L2_xcond_b_cproj': _L2_xcond_in['b_cproj'], 'L2_xcond_W_mlp1': _L2_xcond_in['W_mlp1'], 'L2_xcond_b_mlp1': _L2_xcond_in['b_mlp1'], 'L2_xcond_W_mlp2': _L2_xcond_in['W_mlp2'], 'L2_xcond_b_mlp2': _L2_xcond_in['b_mlp2'], 'L3_xcond_ln1_w': _L3_xcond_in['ln1_w'], 'L3_xcond_ln1_b': _L3_xcond_in['ln1_b'], 'L3_xcond_ln2_w': _L3_xcond_in['ln2_w'], 'L3_xcond_ln2_b': _L3_xcond_in['ln2_b'], 'L3_xcond_ln3_w': _L3_xcond_in['ln3_w'], 'L3_xcond_ln3_b': _L3_xcond_in['ln3_b'], 'L3_xcond_qkv_w': _L3_xcond_in['qkv_w'], 'L3_xcond_sa_out_w': _L3_xcond_in['sa_out_w'], 'L3_xcond_q_w': _L3_xcond_in['q_w'], 'L3_xcond_k_w': _L3_xcond_in['k_w'], 'L3_xcond_v_w': _L3_xcond_in['v_w'], 'L3_xcond_ca_out_w': _L3_xcond_in['ca_out_w'], 'L3_xcond_ffn_w1': _L3_xcond_in['ffn_w1'], 'L3_xcond_ffn_b1': _L3_xcond_in['ffn_b1'], 'L3_xcond_ffn_w2': _L3_xcond_in['ffn_w2'], 'L3_xcond_ffn_b2': _L3_xcond_in['ffn_b2']}

def reference(x, cond_1024, ctx_1024, mask_BxS2_bf0, L0_xcond_ln_gamma, L0_xcond_ln_beta, L0_xcond_Wq, L0_xcond_Wk, L0_xcond_Wv, L0_xcond_router_W, L0_xcond_router_b, L0_xcond_e_w1, L0_xcond_e_b1, L0_xcond_e_w2, L0_xcond_e_b2, L0_xcond_gate_w1, L0_xcond_gate_b1, L0_xcond_gate_w2, L0_xcond_gate_b2, L0_xcond_out_w, L0_xcond_out_b, L1_xcond_ada_w, L1_xcond_ada_b, L1_xcond_qkv_w, L1_xcond_qkv_b, L1_xcond_sa_proj_w, L1_xcond_sa_proj_b, L1_xcond_q_w, L1_xcond_q_b, L1_xcond_kv_w, L1_xcond_kv_b, L1_xcond_ca_proj_w, L1_xcond_ca_proj_b, L1_xcond_fc1_w, L1_xcond_fc1_b, L1_xcond_fc2_w, L1_xcond_fc2_b, L2_xcond_W_mod, L2_xcond_b_mod, L2_xcond_W_qkv, L2_xcond_b_qkv, L2_xcond_W_proj, L2_xcond_b_proj, L2_xcond_W_qc, L2_xcond_b_qc, L2_xcond_W_kvc, L2_xcond_b_kvc, L2_xcond_W_cproj, L2_xcond_b_cproj, L2_xcond_W_mlp1, L2_xcond_b_mlp1, L2_xcond_W_mlp2, L2_xcond_b_mlp2, L3_xcond_ln1_w, L3_xcond_ln1_b, L3_xcond_ln2_w, L3_xcond_ln2_b, L3_xcond_ln3_w, L3_xcond_ln3_b, L3_xcond_qkv_w, L3_xcond_sa_out_w, L3_xcond_q_w, L3_xcond_k_w, L3_xcond_v_w, L3_xcond_ca_out_w, L3_xcond_ffn_w1, L3_xcond_ffn_b1, L3_xcond_ffn_w2, L3_xcond_ffn_b2):
    import jax
    import jax.numpy as jnp

    def _L0_xcond_ref(mix_hidden_states, global_anchor, prototype_bank, ln_gamma, ln_beta, Wq, Wk, Wv, router_W, router_b, e_w1, e_b1, e_w2, e_b2, gate_w1, gate_b1, gate_w2, gate_b2, out_w, out_b):
        import jax, jax.numpy as jnp
        import numpy as np
        H = 128
        RH = 2 * H
        E = 3
        B, T, P = (8, 256, 64)
        LN_EPS = 1e-05

        def _layer_norm(x, gamma, beta):
            mu = jnp.mean(x, axis=-1, keepdims=True)
            var = jnp.mean(jnp.square(x - mu), axis=-1, keepdims=True)
            return (x - mu) * jax.lax.rsqrt(var + LN_EPS) * gamma + beta
        x = mix_hidden_states
        nx = _layer_norm(x, ln_gamma, ln_beta)
        q = nx @ Wq
        k = prototype_bank @ Wk
        v = prototype_bank @ Wv
        scores = jnp.einsum('bth,bph->btp', q, k) * H ** (-0.5)
        weights = jax.nn.softmax(scores, axis=-1)
        evidence = jnp.einsum('btp,bph->bth', weights, v)
        anchor = jnp.broadcast_to(global_anchor[:, None, :], nx.shape)
        combined = jnp.concatenate([nx, evidence, anchor], axis=-1)
        router_logits = combined @ router_W + router_b
        router_probs = jax.nn.softmax(router_logits, axis=-1)
        h = jax.nn.silu(jnp.einsum('btc,ecr->bter', combined, e_w1) + e_b1)
        expert_out = jnp.einsum('bter,erh->bteh', h, e_w2) + e_b2
        routed = jnp.sum(expert_out * router_probs[..., None], axis=-2)
        g = jax.nn.sigmoid(jax.nn.silu(combined @ gate_w1 + gate_b1) @ gate_w2 + gate_b2)
        refined_delta = g * (routed @ out_w + out_b)
        return x + refined_delta

    def _L1_xcond_ref(x, t_emb, context, context_mask, ada_w, ada_b, qkv_w, qkv_b, sa_proj_w, sa_proj_b, q_w, q_b, kv_w, kv_b, ca_proj_w, ca_proj_b, fc1_w, fc1_b, fc2_w, fc2_b):
        import jax, jax.numpy as jnp
        import numpy as np
        D, H, B, N, S = (128, 16, 4, 128, 77)
        HD = D // H
        DF = 4 * D
        EPS = 1e-06
        SCALE = HD ** (-0.5)

        def _ln(x):
            m = jnp.mean(x, axis=-1, keepdims=True)
            v = jnp.mean((x - m) ** 2, axis=-1, keepdims=True)
            return (x - m) / jnp.sqrt(v + EPS)
        Bx, Nx, C = x.shape
        Sx = context.shape[1]
        mod = jax.nn.silu(t_emb) @ ada_w + ada_b
        shift_sa, scale_sa, gate_sa, shift_ff, scale_ff, gate_ff = [m[:, None, :] for m in jnp.split(mod, 6, axis=-1)]
        xm1 = _ln(x) * (1 + scale_sa) + shift_sa
        qkv = (xm1 @ qkv_w + qkv_b).reshape(Bx, Nx, 3, H, HD)
        q, k, v = (qkv[:, :, 0], qkv[:, :, 1], qkv[:, :, 2])
        attn = jnp.einsum('bnhd,bmhd->bhnm', q, k) * SCALE
        attn = jax.nn.softmax(attn, axis=-1)
        sa = jnp.einsum('bhnm,bmhd->bnhd', attn, v).reshape(Bx, Nx, C)
        sa = sa @ sa_proj_w + sa_proj_b
        x = x + gate_sa * sa
        xn2 = _ln(x)
        qc = (xn2 @ q_w + q_b).reshape(Bx, Nx, H, HD)
        kvc = (context @ kv_w + kv_b).reshape(Bx, Sx, 2, H, HD)
        kc, vc = (kvc[:, :, 0], kvc[:, :, 1])
        attn_c = jnp.einsum('bnhd,bshd->bhns', qc, kc) * SCALE
        attn_c = jnp.where(context_mask[:, None, None, :], -jnp.inf, attn_c)
        attn_c = jax.nn.softmax(attn_c, axis=-1)
        ca = jnp.einsum('bhns,bshd->bnhd', attn_c, vc).reshape(Bx, Nx, C)
        ca = ca @ ca_proj_w + ca_proj_b
        x = x + ca
        xm3 = _ln(x) * (1 + scale_ff) + shift_ff
        h = jax.nn.gelu(xm3 @ fc1_w + fc1_b, approximate=False)
        ff = h @ fc2_w + fc2_b
        x = x + gate_ff * ff
        return x

    def _L2_xcond_ref(x, c, context, W_mod, b_mod, W_qkv, b_qkv, W_proj, b_proj, W_qc, b_qc, W_kvc, b_kvc, W_cproj, b_cproj, W_mlp1, b_mlp1, W_mlp2, b_mlp2):
        import jax, jax.numpy as jnp
        import numpy as np
        LN_EPS = 1e-06

        def _ln(x):
            mu = jnp.mean(x, axis=-1, keepdims=True)
            var = jnp.var(x, axis=-1, keepdims=True)
            return (x - mu) * jax.lax.rsqrt(var + LN_EPS)
        B, N, H = x.shape
        NH = 16
        hd = H // NH
        scale = hd ** (-0.5)
        c_proj = jax.nn.silu(c) @ W_mod + b_mod
        shift_a, scale_a, gate_a, shift_m, scale_m, gate_m = jnp.split(c_proj, 6, axis=-1)

        def modulate(t, shift, sc):
            return t * (1 + sc[:, None]) + shift[:, None]
        x_norm = modulate(_ln(x), shift_a, scale_a)
        qkv = x_norm @ W_qkv + b_qkv
        q, k, v = jnp.split(qkv, 3, axis=-1)
        q = q.reshape(B, N, NH, hd).transpose(0, 2, 1, 3)
        k = k.reshape(B, N, NH, hd).transpose(0, 2, 1, 3)
        v = v.reshape(B, N, NH, hd).transpose(0, 2, 1, 3)
        attn_w = jax.nn.softmax(jnp.einsum('bhqd,bhkd->bhqk', q, k) * scale, axis=-1)
        attn_out = jnp.einsum('bhqk,bhkd->bhqd', attn_w, v)
        attn_out = attn_out.transpose(0, 2, 1, 3).reshape(B, N, H)
        attn_out = attn_out @ W_proj + b_proj
        x = x + gate_a[:, None] * attn_out
        S = context.shape[1]
        q_c = _ln(x) @ W_qc + b_qc
        kv_c = _ln(context) @ W_kvc + b_kvc
        k_c, v_c = jnp.split(kv_c, 2, axis=-1)
        q_c = q_c.reshape(B, N, NH, hd).transpose(0, 2, 1, 3)
        k_c = k_c.reshape(B, S, NH, hd).transpose(0, 2, 1, 3)
        v_c = v_c.reshape(B, S, NH, hd).transpose(0, 2, 1, 3)
        c_attn_w = jax.nn.softmax(jnp.einsum('bhqd,bhsd->bhqs', q_c, k_c) * scale, axis=-1)
        c_attn_out = jnp.einsum('bhqs,bhsd->bhqd', c_attn_w, v_c)
        c_attn_out = c_attn_out.transpose(0, 2, 1, 3).reshape(B, N, H)
        c_attn_out = c_attn_out @ W_cproj + b_cproj
        x = x + c_attn_out
        x_norm2 = modulate(_ln(x), shift_m, scale_m)
        h = jax.nn.gelu(x_norm2 @ W_mlp1 + b_mlp1)
        h = h @ W_mlp2 + b_mlp2
        x = x + gate_m[:, None] * h
        return x

    def _L3_xcond_ref(x, noise_emb, context, ln1_w, ln1_b, ln2_w, ln2_b, ln3_w, ln3_b, qkv_w, sa_out_w, q_w, k_w, v_w, ca_out_w, ffn_w1, ffn_b1, ffn_w2, ffn_b2):
        import jax, jax.numpy as jnp
        import numpy as np
        import math
        D_MODEL = 128
        N_HEADS = 16
        HEAD_DIM = D_MODEL // N_HEADS
        D_FF = 512
        EPS = 1e-05
        ROPE_BASE = 10000.0

        def _rope(t):
            L, Dh = (t.shape[1], t.shape[-1])
            half = Dh // 2
            inv_freq = 1.0 / ROPE_BASE ** (jnp.arange(half, dtype=t.dtype) / half)
            ang = jnp.arange(L, dtype=t.dtype)[:, None] * inv_freq[None, :]
            cos = jnp.cos(ang)[None, :, None, :]
            sin = jnp.sin(ang)[None, :, None, :]
            t1, t2 = (t[..., :half], t[..., half:])
            return jnp.concatenate([t1 * cos - t2 * sin, t2 * cos + t1 * sin], axis=-1)

        def _adaln(x, emb, w, b):
            e = emb[:, 0, :]
            gb = e @ w.T + b
            gamma, beta = jnp.split(gb, 2, axis=-1)
            mu = x.mean(-1, keepdims=True)
            var = x.var(-1, keepdims=True)
            xn = (x - mu) * jax.lax.rsqrt(var + EPS)
            return xn * (1.0 + gamma[:, None, :]) + beta[:, None, :]

        def _attn(q, k, v):
            scale = 1.0 / math.sqrt(HEAD_DIM)
            scores = jnp.einsum('bqhd,bkhd->bhqk', q, k) * scale
            w = jax.nn.softmax(scores, axis=-1)
            out = jnp.einsum('bhqk,bkhd->bqhd', w, v)
            B, Lq = (out.shape[0], out.shape[1])
            return out.reshape(B, Lq, D_MODEL)
        B, L, D = x.shape
        L_ctx = context.shape[1]
        res = x
        xn = _adaln(x, noise_emb, ln1_w, ln1_b)
        qkv = xn @ qkv_w.T
        q, k, v = jnp.split(qkv, 3, axis=-1)
        q = _rope(q.reshape(B, L, N_HEADS, HEAD_DIM))
        k = _rope(k.reshape(B, L, N_HEADS, HEAD_DIM))
        v = v.reshape(B, L, N_HEADS, HEAD_DIM)
        sa = _attn(q, k, v) @ sa_out_w.T
        x = res + sa
        res = x
        xn = _adaln(x, noise_emb, ln2_w, ln2_b)
        q = _rope((xn @ q_w.T).reshape(B, L, N_HEADS, HEAD_DIM))
        k = _rope((context @ k_w.T).reshape(B, L_ctx, N_HEADS, HEAD_DIM))
        v = (context @ v_w.T).reshape(B, L_ctx, N_HEADS, HEAD_DIM)
        ca = _attn(q, k, v) @ ca_out_w.T
        x = res + ca
        res = x
        xn = _adaln(x, noise_emb, ln3_w, ln3_b)
        h = jax.nn.gelu(xn @ ffn_w1.T + ffn_b1, approximate=False)
        x = res + (h @ ffn_w2.T + ffn_b2)
        return x
    x = _L0_xcond_ref(x, cond_1024, ctx_1024, L0_xcond_ln_gamma, L0_xcond_ln_beta, L0_xcond_Wq, L0_xcond_Wk, L0_xcond_Wv, L0_xcond_router_W, L0_xcond_router_b, L0_xcond_e_w1, L0_xcond_e_b1, L0_xcond_e_w2, L0_xcond_e_b2, L0_xcond_gate_w1, L0_xcond_gate_b1, L0_xcond_gate_w2, L0_xcond_gate_b2, L0_xcond_out_w, L0_xcond_out_b)
    x = _L1_xcond_ref(x, cond_1024, ctx_1024, mask_BxS2_bf0, L1_xcond_ada_w, L1_xcond_ada_b, L1_xcond_qkv_w, L1_xcond_qkv_b, L1_xcond_sa_proj_w, L1_xcond_sa_proj_b, L1_xcond_q_w, L1_xcond_q_b, L1_xcond_kv_w, L1_xcond_kv_b, L1_xcond_ca_proj_w, L1_xcond_ca_proj_b, L1_xcond_fc1_w, L1_xcond_fc1_b, L1_xcond_fc2_w, L1_xcond_fc2_b)
    x = _L2_xcond_ref(x, cond_1024, ctx_1024, L2_xcond_W_mod, L2_xcond_b_mod, L2_xcond_W_qkv, L2_xcond_b_qkv, L2_xcond_W_proj, L2_xcond_b_proj, L2_xcond_W_qc, L2_xcond_b_qc, L2_xcond_W_kvc, L2_xcond_b_kvc, L2_xcond_W_cproj, L2_xcond_b_cproj, L2_xcond_W_mlp1, L2_xcond_b_mlp1, L2_xcond_W_mlp2, L2_xcond_b_mlp2)
    x = _L3_xcond_ref(x, cond_1024[:, None, :], ctx_1024, L3_xcond_ln1_w, L3_xcond_ln1_b, L3_xcond_ln2_w, L3_xcond_ln2_b, L3_xcond_ln3_w, L3_xcond_ln3_b, L3_xcond_qkv_w, L3_xcond_sa_out_w, L3_xcond_q_w, L3_xcond_k_w, L3_xcond_v_w, L3_xcond_ca_out_w, L3_xcond_ffn_w1, L3_xcond_ffn_b1, L3_xcond_ffn_w2, L3_xcond_ffn_b2)
    return x

_drawn_inputs = setup_inputs


def setup_inputs(seed=0):
    import zlib

    import numpy as np

    out = dict(_drawn_inputs(seed))
    spreads = {'L0_xcond_ln_gamma': (1.0, 0.542),
     'L0_xcond_ln_beta': (0.0, 0.622),
     'L0_xcond_router_b': (0.0, 0.8),
     'L0_xcond_e_b1': (0.0, 0.38),
     'L0_xcond_e_b2': (0.0, 0.1),
     'L0_xcond_gate_b1': (0.0, 0.8),
     'L0_xcond_gate_b2': (0.0, 0.8),
     'L0_xcond_out_b': (0.0, 0.1),
     'L1_xcond_ada_b': (0.0, 0.534),
     'L1_xcond_qkv_b': (0.0, 0.8),
     'L1_xcond_sa_proj_b': (0.0, 0.46),
     'L1_xcond_q_b': (0.0, 2.0),
     'L1_xcond_kv_b': (0.0, 0.922),
     'L1_xcond_ca_proj_b': (0.0, 0.1),
     'L1_xcond_fc1_b': (0.0, 0.8),
     'L1_xcond_fc2_b': (0.0, 0.53),
     'L2_xcond_b_mod': (0.0, 0.1),
     'L2_xcond_b_qkv': (0.0, 0.544),
     'L2_xcond_b_proj': (0.0, 0.599),
     'L2_xcond_b_qc': (0.0, 1.762),
     'L2_xcond_b_kvc': (0.0, 0.342),
     'L2_xcond_b_cproj': (0.0, 0.335),
     'L2_xcond_b_mlp1': (0.0, 0.715),
     'L2_xcond_b_mlp2': (0.0, 0.495)}
    factors = {'L1_xcond_ada_w': 2.823,
     'L1_xcond_qkv_w': 8.0,
     'L1_xcond_sa_proj_w': 8.0,
     'L1_xcond_q_w': 64.0,
     'L1_xcond_fc1_w': 6.991,
     'L1_xcond_fc2_w': 6.055,
     'L3_xcond_ln1_w': 16.09,
     'L3_xcond_ln1_b': 195.753,
     'L3_xcond_ln2_w': 8.0,
     'L3_xcond_ln2_b': 23.778,
     'L3_xcond_ln3_w': 13.476,
     'L3_xcond_ln3_b': 64.0,
     'L3_xcond_q_w': 8.0,
     'L3_xcond_k_w': 8.0,
     'L3_xcond_v_w': 2.981,
     'L3_xcond_ca_out_w': 3.009,
     'L3_xcond_ffn_b1': 49.437,
     'L3_xcond_ffn_b2': 13.061,
     'L1_xcond_kv_w': 6.554}
    for name, (base, spread) in spreads.items():
        noise = np.random.default_rng([zlib.crc32(name.encode()), seed]).standard_normal(out[name].shape)
        drawn = base * np.exp(spread * noise) if base else spread * noise
        out[name] = jnp.asarray(drawn.astype(out[name].dtype))
    for name, factor in factors.items():
        out[name] = (out[name] * factor).astype(out[name].dtype)
    return out
```

```python
from contextlib import ExitStack

import concourse.bass as bass
import numpy as np
from concourse import mybir

F32 = mybir.dt.float32
U8 = mybir.dt.uint8
ALU = mybir.AluOpType
ACT = mybir.ActivationFunctionType
AX_X = mybir.AxisListType.X

D = 128
S = 64
B = 128
GB = 8
T = GB * S
NG = B // GB
NS = 2
LAG = 0
TT = T // 128
NH = 16
HD = D // NH
RG = 4
JH = NH // RG
HP = NH // 2
VW = HD + 1
FC = 4
NE = 3
BANKS = 8
SCALE = float(HD) ** -0.5
SCALE0 = float(D) ** -0.5

M1, M2, M3, MA, MGATE, MCOND = 0, 6, 12, 18, 24, 25
NM = 26

COLS = {}


def _column(name, n):
    COLS[name] = (sum(k for _, k in COLS.values()), n)


for _name, _n in [("L0_xcond_ln_gamma", 1), ("L0_xcond_ln_beta", 1), ("L0_xcond_e_b1", 6), ("L0_xcond_e_b2", 3),
                  ("L0_xcond_gate_b1", 1), ("L0_xcond_gate_b2", 1), ("L0_xcond_out_b", 1),
                  ("L1_xcond_ada_b", 6), ("L1_xcond_qkv_b", 3), ("L1_xcond_sa_proj_b", 1), ("L1_xcond_q_b", 1),
                  ("L1_xcond_kv_b", 2), ("L1_xcond_ca_proj_b", 1), ("L1_xcond_fc1_b", 4), ("L1_xcond_fc2_b", 1),
                  ("L2_xcond_b_mod", 6), ("L2_xcond_b_qkv", 3), ("L2_xcond_b_proj", 1), ("L2_xcond_b_qc", 1),
                  ("L2_xcond_b_kvc", 2), ("L2_xcond_b_cproj", 1), ("L2_xcond_b_mlp1", 4), ("L2_xcond_b_mlp2", 1),
                  ("L3_xcond_ln1_b", 2), ("L3_xcond_ln2_b", 2), ("L3_xcond_ln3_b", 2),
                  ("L3_xcond_ffn_b1", 4), ("L3_xcond_ffn_b2", 1)]:
    _column(_name, _n)
NCOL = sum(k for _, k in COLS.values())

K_ID, K_CEN, K_AVG, K_MASK, K_COS, K_SIN, K_EPS = 0, 128, 256, 384, 388, 452, 516
NK = 518


def shape_constants():
    k = np.zeros((128, NK), np.float32)
    k[:, K_ID:K_ID + 128] = np.eye(128)
    k[:, K_CEN:K_CEN + 128] = np.eye(128) - 1.0 / 128
    k[:, K_AVG:K_AVG + 128] = 1.0 / 128
    p = np.arange(128)
    for j in range(JH):
        k[:, K_MASK + j] = (p // HD) % JH == j
    half = HD // 2
    inv = (np.float32(1.0) / np.float32(10000.0) ** (np.arange(half, dtype=np.float32) / np.float32(half))).astype(np.float32)
    ang = (np.arange(S, dtype=np.float32)[None, :] * inv[p % half][:, None]).astype(np.float32)
    k[:, K_COS:K_COS + S] = np.cos(ang)
    k[:, K_SIN:K_SIN + S] = np.sin(ang)
    k[:, K_EPS] = 1e-5
    k[:, K_EPS + 1] = 1e-6
    return k


class Steps:

    def __init__(self, known, banks):
        self.known, self.banks = known, banks
        self.found, self.tiles, self.count, self.sem = {}, {}, {}, {}

    def start(self, sems):
        self.sem = sems
        self.count = {e: 0 for e in sems}

    def tick(self, engine, *names):
        self.count[engine] += 1
        for n in names:
            assert n not in self.found, n
            self.found[n] = (engine, self.count[engine])
        return self.sem[engine], 1

    def done(self, *name):
        engine, value = self.known.get(name, ("pe", 1))
        return self.sem[engine], value


def build(nc, io, known, tiles):
    st = Steps(known, tiles)
    tick, done = st.tick, st.done

    with ExitStack() as ctx:
        def sb(name, shape, dt=F32):
            return ctx.enter_context(nc.sbuf_tensor(name, shape, dt))

        def sem(name):
            return ctx.enter_context(nc.semaphore(name))

        bank = [ctx.enter_context(nc.psum_tensor(f"bank{i}", [128, 512], F32)) for i in range(BANKS)]

        konst = sb("konst", [128, NK])
        cols = sb("cols", [128, NCOL])
        kbias = sb("kbias", [128, 4, JH])
        rbias, rbias3 = sb("rbias", [4, 1]), sb("rbias3", [NE, 1])
        w0q, w0k, w0v = sb("w0q", [128, D]), sb("w0k", [128, D]), sb("w0v", [128, D])
        w0r = sb("w0r", [128, 3, 4])
        w0e1 = sb("w0e1", [128, NE, 3, 2 * D])
        w0e2 = sb("w0e2", [128, NE, 2, D])
        w0g1, w0g2, w0o = sb("w0g1", [128, 3, D]), sb("w0g2", [128, D]), sb("w0o", [128, D])
        w1 = {n: sb("w1" + n, [128, k, D]) for n, k in (("qkv", 3), ("proj", 1), ("q", 1), ("kv", 2), ("cproj", 1), ("fc1", 4), ("fc2", 4))}
        w2 = {n: sb("w2" + n, [128, k, D]) for n, k in (("qkv", 3), ("proj", 1), ("q", 1), ("kv", 2), ("cproj", 1), ("fc1", 4), ("fc2", 4))}
        w3 = {n: sb("w3" + n, [128, k, D]) for n, k in (("qkv", 3), ("proj", 1), ("q", 1), ("kv", 2), ("cproj", 1), ("fc1", 4), ("fc2", 4), ("rot", 4))}
        table = sb("table", [128, NM, B])
        mask8 = sb("mask8", [128, B // 2, S], U8)

        class Group:

            def __init__(self, n):
                self.n = n

                def own(name, shape, dt=F32):
                    return sb(f"{name}{n}", shape, dt)

                self.rows = own("rows", [128, 2, TT, D])
                self.x, self.cT = own("x", [128, T]), own("cT", [128, T])
                self.mod = own("mod", [128, NM, GB])
                self.pen = own("pen", [128, GB // 2, S])
                self.sq, self.rstd, self.xn = own("sq", [128, T]), own("rstd", [128, T]), own("xn", [128, T])
                self.qT, self.kT, self.km = own("qT", [128, T]), own("kT", [128, T]), own("km", [128, JH, T])
                self.rot, self.on, self.oT = own("rot", [128, T]), own("on", [128, GB // 2, D]), own("oT", [128, T])
                self.vb = own("vb", [128, GB, HP, 2 * VW])
                self.tmp = own("tmp", [128, 2, T])
                self.small = own("small", [128, 6, TT * 4])
                self.mx = own("mx", [128, 3, RG, GB])
                self.rec = own("rec", [128, 2 * NH])
                self.wide = own("wide", [128, 8, T])
                self.ss = self.wide[:, 0:RG, :]
                self.pT = self.wide[:, RG:8, :].rearrange("k c (h q) -> k (c h) q", q=128).rearrange("k (p h) q -> k p h q", p=2)
                self.hid = self.wide[:, 0:6, :]
                self.v0 = self.wide[0:S, 4:6, :]
                self.prob = self.km[:, 0:NE, :]
                self.lg = self.rstd[0:4, :]
                self.cn = self.rot

        groups = [Group(n) for n in range(NS)]
        G0, G1 = groups
        spare = G1.wide[:].rearrange("p c t -> p (c t)").rearrange("p (c n) -> p c n", n=D)
        for i, w in enumerate((w1, w2, w3)):
            w["mod"] = spare[:, 6 * i:6 * i + 6, :]

        ident = konst[:, K_ID:K_ID + 128]
        center = konst[:, K_CEN:K_CEN + 128]
        average = konst[:, K_AVG:K_AVG + 128]

        def col(name, i=0):
            a, _ = COLS[name]
            return cols[:, a + i:a + i + 1]

        def per_seq(G, i):
            return G.mod[:, i, :].unsqueeze(2).broadcast_to((128, GB, S))

        def seqs(ap):
            return ap.rearrange("p (b s) -> p b s", b=GB)

        pe_done, act_done = sem("pe_steps_done"), sem("act_steps_done")
        dve_done, pool_done = sem("dve_steps_done"), sem("pool_steps_done")
        stored = sem("group_stored")
        sems = {"pe": pe_done, "act": act_done, "dve": dve_done, "pool": pool_done}
        loaded = sem("weights_loaded")
        first_in = sem("first_group_loaded")
        nums = [s.num for s in (*sems.values(), stored)]
        assert sorted(nums) == list(range(min(nums), max(nums) + 1))
        counters = range(min(nums), max(nums) + 1)

        x_rows = io["x"].rearrange("b s d -> (b s) d")
        c_rows = io["ctx_1024"].rearrange("b s d -> (b s) d")
        out_rows = io["out"].rearrange("b s d -> (b s) d")

        def load_group(eng, G, first_row, signal):
            for n, rows in enumerate((x_rows, c_rows)):
                eng.dma_start(G.rows[:, n], rows[bass.ds(first_row, T), :].rearrange("(t p) d -> p t d", p=128)).then_inc(signal, 16)

        def vector_in(name):
            a, n = COLS[name]
            v = io[name]
            if len(v.shape) == 2:
                v = v.rearrange("e r -> (e r)")
            return cols[:, a:a + n], v.rearrange("(n p) -> p n", p=128)

        def chunks_in(t, name, rows=1):
            v = io[name]
            dst = t[:, :, :] if len(t.shape) == 3 else t[:, :]
            if rows > 1:
                return dst, v.rearrange("(c p) n -> p c n", p=128)
            return dst, v.rearrange("p (c n) -> p c n", n=128) if len(t.shape) == 3 else v

        straight = [
            (konst[:], io["consts"]),
            (G0.x[:, 0:D], io["cond_1024"]),
            chunks_in(w0q, "L0_xcond_Wq"), chunks_in(w0k, "L0_xcond_Wk"), chunks_in(w0v, "L0_xcond_Wv"),
            (w0e1[:, 0], io["L0_xcond_e_w1"][0].rearrange("(c p) r -> p c r", p=128)),
            (w0e1[:, 1], io["L0_xcond_e_w1"][1].rearrange("(c p) r -> p c r", p=128)),
            (w0e1[:, 2], io["L0_xcond_e_w1"][2].rearrange("(c p) r -> p c r", p=128)),
            (w0e2[:].rearrange("p e c n -> p (e c) n"), io["L0_xcond_e_w2"].rearrange("e (c p) h -> p (e c) h", p=128)),
            (w0g1[:], io["L0_xcond_gate_w1"].rearrange("(c p) h -> p c h", p=128)),
            chunks_in(w0g2, "L0_xcond_gate_w2"), chunks_in(w0o, "L0_xcond_out_w"),
            (w0r[:, :, 0:3], io["L0_xcond_router_W"].rearrange("(c p) e -> p c e", p=128)),
            (rbias3[:], io["L0_xcond_router_b"].rearrange("(e o) -> e o", o=1)),
            chunks_in(w1["mod"], "L1_xcond_ada_w"), chunks_in(w1["qkv"], "L1_xcond_qkv_w"),
            chunks_in(w1["proj"], "L1_xcond_sa_proj_w"), chunks_in(w1["q"], "L1_xcond_q_w"),
            chunks_in(w1["kv"], "L1_xcond_kv_w"), chunks_in(w1["cproj"], "L1_xcond_ca_proj_w"),
            chunks_in(w1["fc1"], "L1_xcond_fc1_w"), chunks_in(w1["fc2"], "L1_xcond_fc2_w", 4),
            chunks_in(w2["mod"], "L2_xcond_W_mod"), chunks_in(w2["qkv"], "L2_xcond_W_qkv"),
            chunks_in(w2["proj"], "L2_xcond_W_proj"), chunks_in(w2["q"], "L2_xcond_W_qc"),
            chunks_in(w2["kv"], "L2_xcond_W_kvc"), chunks_in(w2["cproj"], "L2_xcond_W_cproj"),
            chunks_in(w2["fc1"], "L2_xcond_W_mlp1"), chunks_in(w2["fc2"], "L2_xcond_W_mlp2", 4),
        ]
        turned = [("L3_xcond_ln1_w", "mod", 0, 2), ("L3_xcond_ln2_w", "mod", 2, 2), ("L3_xcond_ln3_w", "mod", 4, 2),
                  ("L3_xcond_qkv_w", "qkv", 0, 3), ("L3_xcond_sa_out_w", "proj", 0, 1), ("L3_xcond_q_w", "q", 0, 1),
                  ("L3_xcond_k_w", "kv", 0, 1), ("L3_xcond_v_w", "kv", 1, 1), ("L3_xcond_ca_out_w", "cproj", 0, 1),
                  ("L3_xcond_ffn_w1", "fc1", 0, 4), ("L3_xcond_ffn_w2", "fc2", 0, 4)]
        blocks = [(w, i) for _, w, a, n in turned for i in range(a, a + n)]
        stage = G0.wide[:].rearrange("p c t -> p (c t)")[:, 0:len(blocks) * D].rearrange("p (c n) -> p c n", n=D)
        at = 0
        for name, w, a, n in turned:
            v = io[name]
            src = v.rearrange("p (c n) -> p c n", n=D) if w == "fc2" else v.rearrange("(c p) n -> p c n", p=128)
            straight.append((stage[:, at:at + n, :], src))
            at += n
        seq_mask = io["mask_BxS2_bf0"].rearrange("(p b) k -> b p k", b=2)
        for b2 in range(2):
            straight.append((mask8[64 * b2:64 * b2 + 64], seq_mask[b2:b2 + 1].broadcast_to((64, B // 2, S))))
        vectors = [vector_in(n) for n in COLS]
        n_sp, n_act = len(straight), len(vectors)

        rot_of = [("qkv", 0), ("qkv", 1), ("q", 0), ("kv", 0)]
        condT, silT = G0.qT[:, 0:B], G0.kT[:, 0:B]
        tables = ([(M1 + i, w1["mod"][:, i, :], silT, col("L1_xcond_ada_b", i), i in (1, 4)) for i in range(6)]
                  + [(M2 + i, w2["mod"][:, i, :], silT, col("L2_xcond_b_mod", i), i in (1, 4)) for i in range(6)]
                  + [(M3 + i, w3["mod"][:, i, :], condT, col(f"L3_xcond_ln{i // 2 + 1}_b", i % 2), i % 2 == 0) for i in range(6)]
                  + [(MA + 2 * e + h, w0e1[:, e, 2, h * D:(h + 1) * D], condT, col("L0_xcond_e_b1", 2 * e + h), False)
                     for e in range(NE) for h in range(2)]
                  + [(MGATE, w0g1[:, 2, :], condT, col("L0_xcond_gate_b1"), False)])

        st.start(sems)
        with nc.Block() as block:
            @block.sync
            def _(sp):
                with nc.allow_non_contiguous_dma("weights in their layouts"):
                    for dst, src in straight:
                        sp.dma_start(dst, src).then_inc(loaded, 16)
                    for G in groups:
                        load_group(sp, G, G.n * T, first_in)
                sp.wait_ge(loaded, 16 * (n_sp + n_act))
                sp.wait_ge(first_in, 32 * NS)

            @block.tensor
            def _(pe):
                pe.wait_ge(loaded, 16 * (n_sp + n_act))
                pe.transpose(bank[7][:, 0:B], G0.x[:, 0:D], ident).then_inc(*tick("pe", ("cond",)))
                for n, (w, i) in enumerate(blocks):
                    if n >= 7:
                        pe.wait_ge(*done("turned", n - 7))
                    pe.transpose(bank[n % 7][:, 0:D], stage[:, n, :], ident).then_inc(*tick("pe", ("turn", n)))
                pe.wait_ge(*done("silu cond"))
                pe.wait_ge(*done("turned", len(blocks) - 1))
                for n, (m, w, rhs, _, _) in enumerate(tables):
                    if n >= 7:
                        pe.wait_ge(*done("table", n - 7))
                    pe.matmul(bank[n % 7][:, 0:B], w, rhs, start=True, stop=True).then_inc(*tick("pe", ("table product", n)))

            @block.scalar
            def _(act):
                with nc.allow_non_contiguous_dma("per-feature vectors"):
                    for dst, src in vectors:
                        act.dma_start(dst, src).then_inc(loaded, 16)
                act.wait_ge(*done("condT"))
                act.activation(silT, condT, ACT.Silu).then_inc(*tick("act", ("silu cond",)))
                act.wait_ge(*done("silu cond"))

            @block.vector
            def _(dve):
                for G in groups:
                    dve.memset(G.vb[:], 0.0).then_inc(*tick("dve", ("vb zero", G.n)))
                    dve.wait_ge(*done("vb zero", G.n))
                    dve.memset(G.vb[0:64, :, :, HD:HD + 1], 1.0)
                    dve.memset(G.vb[64:128, :, :, VW + HD:VW + HD + 1], 1.0)
                dve.memset(w0r[:, :, 3:4], 0.0)
                dve.memset(rbias[:], 0.0).then_inc(*tick("dve", ("rbias zero",)))
                dve.wait_ge(loaded, 16 * (n_sp + n_act))
                dve.wait_ge(*done("cond"))
                dve.tensor_copy(condT, bank[7][:, 0:B]).then_inc(*tick("dve", ("condT",)))
                dve.wait_ge(*done("condT"))
                dve.tensor_copy(table[:, MCOND, :], condT)
                dve.wait_ge(*done("rbias zero"))
                dve.tensor_copy(rbias[0:NE, :], rbias3[:])
                for n, (w, i) in enumerate(blocks):
                    dve.wait_ge(*done("turn", n))
                    dve.tensor_copy(w3[w][:, i, :], bank[n % 7][:, 0:D]).then_inc(*tick("dve", ("turned", n)))
                dve.wait_ge(*done("turned", len(blocks) - 1))
                half = HD // 2
                for n, (w, i) in enumerate(rot_of):
                    src = w3[w][:, i, :].rearrange("p (h t d) -> p h t d", h=NH, t=2)
                    dst = w3["rot"][:, n, :].rearrange("p (h t d) -> p h t d", h=NH, t=2)
                    dve.tensor_scalar(dst[:, :, 0, :], src[:, :, 1, :], -1.0, None, ALU.mult)
                    dve.tensor_copy(dst[:, :, 1, :], src[:, :, 0, :])
                for a, name, i in ((0, "L1_xcond_qkv_b", 1), (1, "L1_xcond_kv_b", 0), (2, "L2_xcond_b_qkv", 1), (3, "L2_xcond_b_kvc", 0)):
                    dve.tensor_scalar(kbias[:, a, :], konst[:, K_MASK:K_MASK + JH], col(name, i), None, ALU.mult)
                for n, (m, w, rhs, b, one) in enumerate(tables):
                    dve.wait_ge(*done("table product", n))
                    dve.tensor_scalar(table[:, m, :], bank[n % 7][:, 0:B], b, 1.0 if one else 0.0, ALU.add, ALU.add)\
                        .then_inc(*tick("dve", ("table", n)))

        nc.all_engine_barrier(sems_to_clear=counters)

        st.start(sems)

        class Ring:

            def __init__(self):
                self.last, self.turn, self.held = {}, 0, {}

            def claim(self, pe, name, hold=None):
                while self.turn in self.held.values():
                    self.turn = (self.turn + 1) % BANKS
                where = self.turn
                self.turn = (self.turn + 1) % BANKS
                if hold:
                    self.held[hold] = where
                if where in self.last:
                    pe.wait_ge(*done("free", self.last[where]))
                self.last[where] = name
                st.tiles[name] = where
                return bank[where]

            def let_go(self, hold):
                del self.held[hold]

        def tile(name):
            return bank[st.banks.get(name, 0)]

        ring = Ring()

        def pe_turn_in(pe, G):
            for n, nm in enumerate(("x", "c")):
                b = ring.claim(pe, (G.n, "in", nm))
                for t in range(TT):
                    ins = pe.transpose(b[:, t * 128:(t + 1) * 128], G.rows[:, n, t, :], ident)
                ins.then_inc(*tick("pe", ("mm", (G.n, "in", nm))))

        def pe_product(pe, name, pairs, hold=None):
            b = ring.claim(pe, name, hold)
            for i, (w, m) in enumerate(pairs):
                ins = pe.matmul(b[0:w.shape[-1], :], w, m, start=(i == 0), stop=(i == len(pairs) - 1))
            ins.then_inc(*tick("pe", ("mm", name)))

        def pe_values(pe, G, tag, src, w):
            for v in range(2):
                b = ring.claim(pe, (G.n, tag, "v", v))
                for i in range(4):
                    tok = src[:, (4 * v + i) * S:(4 * v + i + 1) * S]
                    for e in range(2):
                        ins = pe.matmul(b[64 * e:64 * e + 64, i * D:(i + 1) * D], tok, w, start=True, stop=True)
                ins.then_inc(*tick("pe", ("mm", (G.n, tag, "v", v))))

        def pe_scores(pe, G, tag, u):
            if u == 0:
                pe.wait_ge(*done("qT", G.n, tag))
                pe.wait_ge(*done("km", G.n, tag))
            b4 = [ring.claim(pe, (G.n, tag, "s", u, r)) for r in range(RG)]
            for rows2 in ((0, 1), (2, 3)):
                for p in range(2):
                    for b2 in range(2):
                        tok = (4 * u + 2 * p + b2) * S
                        for r in rows2:
                            rows = slice(32 * r, 32 * r + 32)
                            ins = pe.matmul(b4[r][64 * b2:64 * b2 + 64, p * 256:(p + 1) * 256].rearrange("q (j k) -> q j k", j=JH),
                                            G.qT[rows, tok:tok + S], G.km[rows, :, tok:tok + S], start=True, stop=True)
                            if p == 1 and b2 == 1:
                                ins.then_inc(*tick("pe", ("mm", (G.n, tag, "s", u, r))))

        def pe_mix(pe, G, tag, u):
            for c in range(2):
                for p in range(2):
                    b = ring.claim(pe, (G.n, tag, "pT", u, p, c))
                    for rr in range(2):
                        r = 2 * c + rr
                        pe.wait_ge(*done("exp", G.n, tag, u, r))
                        for jj in range(2):
                            a = p * 256 + jj * 128
                            ins = pe.transpose(b[:, (2 * rr + jj) * 128:(2 * rr + jj + 1) * 128], G.ss[:, r, a:a + 128], ident)
                    ins.then_inc(*tick("pe", ("mm", (G.n, tag, "pT", u, p, c))))
            b = ring.claim(pe, (G.n, tag, "o", u))
            if u == 0:
                pe.wait_ge(*done("vb", G.n, tag))
            for c in range(2):
                for p in range(2):
                    pe.wait_ge(*done("pT", G.n, tag, u, p, c))
                    for hp in range(4 * c, 4 * c + 4):
                        for b2 in range(2):
                            a = (p * HP + hp) * 2 * VW
                            ins = pe.matmul(b[64 * b2:64 * b2 + 64, a:a + 2 * VW], G.pT[:, p, hp, 64 * b2:64 * b2 + 64],
                                            G.vb[:, 4 * u + 2 * p + b2, hp, :], start=True, stop=True)
            ins.then_inc(*tick("pe", ("mm", (G.n, tag, "o", u))))

        def pe_turn_out(pe, G, tag):
            b = ring.claim(pe, (G.n, tag, "oT"))
            for u in range(2):
                pe.wait_ge(*done("on", G.n, tag, u))
                for p in range(2 * u, 2 * u + 2):
                    ins = pe.transpose(b[:, p * 128:(p + 1) * 128], G.on[:, p, :], ident)
            ins.then_inc(*tick("pe", ("mm", (G.n, tag, "oT"))))

        def pe_mlp_out(pe, G, tag, w):
            b = ring.claim(pe, (G.n, tag, "y"))
            for c in range(FC):
                pe.wait_ge(*done("h", G.n, tag, c))
                ins = pe.matmul(b[:], w[:, c, :], G.hid[:, c, :], start=(c == 0), stop=(c == FC - 1))
            ins.then_inc(*tick("pe", ("mm", (G.n, tag, "y"))))

        def act_tables(act, number):
            act.add_instruction(mybir.InstLoadActFuncSet(name=nc.get_next_instruction_name(), act_func_set_id=number, ins=[], outs=[]))

        def act_out(act, G, name, dst, bias, *names, func=ACT.Identity):
            act.wait_ge(*done("mm", (G.n, *name)))
            act.activation(dst, tile((G.n, *name))[0:dst.shape[0], :], func, bias=bias)\
                .then_inc(*tick("act", ("free", (G.n, *name)), *names))

        def act_square(act, G, tag):
            act.wait_ge(*done("mm", (G.n, tag, "cen")))
            act.activation(G.sq[:], tile((G.n, tag, "cen"))[:], ACT.Square).then_inc(*tick("act", ("sq", G.n, tag)))

        def act_rstd(act, G, tag, eps):
            act.wait_ge(*done("mm", (G.n, tag, "var")))
            act.activation(G.rstd[:], tile((G.n, tag, "var"))[:], ACT.Ln, bias=konst[:, K_EPS + eps:K_EPS + eps + 1])\
                .then_inc(*tick("act", ("free", (G.n, tag, "var")), ("ln", G.n, tag)))
            act.wait_ge(*done("ln", G.n, tag))
            act.activation(G.rstd[:], G.rstd[:], ACT.Exp, scale=-0.5).then_inc(*tick("act", ("rstd", G.n, tag)))

        def act_keys(act, G, tag, bk):
            name = (G.n, tag, "k")
            act.wait_ge(*(done("mm", name) if bk is not None else done("kT", G.n, tag)))
            for j in range(JH):
                end = [("km", G.n, tag)] if j == JH - 1 else []
                one = konst[:, K_MASK + j:K_MASK + j + 1]
                if bk is not None:
                    act.activation(G.km[:, j, :], tile(name)[:], ACT.Identity, bias=kbias[:, bk, j:j + 1], scale=one)\
                        .then_inc(*tick("act", *([("free", name)] if end else []), *end))
                else:
                    act.activation(G.km[:, j, :], G.kT[:], ACT.Copy, scale=one).then_inc(*tick("act", *end))

        def act_values(act, G, tag):
            for v in range(2):
                name = (G.n, tag, "v", v)
                act.wait_ge(*done("mm", name))
                src = tile(name)[:].rearrange("k (b h e d) -> k b h e d", b=4, h=HP, e=2)
                for e in range(2):
                    names = ([("free", name)] + ([("vb", G.n, tag)] if v == 1 else [])) if e == 1 else []
                    act.activation(G.vb[64 * e:64 * e + 64, 4 * v:4 * v + 4, :, VW * e:VW * e + HD],
                                   src[64 * e:64 * e + 64, :, :, e, :], ACT.Copy).then_inc(*tick("act", *names))

        def act_exp(act, G, tag, u):
            for r in range(RG):
                act.wait_ge(*done("sub", G.n, tag, u, r))
                act.activation(G.ss[:, r, :], G.ss[:, r, :], ACT.Exp, scale=SCALE).then_inc(*tick("act", ("exp", G.n, tag, u, r)))

        def act_mix(act, G, tag, u):
            for c in range(2):
                for p in range(2):
                    name = (G.n, tag, "pT", u, p, c)
                    act.wait_ge(*done("mm", name))
                    act.activation(G.pT[:, p, 4 * c:4 * c + 4, :].rearrange("k h q -> k (h q)"), tile(name)[:], ACT.Copy)\
                        .then_inc(*tick("act", ("free", name), ("pT", G.n, tag, u, p, c)))

        def dve_norm(dve, G, tag, scale, shift, dst):
            last = scale is None
            cen = (G.n, tag, "cen")
            dve.wait_ge(*done("rstd", G.n, tag))
            dve.tensor_tensor(dst[:], tile(cen)[:], G.rstd[:], ALU.mult)\
                .then_inc(*tick("dve", ("free", cen), ("xn" if last else "xn 1", G.n, tag)))
            if last:
                return
            dve.wait_ge(*done("xn 1", G.n, tag))
            dve.tensor_tensor(seqs(dst[:]), seqs(dst[:]), per_seq(G, scale), ALU.mult).then_inc(*tick("dve", ("xn 2", G.n, tag)))
            dve.wait_ge(*done("xn 2", G.n, tag))
            dve.tensor_tensor(seqs(dst[:]), seqs(dst[:]), per_seq(G, shift), ALU.add).then_inc(*tick("dve", ("xn", G.n, tag)))

        def dve_rotary(dve, G, tag, n, dst, name):
            wide = lambda a: konst[:, a:a + S].unsqueeze(1).broadcast_to((128, GB, S))
            straight, turned = (G.n, tag, n), (G.n, tag, n + " rot")
            dve.wait_ge(*done("mm", straight))
            dve.tensor_tensor(seqs(dst[:]), seqs(tile(straight)[:]), wide(K_COS), ALU.mult)\
                .then_inc(*tick("dve", ("free", straight), ("cos", G.n, tag, n)))
            dve.wait_ge(*done("mm", turned))
            dve.tensor_tensor(seqs(G.rot[:]), seqs(tile(turned)[:]), wide(K_SIN), ALU.mult)\
                .then_inc(*tick("dve", ("free", turned), ("sin", G.n, tag, n)))
            dve.wait_ge(*done("sin", G.n, tag, n))
            dve.tensor_tensor(dst[:], dst[:], G.rot[:], ALU.add).then_inc(*tick("dve", (name, G.n, tag)))
            dve.wait_ge(*done(name, G.n, tag))

        def dve_scores(dve, G, tag, u, masked):
            heads = lambda ap: ap.rearrange("q (g k) -> q g k", k=S)
            for r in range(RG):
                name = (G.n, tag, "s", u, r)
                src = tile(name)[:]
                dve.wait_ge(*done("mm", name))
                if masked:
                    quad = lambda ap, p: ap[:, p * 256:(p + 1) * 256].rearrange("q (j k) -> q j k", j=JH)
                    for p in range(2):
                        dve.tensor_tensor(quad(G.ss[:, r, :], p), quad(src, p),
                                          G.pen[:, 2 * u + p, :].unsqueeze(1).broadcast_to((128, JH, S)), ALU.add)\
                            .then_inc(*tick("dve", ("masked", G.n, tag, u, r, p), *([("free", name)] if p else [])))
                    src = G.ss[:, r, :]
                    dve.wait_ge(*done("masked", G.n, tag, u, r, 1))
                dve.tensor_reduce(G.mx[:, 0, r, :], heads(src), AX_X, ALU.max).then_inc(*tick("dve", ("max", G.n, tag, u, r)))
                dve.wait_ge(*done("max", G.n, tag, u, r))
                dve.tensor_tensor(heads(G.ss[:, r, :]), heads(src), G.mx[:, 0, r, :].unsqueeze(2).broadcast_to((128, GB, S)), ALU.subtract)\
                    .then_inc(*tick("dve", ("sub", G.n, tag, u, r), *([] if masked else [("free", name)])))

        def dve_mix(dve, G, tag, u):
            name = (G.n, tag, "o", u)
            o = tile(name)[:, 0:2 * NH * VW].rearrange("q (h w) -> q h w", w=VW)
            dve.wait_ge(*done("mm", name))
            dve.reciprocal(G.rec[:], o[:, :, HD]).then_inc(*tick("dve", ("rec", G.n, tag, u)))
            dve.wait_ge(*done("rec", G.n, tag, u))
            dve.tensor_tensor(G.on[:, 2 * u:2 * u + 2, :].rearrange("q p (h d) -> q (p h) d", d=HD), o[:, :, 0:HD],
                              G.rec[:].unsqueeze(2).broadcast_to((128, 2 * NH, HD)), ALU.mult)\
                .then_inc(*tick("dve", ("free", name), ("on", G.n, tag, u)))

        def dve_residual(dve, G, name, bias, gate, end):
            name, x = (G.n, *name), G.x
            dve.wait_ge(*done("mm", name))
            if gate is None and bias is None:
                dve.tensor_tensor(x[:], tile(name)[:], x[:], ALU.add).then_inc(*tick("dve", ("free", name), ("x", G.n, end)))
            elif gate is None:
                dve.scalar_tensor_tensor(x[:], tile(name)[:], bias, x[:], ALU.add, ALU.add)\
                    .then_inc(*tick("dve", ("free", name), ("x", G.n, end)))
            else:
                dve.scalar_tensor_tensor(seqs(G.tmp[:, 1, :]), seqs(tile(name)[:]), bias, gate, ALU.add, ALU.mult)\
                    .then_inc(*tick("dve", ("free", name), ("gated", G.n, end)))
                dve.wait_ge(*done("gated", G.n, end))
                dve.tensor_tensor(x[:], x[:], G.tmp[:, 1, :], ALU.add).then_inc(*tick("dve", ("x", G.n, end)))

        def pe_keys0(pe, G):
            pe.wait_ge(*done("c", G.n))
            pe_product(pe, (G.n, "0", "k"), [(w0k[:], G.cT[:])])
            for v in range(2):
                b = ring.claim(pe, (G.n, "0", "v", v))
                for i in range(4):
                    s = (4 * v + i) * S
                    ins = pe.matmul(b[0:S, i * D:(i + 1) * D], G.cT[:, s:s + S], w0v[:], start=True, stop=True)
                ins.then_inc(*tick("pe", ("mm", (G.n, "0", "v", v))))

        def act_keys0(act, G):
            act_out(act, G, ("0", "k"), G.kT[:], 0.0, ("kT", G.n, "0"))
            for v in range(2):
                act_out(act, G, ("0", "v", v), G.v0[:, v, :], 0.0, ("v", G.n, v))

        def dve_norm0(dve, G):
            cen = (G.n, "0", "cen")
            dve.wait_ge(*done("rstd", G.n, "0"))
            dve.scalar_tensor_tensor(G.xn[:], tile(cen)[:], col("L0_xcond_ln_gamma"), G.rstd[:], ALU.mult, ALU.mult)\
                .then_inc(*tick("dve", ("free", cen), ("xn 1", G.n, "0")))
            dve.wait_ge(*done("xn 1", G.n, "0"))
            dve.tensor_scalar(G.xn[:], G.xn[:], col("L0_xcond_ln_beta"), None, ALU.add).then_inc(*tick("dve", ("xn", G.n, "0")))

        def pe_scores0(pe, G):
            pe.wait_ge(*done("qT", G.n, "0"))
            pe.wait_ge(*done("kT", G.n, "0"))
            b = ring.claim(pe, (G.n, "0", "s"))
            for q in range(GB):
                ins = pe.matmul(b[64 * (q % 2):64 * (q % 2) + 64, (q // 2) * S:(q // 2 + 1) * S],
                                G.qT[:, q * S:(q + 1) * S], G.kT[:, q * S:(q + 1) * S], start=True, stop=True)
            ins.then_inc(*tick("pe", ("mm", (G.n, "0", "s"))))

        def dve_scores0(dve, G):
            pairs = lambda ap: ap.rearrange("q (p k) -> q p k", k=S)
            wide = lambda ap: ap.unsqueeze(2).broadcast_to((128, GB // 2, S))
            name = (G.n, "0", "s")
            s, p0 = tile(name)[:, 0:256], G.ss[:, 0, 0:256]
            top, total, rec = (G.mx[:, 0, r, 0:GB // 2] for r in range(3))
            dve.wait_ge(*done("mm", name))
            dve.tensor_reduce(top, pairs(s), AX_X, ALU.max).then_inc(*tick("dve", ("max", G.n, "0")))
            dve.wait_ge(*done("max", G.n, "0"))
            dve.tensor_tensor(pairs(p0), pairs(s), wide(top), ALU.subtract).then_inc(*tick("dve", ("sub", G.n, "0"), ("free", name)))
            dve.wait_ge(*done("exp", G.n, "0"))
            dve.tensor_reduce(total, pairs(p0), AX_X, ALU.add).then_inc(*tick("dve", ("sum", G.n, "0")))
            dve.wait_ge(*done("sum", G.n, "0"))
            dve.reciprocal(rec, total).then_inc(*tick("dve", ("rec", G.n, "0")))
            dve.wait_ge(*done("rec", G.n, "0"))
            dve.tensor_tensor(pairs(p0), pairs(p0), wide(rec), ALU.mult).then_inc(*tick("dve", ("p", G.n, "0")))

        def act_scores0(act, G):
            act.wait_ge(*done("sub", G.n, "0"))
            act.activation(G.ss[:, 0, 0:256], G.ss[:, 0, 0:256], ACT.Exp, scale=SCALE0).then_inc(*tick("act", ("exp", G.n, "0")))

        def pe_turn_probs0(pe, G):
            pe.wait_ge(*done("p", G.n, "0"))
            b = ring.claim(pe, (G.n, "0", "pT"))
            for p in range(GB // 2):
                ins = pe.transpose(b[0:S, p * 128:(p + 1) * 128], G.ss[:, 0, p * S:(p + 1) * S], ident)
            ins.then_inc(*tick("pe", ("mm", (G.n, "0", "pT"))))

        def pe_evidence(pe, G):
            pe.wait_ge(*done("pT", G.n, "0"))
            pe.wait_ge(*done("v", G.n, 1))
            b = ring.claim(pe, (G.n, "0", "ev"))
            for q in range(GB):
                ins = pe.matmul(b[:, q * S:(q + 1) * S], G.v0[:, q // 4, (q % 4) * D:(q % 4 + 1) * D],
                                G.oT[0:S, q * S:(q + 1) * S], start=True, stop=True)
            ins.then_inc(*tick("pe", ("mm", (G.n, "0", "ev"))))

        def pe_route(pe, G):
            pe.wait_ge(*done("lg", G.n))
            b = ring.claim(pe, (G.n, "0", "lgT"))
            for t in range(TT):
                ins = pe.transpose(b[:, 4 * t:4 * t + 4], G.lg[:, t * 128:(t + 1) * 128], ident[0:4, 0:4])
            ins.then_inc(*tick("pe", ("mm", (G.n, "0", "lgT"))))

        def dve_route(dve, G):
            three = lambda ap: ap.rearrange("t (n e) -> t n e", e=4)[:, :, 0:NE]
            wide3 = lambda ap: ap.unsqueeze(2).broadcast_to((128, TT, NE))
            small, name = G.small, (G.n, "0", "lgT")
            top, total, rec = (small[:, 0, i * TT:(i + 1) * TT] for i in range(3))
            lgT = three(tile(name)[:, 0:4 * TT])
            dve.wait_ge(*done("mm", name))
            dve.tensor_reduce(top, lgT, AX_X, ALU.max).then_inc(*tick("dve", ("route max", G.n)))
            dve.wait_ge(*done("route max", G.n))
            dve.tensor_tensor(three(small[:, 1, :]), lgT, wide3(top), ALU.subtract).then_inc(*tick("dve", ("free", name), ("route sub", G.n)))
            dve.wait_ge(*done("route exp", G.n))
            dve.tensor_reduce(total, three(small[:, 2, :]), AX_X, ALU.add).then_inc(*tick("dve", ("route sum", G.n)))
            dve.wait_ge(*done("route sum", G.n))
            dve.reciprocal(rec, total).then_inc(*tick("dve", ("route rec", G.n)))
            dve.wait_ge(*done("route rec", G.n))
            dve.tensor_tensor(three(small[:, 5, :]), three(small[:, 2, :]), wide3(rec), ALU.mult).then_inc(*tick("dve", ("route", G.n)))

        def act_route(act, G):
            three = lambda ap: ap.rearrange("t (n e) -> t n e", e=4)[:, :, 0:NE]
            act.wait_ge(*done("route sub", G.n))
            act.activation(three(G.small[:, 2, :]), three(G.small[:, 1, :]), ACT.Exp).then_inc(*tick("act", ("route exp", G.n)))

        def pe_experts_in(pe, G):
            for e in range(NE):
                for h in range(2):
                    a = h * D
                    pe_product(pe, (G.n, "0", "h", 2 * e + h), [(w0e1[:, e, 0, a:a + D], G.xn[:]), (w0e1[:, e, 1, a:a + D], G.rot[:])])
            pe_product(pe, (G.n, "0", "g1"), [(w0g1[:, 0, :], G.xn[:]), (w0g1[:, 1, :], G.rot[:])])

        def dve_experts_in(dve, G):
            for n in range(2 * NE + 1):
                name = (G.n, "0", "h", n) if n < 2 * NE else (G.n, "0", "g1")
                dve.wait_ge(*done("mm", name))
                if n >= 2:
                    dve.wait_ge(*done("h", G.n, "0", n - 2))
                dve.tensor_tensor(seqs(G.tmp[:, n % 2, :]), seqs(tile(name)[:]), per_seq(G, MA + n), ALU.add)\
                    .then_inc(*tick("dve", ("free", name), ("h pre", G.n, n)))

        def act_experts_in(act, G):
            for n in range(2 * NE + 1):
                act.wait_ge(*done("h pre", G.n, n))
                dst = G.hid[:, n, :] if n < 2 * NE else G.qT[:]
                act.activation(dst, G.tmp[:, n % 2, :], ACT.Silu).then_inc(*tick("act", ("h", G.n, "0", n)))

        def pe_experts_out(pe, G):
            pe.wait_ge(*done("route", G.n))
            for e in range(NE):
                b = ring.claim(pe, (G.n, "0", "pb", e))
                for t in range(TT):
                    ins = pe.matmul(b[:, t * 128:(t + 1) * 128], G.small[:, 5, 4 * t + e:4 * t + e + 1].broadcast_to((128, 128)),
                                    ident, start=True, stop=True)
                ins.then_inc(*tick("pe", ("mm", (G.n, "0", "pb", e))))
            for e in range(NE):
                pe.wait_ge(*done("h", G.n, "0", 2 * e + 1))
                pe_product(pe, (G.n, "0", "e", e), [(w0e2[:, e, h, :], G.hid[:, 2 * e + h, :]) for h in range(2)])
            pe.wait_ge(*done("h", G.n, "0", 2 * NE))
            pe_product(pe, (G.n, "0", "g2"), [(w0g2[:], G.qT[:])])

        def act_experts_out(act, G):
            for e in range(NE):
                act_out(act, G, ("0", "pb", e), G.prob[:, e, :], 0.0, ("pb", G.n, e))

        def dve_experts_out(dve, G):
            for e in range(NE):
                name = (G.n, "0", "e", e)
                dve.wait_ge(*done("mm", name))
                dve.wait_ge(*done("pb", G.n, e))
                dst = G.kT[:] if e == 0 else G.tmp[:, 1, :]
                dve.scalar_tensor_tensor(dst, tile(name)[:], col("L0_xcond_e_b2", e), G.prob[:, e, :], ALU.add, ALU.mult)\
                    .then_inc(*tick("dve", ("free", name), ("routed", G.n, 0) if e == 0 else ("expert", G.n, e)))
                if e:
                    dve.wait_ge(*done("expert", G.n, e))
                    dve.tensor_tensor(G.kT[:], G.kT[:], G.tmp[:, 1, :], ALU.add).then_inc(*tick("dve", ("routed", G.n, e)))
                    dve.wait_ge(*done("routed", G.n, e))

        def norm_stages(G, tag, before, scale, shift, dst, eps, src, more=(None, None)):
            nothing = (None, None, None)
            one, two = (m or nothing for m in more)

            def pe_a(pe):
                pe.wait_ge(*done(*before))
                pe_product(pe, (G.n, tag, "cen"), [(center, src[:])], hold=(G.n, tag))
                if one[0]:
                    one[0](pe)

            def act_a(act):
                act_square(act, G, tag)
                if one[1]:
                    one[1](act)

            def pe_b(pe):
                pe.wait_ge(*done("sq", G.n, tag))
                pe_product(pe, (G.n, tag, "var"), [(average, G.sq[:])])
                ring.let_go((G.n, tag))
                if two[0]:
                    two[0](pe)

            def act_b(act):
                act_rstd(act, G, tag, eps)
                if two[1]:
                    two[1](act)

            def dve_b(dve):
                if tag == "0":
                    dve_norm0(dve, G)
                else:
                    dve_norm(dve, G, tag, scale, shift, dst)
                if two[2]:
                    two[2](dve)

            return [(pe_a, act_a, one[2]), (pe_b, act_b, dve_b)]

        weights = {1: w1, 2: w2, 3: w3}

        def queries(G, tag, L, cross, ready, bq):
            w = weights[L]

            def pe_q(pe):
                pe.wait_ge(*done(*ready))
                pe_product(pe, (G.n, tag, "q"), [(w["q"][:, 0, :] if cross else w["qkv"][:, 0, :], G.xn[:])])
                if L == 3:
                    pe_product(pe, (G.n, tag, "q rot"), [(w["rot"][:, 2 * cross, :], G.xn[:])])

            def act_q(act):
                if L < 3:
                    act_out(act, G, (tag, "q"), G.qT[:], bq, ("qT", G.n, tag))

            def dve_q(dve):
                if L == 3:
                    dve_rotary(dve, G, tag, "q", G.qT, "qT")
            return pe_q, act_q, dve_q

        def keys(G, tag, L, cross, src, ready, bk):
            w = weights[L]

            def pe_k(pe):
                pe.wait_ge(*done(*ready))
                pe_product(pe, (G.n, tag, "k"), [(w["kv"][:, 0, :] if cross else w["qkv"][:, 1, :], src[:])])
                if L == 3:
                    pe_product(pe, (G.n, tag, "k rot"), [(w["rot"][:, 2 * cross + 1, :], src[:])])

            def act_k(act):
                act_keys(act, G, tag, bk if L < 3 else None)

            def dve_k(dve):
                if L == 3:
                    dve_rotary(dve, G, tag, "k", G.kT, "kT")
            return pe_k, act_k, dve_k

        def values(G, tag, L, cross, src):
            w = weights[L]
            return (lambda pe: pe_values(pe, G, tag, src, w["kv"][:, 1, :] if cross else w["qkv"][:, 2, :]),
                    lambda act: act_values(act, G, tag), None)

        def together(*parts):
            def on(k):
                def run(e):
                    for part in parts:
                        if part[k]:
                            part[k](e)
                return run
            return on(0), on(1), on(2)

        def attention_core(G, tag, masked, bv):
            out = []
            for u in range(2):
                out.append((lambda pe, u=u: pe_scores(pe, G, tag, u), lambda act, u=u: act_exp(act, G, tag, u),
                            lambda dve, u=u: dve_scores(dve, G, tag, u, masked)))
                out.append((lambda pe, u=u: pe_mix(pe, G, tag, u), lambda act, u=u: act_mix(act, G, tag, u),
                            lambda dve, u=u: dve_mix(dve, G, tag, u)))
            out.append((lambda pe: pe_turn_out(pe, G, tag),
                        lambda act: act_out(act, G, (tag, "oT"), G.oT[:], bv, ("oT", G.n, tag)), None))
            return out

        def projection(G, tag, w, bias, gate):
            def pe_p(pe):
                pe.wait_ge(*done("oT", G.n, tag))
                pe_product(pe, (G.n, tag, "proj"), [(w[:, 0, :], G.oT[:])])
            return pe_p, None, lambda dve: dve_residual(dve, G, (tag, "proj"), bias, gate, tag)

        def mlp_stages(G, tag, L, func, b1, b2, gate, end):
            w = weights[L]

            def pe_h(pe):
                pe.wait_ge(*done("xn", G.n, tag))
                for c in range(FC):
                    pe_product(pe, (G.n, tag, "h", c), [(w["fc1"][:, c, :], G.xn[:])])

            def act_h(act):
                for c in range(FC):
                    act_out(act, G, (tag, "h", c), G.hid[:, c, :], col(b1, c), ("h", G.n, tag, c), func=func)
                if G.n == NS - 1:
                    act_tables(act, 6)
            return [(pe_h, act_h, None),
                    (lambda pe: pe_mlp_out(pe, G, tag, w["fc2"]), None,
                     lambda dve: dve_residual(dve, G, (tag, "y"), col(b2), gate, end))]

        def stages_of(G):
            n = G.n

            def act_in(act):
                for nm, dst in (("x", G.x), ("c", G.cT)):
                    act_out(act, G, ("in", nm), dst[:], 0.0, ("x", n, "in") if nm == "x" else ("c", n))

            out = [(lambda pe: pe_turn_in(pe, G), act_in, None)]
            out += norm_stages(G, "0", ("x", n, "in"), None, None, G.xn, 0, G.x,
                               more=((lambda pe: pe_keys0(pe, G), lambda act: act_keys0(act, G), None), None))

            def pe_q0(pe):
                pe.wait_ge(*done("xn", n, "0"))
                pe_product(pe, (n, "0", "q"), [(w0q[:], G.xn[:])])

            out.append((pe_q0, lambda act: act_out(act, G, ("0", "q"), G.qT[:], 0.0, ("qT", n, "0")), None))
            out.append((lambda pe: pe_scores0(pe, G), lambda act: act_scores0(act, G), lambda dve: dve_scores0(dve, G)))
            out.append((lambda pe: pe_turn_probs0(pe, G),
                        lambda act: act_out(act, G, ("0", "pT"), G.oT[0:S, :], 0.0, ("pT", n, "0")), None))
            out.append((lambda pe: pe_evidence(pe, G), lambda act: act_out(act, G, ("0", "ev"), G.rot[:], 0.0, ("ev", n)), None))

            def pe_logits(pe):
                pe.wait_ge(*done("ev", n))
                pe_product(pe, (n, "0", "lg"), [(w0r[:, 0, :], G.xn[:]), (w0r[:, 1, :], G.rot[:]), (w0r[:, 2, :], per_seq(G, MCOND))])

            out.append((pe_logits, lambda act: act_out(act, G, ("0", "lg"), G.lg, rbias[:], ("lg", n)), None))
            out.append((lambda pe: pe_route(pe, G), lambda act: act_route(act, G), lambda dve: dve_route(dve, G)))
            out.append((lambda pe: pe_experts_in(pe, G), lambda act: act_experts_in(act, G), lambda dve: dve_experts_in(dve, G)))
            out.append((lambda pe: pe_experts_out(pe, G), lambda act: act_experts_out(act, G), lambda dve: dve_experts_out(dve, G)))

            def pe_out0(pe):
                pe.wait_ge(*done("routed", n, NE - 1))
                pe_product(pe, (n, "0", "out"), [(w0o[:], G.kT[:])])

            def act_gate(act):
                act_out(act, G, ("0", "g2"), G.sq[:], col("L0_xcond_gate_b2"), ("gate", n), func=ACT.Sigmoid)
                if n == NS - 1:
                    act_tables(act, 6)

            def dve_out0(dve):
                dve.wait_ge(*done("gate", n))
                dve_residual(dve, G, ("0", "out"), col("L0_xcond_out_b"), seqs(G.sq[:]), "0")

            out.append((pe_out0, act_gate, dve_out0))

            for L, p in ((1, "L1_xcond_"), (2, "L2_xcond_"), (3, "L3_xcond_")):
                eps = 0 if L == 3 else 1
                s, c, a, b, m = (f"{L}{k}" for k in "sxabm")
                w, last = weights[L], f"{L - 1}"
                base = {1: M1, 2: M2, 3: M3}[L]
                na, nb, nm = {1: ((1, 0), None, (4, 3)), 2: ((1, 0), None, (4, 3)), 3: ((0, 1), (2, 3), (4, 5))}[L]
                na, nb, nm = ((base + i[0], base + i[1]) if i else (None, None) for i in (na, nb, nm))
                ga, gm = (per_seq(G, base + 2), per_seq(G, base + 5)) if L < 3 else (None, None)
                bias = {1: lambda k, i=0: col(p + {"q": "qkv_b", "v": "qkv_b", "proj": "sa_proj_b", "cq": "q_b", "cv": "kv_b",
                                                   "cproj": "ca_proj_b"}[k], i),
                        2: lambda k, i=0: col(p + {"q": "b_qkv", "v": "b_qkv", "proj": "b_proj", "cq": "b_qc", "cv": "b_kvc",
                                                   "cproj": "b_cproj"}[k], i)}.get(L)
                ctx_src, ctx_ready = (G.cn, ("xn", n, "2c")) if L == 2 else (G.cT, ("c", n))

                out += norm_stages(G, a, ("x", n, last), *na, G.xn, eps, G.x)
                out.append(together(queries(G, s, L, 0, ("xn", n, a), bias("q", 0) if bias else 0.0),
                                    keys(G, s, L, 0, G.xn, ("xn", n, a), {1: 0, 2: 2, 3: None}[L]),
                                    values(G, s, L, 0, G.xn)))
                out += attention_core(G, s, False, bias("v", 2) if bias else 0.0)
                if L == 2:
                    out += norm_stages(G, "2c", ("c", n), None, None, G.cn, 1, G.cT)
                out.append(projection(G, s, w["proj"], bias("proj") if bias else None, ga))
                out += norm_stages(G, b, ("x", n, s), *nb, G.xn, eps, G.x,
                                   more=(keys(G, c, L, 1, ctx_src, ctx_ready, {1: 1, 2: 3, 3: None}[L]), values(G, c, L, 1, ctx_src)))
                out.append(queries(G, c, L, 1, ("xn", n, b), bias("cq") if bias else 0.0))
                out += attention_core(G, c, L == 1, bias("cv", 1) if bias else 0.0)
                out.append(projection(G, c, w["cproj"], bias("cproj") if bias else None, None))
                out += norm_stages(G, m, ("x", n, c), *nm, G.xn, eps, G.x)
                b1, b2 = {1: ("fc1_b", "fc2_b"), 2: ("b_mlp1", "b_mlp2"), 3: ("ffn_b1", "ffn_b2")}[L]
                out += mlp_stages(G, m, L, ACT.Gelu_apprx_tanh if L == 2 else ACT.Gelu, p + b1, p + b2, gm, f"{L}")

            def pe_out(pe):
                pe.wait_ge(*done("x", n, "3"))
                b = ring.claim(pe, (n, "out"))
                for t in range(TT):
                    ins = pe.transpose(b[:, t * 128:(t + 1) * 128], G.x[:, t * 128:(t + 1) * 128], ident)
                ins.then_inc(*tick("pe", ("mm", (n, "out"))))

            out.append((pe_out, lambda act: act_out(act, G, ("out",), G.tmp[:, 0, :], 0.0, ("rows", n)), None))
            return out

        lists = [stages_of(G) for G in groups]
        order = [lists[g][k - LAG * g] for k in range(len(lists[0]) + LAG * (NS - 1)) for g in range(NS)
                 if 0 <= k - LAG * g < len(lists[g])]

        with nc.Fori(0, NG // NS) as i:
            with nc.Block() as block:
                @block.sync
                def _(sp):
                    for G in groups:
                        sp.wait_ge(*done("mm", (G.n, "in", "c")))
                        load_group(sp, G, next_row(i, G.n), stored)
                    for G in groups:
                        sp.wait_ge(*done("rows", G.n))
                        sp.dma_start(out_rows[bass.ds((i * NS + G.n) * T, T), :].rearrange("(t p) d -> p t d", p=128),
                                     G.tmp[:, 0, :].rearrange("p (t d) -> p t d", d=D)).then_inc(stored, 16)
                    sp.wait_ge(stored, 48 * NS)

                @block.tensor
                def _(pe):
                    pe.wait_ge(*done("mod", NS - 1))
                    for stage in order:
                        if stage[0]:
                            stage[0](pe)

                @block.scalar
                def _(act):
                    act_tables(act, 6)
                    for stage in order:
                        if stage[1]:
                            stage[1](act)

                @block.vector
                def _(dve):
                    for G in groups:
                        g = i * NS + G.n
                        dve.tensor_copy(G.mod[:], table[:, :, bass.ds(g * GB, GB)]).then_inc(*tick("dve", ("mod", G.n)))
                        dve.tensor_scalar(G.pen[:], mask8[:, bass.ds(g * (GB // 2), GB // 2), :], -3e38, 1e10, ALU.mult, ALU.mult)\
                            .then_inc(*tick("dve", ("pen", G.n)))
                    dve.wait_ge(*done("pen", NS - 1))
                    for stage in order:
                        if stage[2]:
                            stage[2](dve)

            nc.all_engine_barrier(sems_to_clear=counters)
    return st


def next_row(i, n):
    return ((NS * (i + 1) + n) % NG) * T


_INS = ["x", "cond_1024", "ctx_1024", "mask_BxS2_bf0"] + list(COLS) + [
    "L0_xcond_Wq", "L0_xcond_Wk", "L0_xcond_Wv", "L0_xcond_router_W", "L0_xcond_router_b", "L0_xcond_e_w1", "L0_xcond_e_w2",
    "L0_xcond_gate_w1", "L0_xcond_gate_w2", "L0_xcond_out_w", "L1_xcond_ada_w", "L1_xcond_qkv_w", "L1_xcond_sa_proj_w",
    "L1_xcond_q_w", "L1_xcond_kv_w", "L1_xcond_ca_proj_w", "L1_xcond_fc1_w", "L1_xcond_fc2_w", "L2_xcond_W_mod",
    "L2_xcond_W_qkv", "L2_xcond_W_proj", "L2_xcond_W_qc", "L2_xcond_W_kvc", "L2_xcond_W_cproj", "L2_xcond_W_mlp1",
    "L2_xcond_W_mlp2", "L3_xcond_ln1_w", "L3_xcond_ln2_w", "L3_xcond_ln3_w", "L3_xcond_qkv_w", "L3_xcond_sa_out_w",
    "L3_xcond_q_w", "L3_xcond_k_w", "L3_xcond_v_w", "L3_xcond_ca_out_w", "L3_xcond_ffn_w1", "L3_xcond_ffn_w2"]


def kernel(**inputs):
    import concourse.bacc as bacc
    from concourse.bass_utils import run_bass_kernel_spmd

    arrays = {n: np.ascontiguousarray(inputs[n]) for n in _INS}
    arrays["consts"] = shape_constants()
    found, tiles = {}, {}
    for _ in range(2):
        nc = bacc.Bacc("TRN2", target_bir_lowering=False, num_devices=1)
        io = {n: nc.dram_tensor(f"in_{n}_dram", a.shape, mybir.dt.from_np(a.dtype), kind="ExternalInput").ap()
              for n, a in arrays.items()}
        io["out"] = nc.dram_tensor("out_0_dram", (B, S, D), F32, kind="ExternalOutput").ap()
        steps = build(nc, io, found, tiles)
        found, tiles = steps.found, steps.tiles
    r = run_bass_kernel_spmd(nc, [{f"in_{n}_dram": a for n, a in arrays.items()}], core_ids=[0])
    return r.results[0]["out_0_dram"]
```

```python
from contextlib import ExitStack

import concourse.bass as bass
import numpy as np
from concourse import mybir

F32 = mybir.dt.float32
U8 = mybir.dt.uint8
ALU = mybir.AluOpType
ACT = mybir.ActivationFunctionType
AX_X = mybir.AxisListType.X

D = 128
S = 64
B = 128
GB = 8
T = GB * S
NG = B // GB
NS = 2
LAG = 4.0
PACE = {"turn in": 3, "center": 1.44, "norm": 4, "product": 2, "keys": 2.7, "values": 1.88, "scores": 3, "exps": 0.3, "turn": 1, "mix": 1.3, "turn out": 2, "mlp in": 4, "mlp out": 4, "scores 0": 5, "route": 3, "experts in": 13, "experts out": 9.3, "first scores": 3, "first mix": 1.3}
TT = T // 128
NH = 16
HD = D // NH
RG = 4
JH = NH // RG
HP = NH // 2
PV = 2 * HD
FC = 4
NE = 3
BANKS = 8
SCALE = float(HD) ** -0.5
SCALE0 = float(D) ** -0.5

M1, M2, M3, MA, MGATE, MCOND = 0, 6, 12, 18, 24, 25
NM = 26

COLS = {}


def _column(name, n):
    COLS[name] = (sum(k for _, k in COLS.values()), n)


for _name, _n in [("L0_xcond_ln_gamma", 1), ("L0_xcond_ln_beta", 1), ("L0_xcond_e_b1", 6), ("L0_xcond_e_b2", 3),
                  ("L0_xcond_gate_b1", 1), ("L0_xcond_gate_b2", 1), ("L0_xcond_out_b", 1),
                  ("L1_xcond_ada_b", 6), ("L1_xcond_qkv_b", 3), ("L1_xcond_sa_proj_b", 1), ("L1_xcond_q_b", 1),
                  ("L1_xcond_kv_b", 2), ("L1_xcond_ca_proj_b", 1), ("L1_xcond_fc1_b", 4), ("L1_xcond_fc2_b", 1),
                  ("L2_xcond_b_mod", 6), ("L2_xcond_b_qkv", 3), ("L2_xcond_b_proj", 1), ("L2_xcond_b_qc", 1),
                  ("L2_xcond_b_kvc", 2), ("L2_xcond_b_cproj", 1), ("L2_xcond_b_mlp1", 4), ("L2_xcond_b_mlp2", 1),
                  ("L3_xcond_ln1_b", 2), ("L3_xcond_ln2_b", 2), ("L3_xcond_ln3_b", 2),
                  ("L3_xcond_ffn_b1", 4), ("L3_xcond_ffn_b2", 1)]:
    _column(_name, _n)
NCOL = sum(k for _, k in COLS.values())

K_ID, K_CEN, K_AVG, K_MASK, K_COS, K_SIN, K_EPS, K_ONE = 0, 128, 256, 384, 388, 452, 516, 518
NK = K_ONE + 3 * PV


def shape_constants():
    k = np.zeros((128, NK), np.float32)
    k[:, K_ID:K_ID + 128] = np.eye(128)
    k[:, K_CEN:K_CEN + 128] = np.eye(128) - 1.0 / 128
    k[:, K_AVG:K_AVG + 128] = 1.0 / 128
    p = np.arange(128)
    for j in range(JH):
        k[:, K_MASK + j] = (p // HD) % JH == j
    half = HD // 2
    inv = (np.float32(1.0) / np.float32(10000.0) ** (np.arange(half, dtype=np.float32) / np.float32(half))).astype(np.float32)
    ang = (np.arange(S, dtype=np.float32)[None, :] * inv[p % half][:, None]).astype(np.float32)
    k[:, K_COS:K_COS + S] = np.cos(ang)
    k[:, K_SIN:K_SIN + S] = np.sin(ang)
    k[:, K_EPS] = 1e-5
    k[:, K_EPS + 1] = 1e-6
    for start in (K_ONE, K_ONE + 2 * PV):
        k[0:64, start:start + HD] = 1
        k[64:128, start + HD:start + PV] = 1
    return k


class Steps:

    def __init__(self, known, banks):
        self.known, self.banks = known, banks
        self.found, self.tiles, self.count, self.sem = {}, {}, {}, {}

    def start(self, sems):
        self.sem = sems
        self.count = {e: 0 for e in sems}

    def tick(self, engine, *names):
        self.count[engine] += 1
        for n in names:
            assert n not in self.found, n
            self.found[n] = (engine, self.count[engine])
        return self.sem[engine], 1

    def done(self, *name):
        engine, value = self.known.get(name, ("pe", 1))
        return self.sem[engine], value


def build(nc, io, known, tiles):
    st = Steps(known, tiles)
    tick, done = st.tick, st.done

    with ExitStack() as ctx:
        def sb(name, shape, dt=F32):
            return ctx.enter_context(nc.sbuf_tensor(name, shape, dt))

        def sem(name):
            return ctx.enter_context(nc.semaphore(name))

        bank = [ctx.enter_context(nc.psum_tensor(f"bank{i}", [128, 512], F32)) for i in range(BANKS)]

        konst = sb("konst", [128, NK])
        cols = sb("cols", [128, NCOL])
        kbias = sb("kbias", [128, 4, JH])
        rbias, rbias3 = sb("rbias", [4, 1]), sb("rbias3", [NE, 1])
        w0q, w0k, w0v = sb("w0q", [128, D]), sb("w0k", [128, D]), sb("w0v", [128, D])
        w0r = sb("w0r", [128, 3, 4])
        w0e1 = sb("w0e1", [128, NE, 3, 2 * D])
        w0e2 = sb("w0e2", [128, NE, 2, D])
        w0g1, w0g2, w0o = sb("w0g1", [128, 3, D]), sb("w0g2", [128, D]), sb("w0o", [128, D])
        w1 = {n: sb("w1" + n, [128, k, D]) for n, k in (("qkv", 3), ("proj", 1), ("q", 1), ("kv", 2), ("cproj", 1), ("fc1", 4), ("fc2", 4))}
        w2 = {n: sb("w2" + n, [128, k, D]) for n, k in (("qkv", 3), ("proj", 1), ("q", 1), ("kv", 2), ("cproj", 1), ("fc1", 4), ("fc2", 4))}
        w3 = {n: sb("w3" + n, [128, k, D]) for n, k in (("qkv", 3), ("proj", 1), ("q", 1), ("kv", 2), ("cproj", 1), ("fc1", 4), ("fc2", 4), ("rot", 4))}
        table = sb("table", [128, NM, B])
        mask8 = sb("mask8", [128, B // 2, S], U8)

        class Group:

            def __init__(self, n):
                self.n = n

                def own(name, shape, dt=F32):
                    return sb(f"{name}{n}", shape, dt)

                self.rows = own("rows", [128, 2, TT, D])
                self.x, self.cT = own("x", [128, T]), own("cT", [128, T])
                self.mod = own("mod", [128, NM, GB])
                self.pen = own("pen", [128, GB // 2, S])
                self.sq, self.rstd, self.xn = own("sq", [128, T]), own("rstd", [128, T]), own("xn", [128, T])
                self.qT, self.kT, self.km = own("qT", [128, T]), own("kT", [128, T]), own("km", [128, JH, T])
                self.rot, self.oT = own("rot", [128, T]), own("oT", [128, T])
                self.vb = {k: own("vb" + k, [128, 2, GB // 2, HP // 2, 3 * PV]) for k in "sx"}
                self.tmp = own("tmp", [128, 2, T])
                self.small = own("small", [128, 6, TT * 4])
                self.mx = own("mx", [128, 3, RG, GB])
                self.rec = own("rec", [128, 2, T // 2])
                self.wide = own("wide", [128, 8, T])
                self.ss = self.wide[:, 0:RG, :]
                self.pT = self.wide[:, RG:8, :].rearrange("k c (h q) -> k (c h) q", q=128).rearrange("k (p h) q -> k p h q", p=2)
                self.hid = self.wide[:, 0:6, :]
                self.v0 = self.wide[0:S, 4:6, :]
                self.prob = self.km[:, 0:NE, :]
                self.lg = self.rstd[0:4, :]
                self.cn = self.rot

        groups = [Group(n) for n in range(NS)]
        G0, G1 = groups
        spare = G1.wide[:].rearrange("p c t -> p (c t)").rearrange("p (c n) -> p c n", n=D)
        for i, w in enumerate((w1, w2, w3)):
            w["mod"] = spare[:, 6 * i:6 * i + 6, :]

        ident = konst[:, K_ID:K_ID + 128]
        center = konst[:, K_CEN:K_CEN + 128]
        average = konst[:, K_AVG:K_AVG + 128]

        def col(name, i=0):
            a, _ = COLS[name]
            return cols[:, a + i:a + i + 1]

        def per_seq(G, i):
            return G.mod[:, i, :].unsqueeze(2).broadcast_to((128, GB, S))

        def seqs(ap):
            return ap.rearrange("p (b s) -> p b s", b=GB)

        pe_done, act_done = sem("pe_steps_done"), sem("act_steps_done")
        dve_done, pool_done = sem("dve_steps_done"), sem("pool_steps_done")
        stored = sem("group_stored")
        sems = {"pe": pe_done, "act": act_done, "dve": dve_done, "pool": pool_done}
        loaded = sem("weights_loaded")
        first_in = sem("first_group_loaded")
        nums = [s.num for s in (*sems.values(), stored)]
        assert sorted(nums) == list(range(min(nums), max(nums) + 1))
        counters = range(min(nums), max(nums) + 1)

        x_rows = io["x"].rearrange("b s d -> (b s) d")
        c_rows = io["ctx_1024"].rearrange("b s d -> (b s) d")
        out_rows = io["out"].rearrange("b s d -> (b s) d")

        def load_group(eng, G, first_row, signal):
            for n, rows in enumerate((x_rows, c_rows)):
                eng.dma_start(G.rows[:, n], rows[bass.ds(first_row, T), :].rearrange("(t p) d -> p t d", p=128)).then_inc(signal, 16)

        def vector_in(name):
            a, n = COLS[name]
            v = io[name]
            if len(v.shape) == 2:
                v = v.rearrange("e r -> (e r)")
            return cols[:, a:a + n], v.rearrange("(n p) -> p n", p=128)

        def chunks_in(t, name, rows=1):
            v = io[name]
            dst = t[:, :, :] if len(t.shape) == 3 else t[:, :]
            if rows > 1:
                return dst, v.rearrange("(c p) n -> p c n", p=128)
            return dst, v.rearrange("p (c n) -> p c n", n=128) if len(t.shape) == 3 else v

        straight = [
            (konst[:], io["consts"]),
            (G0.x[:, 0:D], io["cond_1024"]),
            chunks_in(w0q, "L0_xcond_Wq"), chunks_in(w0k, "L0_xcond_Wk"), chunks_in(w0v, "L0_xcond_Wv"),
            (w0e1[:, 0], io["L0_xcond_e_w1"][0].rearrange("(c p) r -> p c r", p=128)),
            (w0e1[:, 1], io["L0_xcond_e_w1"][1].rearrange("(c p) r -> p c r", p=128)),
            (w0e1[:, 2], io["L0_xcond_e_w1"][2].rearrange("(c p) r -> p c r", p=128)),
            (w0e2[:].rearrange("p e c n -> p (e c) n"), io["L0_xcond_e_w2"].rearrange("e (c p) h -> p (e c) h", p=128)),
            (w0g1[:], io["L0_xcond_gate_w1"].rearrange("(c p) h -> p c h", p=128)),
            chunks_in(w0g2, "L0_xcond_gate_w2"), chunks_in(w0o, "L0_xcond_out_w"),
            (w0r[:, :, 0:3], io["L0_xcond_router_W"].rearrange("(c p) e -> p c e", p=128)),
            (rbias3[:], io["L0_xcond_router_b"].rearrange("(e o) -> e o", o=1)),
            chunks_in(w1["mod"], "L1_xcond_ada_w"), chunks_in(w1["qkv"], "L1_xcond_qkv_w"),
            chunks_in(w1["proj"], "L1_xcond_sa_proj_w"), chunks_in(w1["q"], "L1_xcond_q_w"),
            chunks_in(w1["kv"], "L1_xcond_kv_w"), chunks_in(w1["cproj"], "L1_xcond_ca_proj_w"),
            chunks_in(w1["fc1"], "L1_xcond_fc1_w"), chunks_in(w1["fc2"], "L1_xcond_fc2_w", 4),
            chunks_in(w2["mod"], "L2_xcond_W_mod"), chunks_in(w2["qkv"], "L2_xcond_W_qkv"),
            chunks_in(w2["proj"], "L2_xcond_W_proj"), chunks_in(w2["q"], "L2_xcond_W_qc"),
            chunks_in(w2["kv"], "L2_xcond_W_kvc"), chunks_in(w2["cproj"], "L2_xcond_W_cproj"),
            chunks_in(w2["fc1"], "L2_xcond_W_mlp1"), chunks_in(w2["fc2"], "L2_xcond_W_mlp2", 4),
        ]
        turned = [("L3_xcond_ln1_w", "mod", 0, 2), ("L3_xcond_ln2_w", "mod", 2, 2), ("L3_xcond_ln3_w", "mod", 4, 2),
                  ("L3_xcond_qkv_w", "qkv", 0, 3), ("L3_xcond_sa_out_w", "proj", 0, 1), ("L3_xcond_q_w", "q", 0, 1),
                  ("L3_xcond_k_w", "kv", 0, 1), ("L3_xcond_v_w", "kv", 1, 1), ("L3_xcond_ca_out_w", "cproj", 0, 1),
                  ("L3_xcond_ffn_w1", "fc1", 0, 4), ("L3_xcond_ffn_w2", "fc2", 0, 4)]
        blocks = [(w, i) for _, w, a, n in turned for i in range(a, a + n)]
        stage = G0.wide[:].rearrange("p c t -> p (c t)")[:, 0:len(blocks) * D].rearrange("p (c n) -> p c n", n=D)
        at = 0
        for name, w, a, n in turned:
            v = io[name]
            src = v.rearrange("p (c n) -> p c n", n=D) if w == "fc2" else v.rearrange("(c p) n -> p c n", p=128)
            straight.append((stage[:, at:at + n, :], src))
            at += n
        seq_mask = io["mask_BxS2_bf0"].rearrange("(p b) k -> b p k", b=2)
        for b2 in range(2):
            straight.append((mask8[64 * b2:64 * b2 + 64], seq_mask[b2:b2 + 1].broadcast_to((64, B // 2, S))))
        vectors = [vector_in(n) for n in COLS]
        n_sp, n_act = len(straight), len(vectors)

        rot_of = [("qkv", 0), ("qkv", 1), ("q", 0), ("kv", 0)]
        condT, silT = G0.qT[:, 0:B], G0.kT[:, 0:B]
        tables = ([(M1 + i, w1["mod"][:, i, :], silT, col("L1_xcond_ada_b", i), i in (1, 4)) for i in range(6)]
                  + [(M2 + i, w2["mod"][:, i, :], silT, col("L2_xcond_b_mod", i), i in (1, 4)) for i in range(6)]
                  + [(M3 + i, w3["mod"][:, i, :], condT, col(f"L3_xcond_ln{i // 2 + 1}_b", i % 2), i % 2 == 0) for i in range(6)]
                  + [(MA + 2 * e + h, w0e1[:, e, 2, h * D:(h + 1) * D], condT, col("L0_xcond_e_b1", 2 * e + h), False)
                     for e in range(NE) for h in range(2)]
                  + [(MGATE, w0g1[:, 2, :], condT, col("L0_xcond_gate_b1"), False)])

        passed = [(w["proj"], col(p + qkv, 2), col(p + b)) for w, p, qkv, b in (
            (w1, "L1_xcond_", "qkv_b", "sa_proj_b"), (w2, "L2_xcond_", "b_qkv", "b_proj"))]
        passed += [(w["cproj"], col(p + kv, 1), col(p + b)) for w, p, kv, b in (
            (w1, "L1_xcond_", "kv_b", "ca_proj_b"), (w2, "L2_xcond_", "b_kvc", "b_cproj"))]

        st.start(sems)
        with nc.Block() as block:
            @block.sync
            def _(sp):
                with nc.allow_non_contiguous_dma("weights in their layouts"):
                    for dst, src in straight:
                        sp.dma_start(dst, src).then_inc(loaded, 16)
                    for G in groups:
                        load_group(sp, G, G.n * T, first_in)
                sp.wait_ge(loaded, 16 * (n_sp + n_act))
                sp.wait_ge(first_in, 32 * NS)

            @block.tensor
            def _(pe):
                pe.wait_ge(loaded, 16 * (n_sp + n_act))
                pe.transpose(bank[7][:, 0:B], G0.x[:, 0:D], ident).then_inc(*tick("pe", ("cond",)))
                for n, (w, i) in enumerate(blocks):
                    if n >= 7:
                        pe.wait_ge(*done("turned", n - 7))
                    pe.transpose(bank[n % 7][:, 0:D], stage[:, n, :], ident).then_inc(*tick("pe", ("turn", n)))
                pe.wait_ge(*done("silu cond"))
                for n, (w, v, _) in enumerate(passed):
                    ins = pe.matmul(bank[7][:, 2 * n:2 * n + 1], w[:, 0, :], v, start=True, stop=True)
                ins.then_inc(*tick("pe", ("passed",)))
                pe.wait_ge(*done("turned", len(blocks) - 1))
                for n, (m, w, rhs, _, _) in enumerate(tables):
                    if n >= 7:
                        pe.wait_ge(*done("table", n - 7))
                    pe.matmul(bank[n % 7][:, 0:B], w, rhs, start=True, stop=True).then_inc(*tick("pe", ("table product", n)))

            @block.scalar
            def _(act):
                with nc.allow_non_contiguous_dma("per-feature vectors"):
                    for dst, src in vectors:
                        act.dma_start(dst, src).then_inc(loaded, 16)
                act.wait_ge(*done("condT"))
                act.activation(silT, condT, ACT.Silu).then_inc(*tick("act", ("silu cond",)))
                act.wait_ge(*done("silu cond"))

            @block.vector
            def _(dve):
                for G in groups:
                    for k, vb in G.vb.items():
                        dve.memset(vb[:], 0.0).then_inc(*tick("dve", ("vb zero", G.n, k)))
                dve.memset(w0r[:, :, 3:4], 0.0)
                dve.memset(rbias[:], 0.0).then_inc(*tick("dve", ("rbias zero",)))
                dve.wait_ge(loaded, 16 * (n_sp + n_act))
                dve.wait_ge(*done("cond"))
                dve.tensor_copy(condT, bank[7][:, 0:B]).then_inc(*tick("dve", ("condT",)))
                dve.wait_ge(*done("condT"))
                dve.tensor_copy(table[:, MCOND, :], condT)
                dve.wait_ge(*done("rbias zero"))
                dve.tensor_copy(rbias[0:NE, :], rbias3[:])
                for n, (w, i) in enumerate(blocks):
                    dve.wait_ge(*done("turn", n))
                    dve.tensor_copy(w3[w][:, i, :], bank[n % 7][:, 0:D]).then_inc(*tick("dve", ("turned", n)))
                dve.wait_ge(*done("turned", len(blocks) - 1))
                half = HD // 2
                for n, (w, i) in enumerate(rot_of):
                    src = w3[w][:, i, :].rearrange("p (h t d) -> p h t d", h=NH, t=2)
                    dst = w3["rot"][:, n, :].rearrange("p (h t d) -> p h t d", h=NH, t=2)
                    dve.tensor_scalar(dst[:, :, 0, :], src[:, :, 1, :], -1.0, None, ALU.mult)
                    dve.tensor_copy(dst[:, :, 1, :], src[:, :, 0, :])
                dve.wait_ge(*done("passed"))
                for n, (_, _, b) in enumerate(passed):
                    dve.tensor_tensor(b, b, bank[7][:, 2 * n:2 * n + 1], ALU.add)
                for a, name, i in ((0, "L1_xcond_qkv_b", 1), (1, "L1_xcond_kv_b", 0), (2, "L2_xcond_b_qkv", 1), (3, "L2_xcond_b_kvc", 0)):
                    dve.tensor_scalar(kbias[:, a, :], konst[:, K_MASK:K_MASK + JH], col(name, i), None, ALU.mult)
                for n, (m, w, rhs, b, one) in enumerate(tables):
                    dve.wait_ge(*done("table product", n))
                    dve.tensor_scalar(table[:, m, :], bank[n % 7][:, 0:B], b, 1.0 if one else 0.0, ALU.add, ALU.add)\
                        .then_inc(*tick("dve", ("table", n)))

        nc.all_engine_barrier(sems_to_clear=counters)

        st.start(sems)

        class Ring:

            def __init__(self):
                self.last, self.turn, self.held = {}, 0, {}

            def claim(self, pe, name, hold=None):
                while self.turn in self.held.values():
                    self.turn = (self.turn + 1) % BANKS
                where = self.turn
                self.turn = (self.turn + 1) % BANKS
                if hold:
                    self.held[hold] = where
                if where in self.last:
                    pe.wait_ge(*done("free", self.last[where]))
                self.last[where] = name
                st.tiles[name] = where
                return bank[where]

            def let_go(self, hold):
                del self.held[hold]

        def tile(name):
            return bank[st.banks.get(name, 0)]

        ring = Ring()

        def pe_turn_in(pe, G):
            for n, nm in enumerate(("x", "c")):
                b = ring.claim(pe, (G.n, "in", nm))
                for t in range(TT):
                    ins = pe.transpose(b[:, t * 128:(t + 1) * 128], G.rows[:, n, t, :], ident)
                ins.then_inc(*tick("pe", ("mm", (G.n, "in", nm))))

        def pe_product(pe, name, pairs, hold=None):
            b = ring.claim(pe, name, hold)
            for i, (w, m) in enumerate(pairs):
                ins = pe.matmul(b[0:w.shape[-1], :], w, m, start=(i == 0), stop=(i == len(pairs) - 1))
            ins.then_inc(*tick("pe", ("mm", name)))

        def pe_values(pe, G, tag, src, w):
            b = ring.claim(pe, (G.n, tag, "v"))
            for p in range(TT):
                ins = pe.matmul(b[:, p * D:(p + 1) * D], src[:, p * 128:(p + 1) * 128], w, start=True, stop=True)
            ins.then_inc(*tick("pe", ("mm", (G.n, tag, "v"))))

        def pe_scores(pe, G, tag, u, c):
            if (u, c) == (0, 0):
                pe.wait_ge(*done("qT", G.n, tag))
                pe.wait_ge(*done("km", G.n, tag))
            rows2 = (2 * c, 2 * c + 1)
            b2s = [ring.claim(pe, (G.n, tag, "s", u, r)) for r in rows2]
            for p in range(2):
                for b2 in range(2):
                    tok = (4 * u + 2 * p + b2) * S
                    for r, b in zip(rows2, b2s):
                        rows = slice(32 * r, 32 * r + 32)
                        ins = pe.matmul(b[64 * b2:64 * b2 + 64, p * 256:(p + 1) * 256].rearrange("q (j k) -> q j k", j=JH),
                                        G.qT[rows, tok:tok + S], G.km[rows, :, tok:tok + S], start=True, stop=True)
                        if p == 1 and b2 == 1:
                            ins.then_inc(*tick("pe", ("mm", (G.n, tag, "s", u, r))))

        def pe_turn_probs(pe, G, tag, u, c):
            for p in range(2):
                b = ring.claim(pe, (G.n, tag, "pT", u, p, c))
                for rr in range(2):
                    r = 2 * c + rr
                    pe.wait_ge(*done("exp", G.n, tag, u, r))
                    for jj in range(2):
                        a = p * 256 + jj * 128
                        ins = pe.transpose(b[:, (2 * rr + jj) * 128:(2 * rr + jj + 1) * 128], G.ss[:, r, a:a + 128], ident)
                ins.then_inc(*tick("pe", ("mm", (G.n, tag, "pT", u, p, c))))

        def pe_mix(pe, G, tag, u):
            b = ring.claim(pe, (G.n, tag, "o", u))
            if u == 0:
                pe.wait_ge(*done("vb", G.n, tag))
            for c in range(2):
                for p in range(2):
                    pe.wait_ge(*done("pT", G.n, tag, u, p, c))
            for p in range(2):
                for b2 in range(2):
                    for odd in range(2):
                        for m in range(HP // 2):
                            a = (2 * p + b2) * S
                            pe.matmul(b[32 * m:32 * m + 32, a:a + S], G.vb[tag[-1]][:, b2, 2 * u + p, m, odd * PV:odd * PV + 2 * PV],
                                      G.pT[:, p, 2 * m + odd, 64 * b2:64 * b2 + 64], start=not odd, stop=bool(odd))
            for odd in range(2):
                one = konst[:, K_ONE + odd * PV:K_ONE + odd * PV + 2 * PV]
                for m in range(HP // 2):
                    ins = pe.matmul(b[32 * m:32 * m + 32, T // 2:T].rearrange("f (p q) -> f p q", p=2), one,
                                    G.pT[:, :, 2 * m + odd, :], start=not odd, stop=bool(odd))
            ins.then_inc(*tick("pe", ("mm", (G.n, tag, "o", u))))

        def pe_mlp_out(pe, G, tag, w):
            b = ring.claim(pe, (G.n, tag, "y"))
            for c in range(FC):
                pe.wait_ge(*done("h", G.n, tag, c))
                ins = pe.matmul(b[:], w[:, c, :], G.hid[:, c, :], start=(c == 0), stop=(c == FC - 1))
            ins.then_inc(*tick("pe", ("mm", (G.n, tag, "y"))))

        def act_tables(act, number):
            act.add_instruction(mybir.InstLoadActFuncSet(name=nc.get_next_instruction_name(), act_func_set_id=number, ins=[], outs=[]))

        def act_out(act, G, name, dst, bias, *names, func=ACT.Identity):
            act.wait_ge(*done("mm", (G.n, *name)))
            act.activation(dst, tile((G.n, *name))[0:dst.shape[0], :], func, bias=bias)\
                .then_inc(*tick("act", ("free", (G.n, *name)), *names))

        def act_square(act, G, tag):
            act.wait_ge(*done("mm", (G.n, tag, "cen")))
            act.activation(G.sq[:], tile((G.n, tag, "cen"))[:], ACT.Square).then_inc(*tick("act", ("sq", G.n, tag)))

        def act_rstd(act, G, tag, eps):
            act.wait_ge(*done("mm", (G.n, tag, "var")))
            act.activation(G.rstd[:], tile((G.n, tag, "var"))[:], ACT.Ln, bias=konst[:, K_EPS + eps:K_EPS + eps + 1])\
                .then_inc(*tick("act", ("free", (G.n, tag, "var")), ("ln", G.n, tag)))
            act.wait_ge(*done("ln", G.n, tag))
            act.activation(G.rstd[:], G.rstd[:], ACT.Exp, scale=-0.5).then_inc(*tick("act", ("rstd", G.n, tag)))

        def act_keys(act, G, tag, bk):
            name = (G.n, tag, "k")
            act.wait_ge(*(done("mm", name) if bk is not None else done("kT", G.n, tag)))
            for j in range(JH):
                end = [("km", G.n, tag)] if j == JH - 1 else []
                one = konst[:, K_MASK + j:K_MASK + j + 1]
                if bk is not None:
                    act.activation(G.km[:, j, :], tile(name)[:], ACT.Identity, bias=kbias[:, bk, j:j + 1], scale=one)\
                        .then_inc(*tick("act", *([("free", name)] if end else []), *end))
                else:
                    act.activation(G.km[:, j, :], G.kT[:], ACT.Copy, scale=one).then_inc(*tick("act", *end))

        def act_values(act, G, tag):
            name = (G.n, tag, "v")
            act.wait_ge(*done("mm", name))
            src = tile(name)[:].rearrange("k (h o e d) -> k h o e d", h=TT * HP // 2, o=2, e=2)
            for b2 in range(2):
                dst = G.vb[tag[-1]][:, b2].rearrange("k p m (t w) -> k (p m) t w", t=3)
                for e in range(2):
                    end = [("free", name), ("vb", G.n, tag)] if (b2, e) == (1, 1) else []
                    act.activation(dst[64 * e:64 * e + 64, :, 0:3:2, HD * e:HD * e + HD], src[64 * b2:64 * b2 + 64, :, :, e, :],
                                   ACT.Copy).then_inc(*tick("act", *end))

        def act_exp(act, G, tag, u, c):
            for r in (2 * c, 2 * c + 1):
                act.wait_ge(*done("sub", G.n, tag, u, r))
                act.activation(G.ss[:, r, :], G.ss[:, r, :], ACT.Exp, scale=SCALE).then_inc(*tick("act", ("exp", G.n, tag, u, r)))

        def act_turn_probs(act, G, tag, u, c):
            for p in range(2):
                name = (G.n, tag, "pT", u, p, c)
                act.wait_ge(*done("mm", name))
                act.activation(G.pT[:, p, 4 * c:4 * c + 4, :].rearrange("k h q -> k (h q)"), tile(name)[:], ACT.Copy)\
                    .then_inc(*tick("act", ("free", name), ("pT", G.n, tag, u, p, c)))

        def act_mix(act, G, tag, u):
            name, rec = (G.n, tag, "o", u), G.rec[:, u]
            act.wait_ge(*done("mm", name))
            act.activation(rec, tile(name)[:, T // 2:T], ACT.Ln).then_inc(*tick("act", ("ln sum", G.n, tag, u)))
            act.wait_ge(*done("ln sum", G.n, tag, u))
            act.activation(rec, rec, ACT.Exp, scale=-1.0).then_inc(*tick("act", ("rec", G.n, tag, u)))

        def dve_scale(dve, G, tag, scale, dst):
            cen = (G.n, tag, "cen")
            dve.wait_ge(*done("sq", G.n, tag))
            dve.tensor_tensor(seqs(dst[:]), seqs(tile(cen)[:]), per_seq(G, scale), ALU.mult)\
                .then_inc(*tick("dve", ("free", cen), ("scaled", G.n, tag)))

        def dve_norm(dve, G, tag, shift, dst):
            cen = (G.n, tag, "cen")
            dve.wait_ge(*done("rstd", G.n, tag))
            if shift is None:
                dve.tensor_tensor(dst[:], tile(cen)[:], G.rstd[:], ALU.mult).then_inc(*tick("dve", ("free", cen), ("xn", G.n, tag)))
                return
            dve.wait_ge(*done("scaled", G.n, tag))
            dve.tensor_tensor(dst[:], dst[:], G.rstd[:], ALU.mult).then_inc(*tick("dve", ("xn 1", G.n, tag)))
            dve.wait_ge(*done("xn 1", G.n, tag))
            dve.tensor_tensor(seqs(dst[:]), seqs(dst[:]), per_seq(G, shift), ALU.add).then_inc(*tick("dve", ("xn", G.n, tag)))

        def dve_rotary(dve, G, tag, n, dst, name):
            wide = lambda a: konst[:, a:a + S].unsqueeze(1).broadcast_to((128, GB, S))
            straight, turned = (G.n, tag, n), (G.n, tag, n + " rot")
            dve.wait_ge(*done("mm", straight))
            dve.tensor_tensor(seqs(dst[:]), seqs(tile(straight)[:]), wide(K_COS), ALU.mult)\
                .then_inc(*tick("dve", ("free", straight), ("cos", G.n, tag, n)))
            dve.wait_ge(*done("mm", turned))
            dve.tensor_tensor(seqs(G.rot[:]), seqs(tile(turned)[:]), wide(K_SIN), ALU.mult)\
                .then_inc(*tick("dve", ("free", turned), ("sin", G.n, tag, n)))
            dve.wait_ge(*done("sin", G.n, tag, n))
            dve.tensor_tensor(dst[:], dst[:], G.rot[:], ALU.add).then_inc(*tick("dve", (name, G.n, tag)))
            dve.wait_ge(*done(name, G.n, tag))

        def dve_scores(dve, G, tag, u, c, masked):
            heads = lambda ap: ap.rearrange("q (g k) -> q g k", k=S)
            for r in (2 * c, 2 * c + 1):
                name = (G.n, tag, "s", u, r)
                src = tile(name)[:]
                dve.wait_ge(*done("mm", name))
                if masked:
                    quad = lambda ap, p: ap[:, p * 256:(p + 1) * 256].rearrange("q (j k) -> q j k", j=JH)
                    for p in range(2):
                        dve.tensor_tensor(quad(G.ss[:, r, :], p), quad(src, p),
                                          G.pen[:, 2 * u + p, :].unsqueeze(1).broadcast_to((128, JH, S)), ALU.add)\
                            .then_inc(*tick("dve", ("masked", G.n, tag, u, r, p), *([("free", name)] if p else [])))
                    src = G.ss[:, r, :]
                    dve.wait_ge(*done("masked", G.n, tag, u, r, 1))
                dve.tensor_reduce(G.mx[:, 0, r, :], heads(src), AX_X, ALU.max).then_inc(*tick("dve", ("max", G.n, tag, u, r)))
                dve.wait_ge(*done("max", G.n, tag, u, r))
                dve.tensor_tensor(heads(G.ss[:, r, :]), heads(src), G.mx[:, 0, r, :].unsqueeze(2).broadcast_to((128, GB, S)), ALU.subtract)\
                    .then_inc(*tick("dve", ("sub", G.n, tag, u, r), *([] if masked else [("free", name)])))

        def dve_mix(dve, G, tag, u):
            name, half = (G.n, tag, "o", u), T // 2
            dve.wait_ge(*done("rec", G.n, tag, u))
            dve.tensor_tensor(G.oT[:, u * half:(u + 1) * half], tile(name)[:, 0:half], G.rec[:, u], ALU.mult)\
                .then_inc(*tick("dve", ("free", name), ("oT", G.n, tag, u)))

        def dve_residual(dve, G, name, bias, gate, end):
            name, x = (G.n, *name), G.x
            dve.wait_ge(*done("mm", name))
            if gate is None and bias is None:
                dve.tensor_tensor(x[:], tile(name)[:], x[:], ALU.add).then_inc(*tick("dve", ("free", name), ("x", G.n, end)))
            elif gate is None:
                dve.scalar_tensor_tensor(x[:], tile(name)[:], bias, x[:], ALU.add, ALU.add)\
                    .then_inc(*tick("dve", ("free", name), ("x", G.n, end)))
            else:
                dve.scalar_tensor_tensor(seqs(G.tmp[:, 1, :]), seqs(tile(name)[:]), bias, gate, ALU.add, ALU.mult)\
                    .then_inc(*tick("dve", ("free", name), ("gated", G.n, end)))
                dve.wait_ge(*done("gated", G.n, end))
                dve.tensor_tensor(x[:], x[:], G.tmp[:, 1, :], ALU.add).then_inc(*tick("dve", ("x", G.n, end)))

        def pe_keys0(pe, G):
            pe.wait_ge(*done("c", G.n))
            pe_product(pe, (G.n, "0", "k"), [(w0k[:], G.cT[:])])
            for v in range(2):
                b = ring.claim(pe, (G.n, "0", "v", v))
                for i in range(4):
                    s = (4 * v + i) * S
                    ins = pe.matmul(b[0:S, i * D:(i + 1) * D], G.cT[:, s:s + S], w0v[:], start=True, stop=True)
                ins.then_inc(*tick("pe", ("mm", (G.n, "0", "v", v))))

        def act_keys0(act, G):
            act_out(act, G, ("0", "k"), G.kT[:], 0.0, ("kT", G.n, "0"))
            for v in range(2):
                act_out(act, G, ("0", "v", v), G.v0[:, v, :], 0.0, ("v", G.n, v))

        def dve_norm0(dve, G):
            cen = (G.n, "0", "cen")
            dve.wait_ge(*done("rstd", G.n, "0"))
            dve.scalar_tensor_tensor(G.xn[:], tile(cen)[:], col("L0_xcond_ln_gamma"), G.rstd[:], ALU.mult, ALU.mult)\
                .then_inc(*tick("dve", ("free", cen), ("xn 1", G.n, "0")))
            dve.wait_ge(*done("xn 1", G.n, "0"))
            dve.tensor_scalar(G.xn[:], G.xn[:], col("L0_xcond_ln_beta"), None, ALU.add).then_inc(*tick("dve", ("xn", G.n, "0")))

        def pe_scores0(pe, G):
            pe.wait_ge(*done("qT", G.n, "0"))
            pe.wait_ge(*done("kT", G.n, "0"))
            b = ring.claim(pe, (G.n, "0", "s"))
            for q in range(GB):
                ins = pe.matmul(b[64 * (q % 2):64 * (q % 2) + 64, (q // 2) * S:(q // 2 + 1) * S],
                                G.qT[:, q * S:(q + 1) * S], G.kT[:, q * S:(q + 1) * S], start=True, stop=True)
            ins.then_inc(*tick("pe", ("mm", (G.n, "0", "s"))))

        def dve_scores0(dve, G):
            pairs = lambda ap: ap.rearrange("q (p k) -> q p k", k=S)
            wide = lambda ap: ap.unsqueeze(2).broadcast_to((128, GB // 2, S))
            name = (G.n, "0", "s")
            s, p0 = tile(name)[:, 0:256], G.ss[:, 0, 0:256]
            top, total, rec = (G.mx[:, 0, r, 0:GB // 2] for r in range(3))
            dve.wait_ge(*done("mm", name))
            dve.tensor_reduce(top, pairs(s), AX_X, ALU.max).then_inc(*tick("dve", ("max", G.n, "0")))
            dve.wait_ge(*done("max", G.n, "0"))
            dve.tensor_tensor(pairs(p0), pairs(s), wide(top), ALU.subtract).then_inc(*tick("dve", ("sub", G.n, "0"), ("free", name)))
            dve.wait_ge(*done("exp", G.n, "0"))
            dve.tensor_reduce(total, pairs(p0), AX_X, ALU.add).then_inc(*tick("dve", ("sum", G.n, "0")))
            dve.wait_ge(*done("sum", G.n, "0"))
            dve.reciprocal(rec, total).then_inc(*tick("dve", ("rec", G.n, "0")))
            dve.wait_ge(*done("rec", G.n, "0"))
            dve.tensor_tensor(pairs(p0), pairs(p0), wide(rec), ALU.mult).then_inc(*tick("dve", ("p", G.n, "0")))

        def act_scores0(act, G):
            act.wait_ge(*done("sub", G.n, "0"))
            act.activation(G.ss[:, 0, 0:256], G.ss[:, 0, 0:256], ACT.Exp, scale=SCALE0).then_inc(*tick("act", ("exp", G.n, "0")))

        def pe_turn_probs0(pe, G):
            pe.wait_ge(*done("p", G.n, "0"))
            b = ring.claim(pe, (G.n, "0", "pT"))
            for p in range(GB // 2):
                ins = pe.transpose(b[0:S, p * 128:(p + 1) * 128], G.ss[:, 0, p * S:(p + 1) * S], ident)
            ins.then_inc(*tick("pe", ("mm", (G.n, "0", "pT"))))

        def pe_evidence(pe, G):
            pe.wait_ge(*done("pT", G.n, "0"))
            pe.wait_ge(*done("v", G.n, 1))
            b = ring.claim(pe, (G.n, "0", "ev"))
            for q in range(GB):
                ins = pe.matmul(b[:, q * S:(q + 1) * S], G.v0[:, q // 4, (q % 4) * D:(q % 4 + 1) * D],
                                G.oT[0:S, q * S:(q + 1) * S], start=True, stop=True)
            ins.then_inc(*tick("pe", ("mm", (G.n, "0", "ev"))))

        def pe_route(pe, G):
            pe.wait_ge(*done("lg", G.n))
            b = ring.claim(pe, (G.n, "0", "lgT"))
            for t in range(TT):
                ins = pe.transpose(b[:, 4 * t:4 * t + 4], G.lg[:, t * 128:(t + 1) * 128], ident[0:4, 0:4])
            ins.then_inc(*tick("pe", ("mm", (G.n, "0", "lgT"))))

        def dve_route(dve, G):
            three = lambda ap: ap.rearrange("t (n e) -> t n e", e=4)[:, :, 0:NE]
            wide3 = lambda ap: ap.unsqueeze(2).broadcast_to((128, TT, NE))
            small, name = G.small, (G.n, "0", "lgT")
            top, total, rec = (small[:, 0, i * TT:(i + 1) * TT] for i in range(3))
            lgT = three(tile(name)[:, 0:4 * TT])
            dve.wait_ge(*done("mm", name))
            dve.tensor_reduce(top, lgT, AX_X, ALU.max).then_inc(*tick("dve", ("route max", G.n)))
            dve.wait_ge(*done("route max", G.n))
            dve.tensor_tensor(three(small[:, 1, :]), lgT, wide3(top), ALU.subtract).then_inc(*tick("dve", ("free", name), ("route sub", G.n)))
            dve.wait_ge(*done("route exp", G.n))
            dve.tensor_reduce(total, three(small[:, 2, :]), AX_X, ALU.add).then_inc(*tick("dve", ("route sum", G.n)))
            dve.wait_ge(*done("route sum", G.n))
            dve.reciprocal(rec, total).then_inc(*tick("dve", ("route rec", G.n)))
            dve.wait_ge(*done("route rec", G.n))
            dve.tensor_tensor(three(small[:, 5, :]), three(small[:, 2, :]), wide3(rec), ALU.mult).then_inc(*tick("dve", ("route", G.n)))

        def act_route(act, G):
            three = lambda ap: ap.rearrange("t (n e) -> t n e", e=4)[:, :, 0:NE]
            act.wait_ge(*done("route sub", G.n))
            act.activation(three(G.small[:, 2, :]), three(G.small[:, 1, :]), ACT.Exp).then_inc(*tick("act", ("route exp", G.n)))

        def pe_experts_in(pe, G):
            for e in range(NE):
                for h in range(2):
                    a = h * D
                    pe_product(pe, (G.n, "0", "h", 2 * e + h), [(w0e1[:, e, 0, a:a + D], G.xn[:]), (w0e1[:, e, 1, a:a + D], G.rot[:])])
            pe_product(pe, (G.n, "0", "g1"), [(w0g1[:, 0, :], G.xn[:]), (w0g1[:, 1, :], G.rot[:])])

        def dve_experts_in(dve, G):
            for n in range(2 * NE + 1):
                name = (G.n, "0", "h", n) if n < 2 * NE else (G.n, "0", "g1")
                dve.wait_ge(*done("mm", name))
                if n >= 2:
                    dve.wait_ge(*done("h", G.n, "0", n - 2))
                dve.tensor_tensor(seqs(G.tmp[:, n % 2, :]), seqs(tile(name)[:]), per_seq(G, MA + n), ALU.add)\
                    .then_inc(*tick("dve", ("free", name), ("h pre", G.n, n)))

        def act_experts_in(act, G):
            for n in range(2 * NE + 1):
                act.wait_ge(*done("h pre", G.n, n))
                dst = G.hid[:, n, :] if n < 2 * NE else G.qT[:]
                act.activation(dst, G.tmp[:, n % 2, :], ACT.Silu).then_inc(*tick("act", ("h", G.n, "0", n)))

        def pe_experts_out(pe, G):
            pe.wait_ge(*done("route", G.n))
            for e in range(NE):
                b = ring.claim(pe, (G.n, "0", "pb", e))
                for t in range(TT):
                    ins = pe.matmul(b[:, t * 128:(t + 1) * 128], G.small[:, 5, 4 * t + e:4 * t + e + 1].broadcast_to((128, 128)),
                                    ident, start=True, stop=True)
                ins.then_inc(*tick("pe", ("mm", (G.n, "0", "pb", e))))
            for e in range(NE):
                pe.wait_ge(*done("h", G.n, "0", 2 * e + 1))
                pe_product(pe, (G.n, "0", "e", e), [(w0e2[:, e, h, :], G.hid[:, 2 * e + h, :]) for h in range(2)])

        def act_experts_out(act, G):
            for e in range(NE):
                act_out(act, G, ("0", "pb", e), G.prob[:, e, :], 0.0, ("pb", G.n, e))

        def dve_experts_out(dve, G):
            for e in range(NE):
                name = (G.n, "0", "e", e)
                dve.wait_ge(*done("mm", name))
                dve.wait_ge(*done("pb", G.n, e))
                dst = G.kT[:] if e == 0 else G.tmp[:, 1, :]
                dve.scalar_tensor_tensor(dst, tile(name)[:], col("L0_xcond_e_b2", e), G.prob[:, e, :], ALU.add, ALU.mult)\
                    .then_inc(*tick("dve", ("free", name), ("routed", G.n, 0) if e == 0 else ("expert", G.n, e)))
                if e:
                    dve.wait_ge(*done("expert", G.n, e))
                    dve.tensor_tensor(G.kT[:], G.kT[:], G.tmp[:, 1, :], ALU.add).then_inc(*tick("dve", ("routed", G.n, e)))
                    dve.wait_ge(*done("routed", G.n, e))

        def norm_stages(G, tag, before, scale, shift, dst, eps, src, more=(None, None)):
            nothing = (None, None, None)
            one, two = (m or nothing for m in more)

            def pe_a(pe):
                pe.wait_ge(*done(*before))
                pe_product(pe, (G.n, tag, "cen"), [(center, src[:])], hold=(G.n, tag))
                if one[0]:
                    one[0](pe)

            def act_a(act):
                act_square(act, G, tag)
                if one[1]:
                    one[1](act)

            def pe_b(pe):
                pe.wait_ge(*done("sq", G.n, tag))
                pe_product(pe, (G.n, tag, "var"), [(average, G.sq[:])])
                ring.let_go((G.n, tag))
                if two[0]:
                    two[0](pe)

            def act_b(act):
                act_rstd(act, G, tag, eps)
                if two[1]:
                    two[1](act)

            def dve_b(dve):
                if tag == "0":
                    dve_norm0(dve, G)
                else:
                    dve_norm(dve, G, tag, shift, dst)
                if two[2]:
                    two[2](dve)

            def dve_a(dve):
                if scale is not None:
                    dve_scale(dve, G, tag, scale, dst)

            return [(pe_a, act_a, dve_a, "center"), (pe_b, act_b, dve_b, "norm")]

        weights = {1: w1, 2: w2, 3: w3}

        def queries(G, tag, L, cross, ready, bq):
            w = weights[L]

            def pe_q(pe):
                pe.wait_ge(*done(*ready))
                pe_product(pe, (G.n, tag, "q"), [(w["q"][:, 0, :] if cross else w["qkv"][:, 0, :], G.xn[:])])
                if L == 3:
                    pe_product(pe, (G.n, tag, "q rot"), [(w["rot"][:, 2 * cross, :], G.xn[:])])

            def act_q(act):
                if L < 3:
                    act_out(act, G, (tag, "q"), G.qT[:], bq, ("qT", G.n, tag))

            def dve_q(dve):
                if L == 3:
                    dve_rotary(dve, G, tag, "q", G.qT, "qT")
            return pe_q, act_q, dve_q, "product"

        def keys(G, tag, L, cross, src, ready, bk):
            w = weights[L]

            def pe_k(pe):
                pe.wait_ge(*done(*ready))
                pe_product(pe, (G.n, tag, "k"), [(w["kv"][:, 0, :] if cross else w["qkv"][:, 1, :], src[:])])
                if L == 3:
                    pe_product(pe, (G.n, tag, "k rot"), [(w["rot"][:, 2 * cross + 1, :], src[:])])

            def act_k(act):
                act_keys(act, G, tag, bk if L < 3 else None)

            def dve_k(dve):
                if L == 3:
                    dve_rotary(dve, G, tag, "k", G.kT, "kT")
            return pe_k, act_k, dve_k, "keys"

        def values(G, tag, L, cross, src):
            w = weights[L]
            return (lambda pe: pe_values(pe, G, tag, src, w["kv"][:, 1, :] if cross else w["qkv"][:, 2, :]),
                    lambda act: act_values(act, G, tag), None, "values")

        def attention_core(G, tag, masked, tail):
            def scores(u, c):
                return (lambda pe: pe_scores(pe, G, tag, u, c), None, lambda dve: dve_scores(dve, G, tag, u, c, masked), "scores")

            def exps(u, c):
                return None, lambda act: act_exp(act, G, tag, u, c), None, "exps"

            def turn(u, c):
                return lambda pe: pe_turn_probs(pe, G, tag, u, c), lambda act: act_turn_probs(act, G, tag, u, c), None, "turn"

            def mix(u):
                return lambda pe: pe_mix(pe, G, tag, u), lambda act: act_mix(act, G, tag, u), lambda dve: dve_mix(dve, G, tag, u), "mix"

            tail = tail + [None, None]
            return [t for t in (
                (*scores(0, 0)[0:3], "first scores"), scores(0, 1), exps(0, 0), turn(0, 0), scores(1, 0), exps(0, 1), turn(0, 1), scores(1, 1),
                exps(1, 0), (*mix(0)[0:3], "first mix"), turn(1, 0),
                exps(1, 1), tail[0], turn(1, 1), tail[1], mix(1), *tail[2:]) if t]

        def projection(G, tag, w, bias, gate):
            def pe_p(pe):
                for u in range(2):
                    pe.wait_ge(*done("oT", G.n, tag, u))
                pe_product(pe, (G.n, tag, "proj"), [(w[:, 0, :], G.oT[:])])
            return pe_p, None, lambda dve: dve_residual(dve, G, (tag, "proj"), bias, gate, tag), "product"

        def mlp_stages(G, tag, L, func, b1, b2, gate, end):
            w = weights[L]

            def pe_h(pe):
                pe.wait_ge(*done("xn", G.n, tag))
                for c in range(FC):
                    pe_product(pe, (G.n, tag, "h", c), [(w["fc1"][:, c, :], G.xn[:])])

            def act_h(act):
                for c in range(FC):
                    act_out(act, G, (tag, "h", c), G.hid[:, c, :], col(b1, c), ("h", G.n, tag, c), func=func)
                act_tables(act, 6)
            return [(pe_h, act_h, None, "mlp in"),
                    (lambda pe: pe_mlp_out(pe, G, tag, w["fc2"]), None,
                     lambda dve: dve_residual(dve, G, (tag, "y"), col(b2), gate, end), "mlp out")]

        def stages_of(G):
            n = G.n

            def act_in(act):
                for nm, dst in (("x", G.x), ("c", G.cT)):
                    act_out(act, G, ("in", nm), dst[:], 0.0, ("x", n, "in") if nm == "x" else ("c", n))

            out = [(lambda pe: pe_turn_in(pe, G), act_in, None, "turn in")]
            out += norm_stages(G, "0", ("x", n, "in"), None, None, G.xn, 0, G.x,
                               more=((lambda pe: pe_keys0(pe, G), lambda act: act_keys0(act, G), None), None))

            def pe_q0(pe):
                pe.wait_ge(*done("xn", n, "0"))
                pe_product(pe, (n, "0", "q"), [(w0q[:], G.xn[:])])

            out.append((pe_q0, lambda act: act_out(act, G, ("0", "q"), G.qT[:], 0.0, ("qT", n, "0")), None, "product"))
            out.append((lambda pe: pe_scores0(pe, G), lambda act: act_scores0(act, G), lambda dve: dve_scores0(dve, G), "scores 0"))
            out.append((lambda pe: pe_turn_probs0(pe, G),
                        lambda act: act_out(act, G, ("0", "pT"), G.oT[0:S, :], 0.0, ("pT", n, "0")), None, "turn"))
            out.append((lambda pe: pe_evidence(pe, G), lambda act: act_out(act, G, ("0", "ev"), G.rot[:], 0.0, ("ev", n)), None, "product"))

            def pe_logits(pe):
                pe.wait_ge(*done("ev", n))
                pe_product(pe, (n, "0", "lg"), [(w0r[:, 0, :], G.xn[:]), (w0r[:, 1, :], G.rot[:]), (w0r[:, 2, :], per_seq(G, MCOND))])

            out.append((pe_logits, lambda act: act_out(act, G, ("0", "lg"), G.lg, rbias[:], ("lg", n)), None, "product"))
            out.append((lambda pe: pe_route(pe, G), lambda act: act_route(act, G), lambda dve: dve_route(dve, G), "route"))
            out.append((lambda pe: pe_experts_in(pe, G), lambda act: act_experts_in(act, G), lambda dve: dve_experts_in(dve, G), "experts in"))
            out.append((lambda pe: pe_experts_out(pe, G), lambda act: act_experts_out(act, G), lambda dve: dve_experts_out(dve, G), "experts out"))

            def pe_out0(pe):
                pe.wait_ge(*done("h", n, "0", 2 * NE))
                pe_product(pe, (n, "0", "g2"), [(w0g2[:], G.qT[:])])
                pe.wait_ge(*done("routed", n, NE - 1))
                pe_product(pe, (n, "0", "out"), [(w0o[:], G.kT[:])])

            def act_gate(act):
                act_out(act, G, ("0", "g2"), G.sq[:], col("L0_xcond_gate_b2"), ("gate", n), func=ACT.Sigmoid)
                act_tables(act, 6)

            def dve_out0(dve):
                dve.wait_ge(*done("gate", n))
                dve_residual(dve, G, ("0", "out"), col("L0_xcond_out_b"), seqs(G.sq[:]), "0")

            out.append((pe_out0, act_gate, dve_out0, "product"))

            for L, p in ((1, "L1_xcond_"), (2, "L2_xcond_"), (3, "L3_xcond_")):
                eps = 0 if L == 3 else 1
                s, c, a, b, m = (f"{L}{k}" for k in "sxabm")
                w, last = weights[L], f"{L - 1}"
                base = {1: M1, 2: M2, 3: M3}[L]
                na, nb, nm = {1: ((1, 0), None, (4, 3)), 2: ((1, 0), None, (4, 3)), 3: ((0, 1), (2, 3), (4, 5))}[L]
                na, nb, nm = ((base + i[0], base + i[1]) if i else (None, None) for i in (na, nb, nm))
                ga, gm = (per_seq(G, base + 2), per_seq(G, base + 5)) if L < 3 else (None, None)
                bias = {1: lambda k, i=0: col(p + {"q": "qkv_b", "proj": "sa_proj_b", "cq": "q_b", 
                                                   "cproj": "ca_proj_b"}[k], i),
                        2: lambda k, i=0: col(p + {"q": "b_qkv", "proj": "b_proj", "cq": "b_qc", 
                                                   "cproj": "b_cproj"}[k], i)}.get(L)
                ctx_src, ctx_ready = (G.cn, ("xn", n, "2c")) if L == 2 else (G.cT, ("c", n))

                out += norm_stages(G, a, ("x", n, last), *na, G.xn, eps, G.x)
                out.append(queries(G, s, L, 0, ("xn", n, a), bias("q", 0) if bias else 0.0))
                out.append(keys(G, s, L, 0, G.xn, ("xn", n, a), {1: 0, 2: 2, 3: None}[L]))
                out.append(values(G, s, L, 0, G.xn))
                tail = norm_stages(G, "2c", ("c", n), None, None, G.cn, 1, G.cT) if L == 2 else []
                tail += [keys(G, c, L, 1, ctx_src, ctx_ready, {1: 1, 2: 3, 3: None}[L]), values(G, c, L, 1, ctx_src)]
                out += attention_core(G, s, False, tail)
                out.append(projection(G, s, w["proj"], bias("proj") if bias else None, ga))
                out += norm_stages(G, b, ("x", n, s), *nb, G.xn, eps, G.x)
                out.append(queries(G, c, L, 1, ("xn", n, b), bias("cq") if bias else 0.0))
                out += attention_core(G, c, L == 1, [])
                out.append(projection(G, c, w["cproj"], bias("cproj") if bias else None, None))
                out += norm_stages(G, m, ("x", n, c), *nm, G.xn, eps, G.x)
                b1, b2 = {1: ("fc1_b", "fc2_b"), 2: ("b_mlp1", "b_mlp2"), 3: ("ffn_b1", "ffn_b2")}[L]
                out += mlp_stages(G, m, L, ACT.Gelu_apprx_tanh if L == 2 else ACT.Gelu, p + b1, p + b2, gm, f"{L}")

            def pe_out(pe):
                pe.wait_ge(*done("x", n, "3"))
                b = ring.claim(pe, (n, "out"))
                for t in range(TT):
                    ins = pe.transpose(b[:, t * 128:(t + 1) * 128], G.x[:, t * 128:(t + 1) * 128], ident)
                ins.then_inc(*tick("pe", ("mm", (n, "out"))))

            out.append((pe_out, lambda act: act_out(act, G, ("out",), G.tmp[:, 0, :], 0.0, ("rows", n)), None, "turn out"))
            return out

        plan = []
        for g, G in enumerate(groups):
            start = LAG * g
            for k, stage in enumerate(stages_of(G)):
                plan.append((start, g, k, stage))
                start += PACE[stage[3]]
        order = [p[3] for p in sorted(plan, key=lambda p: p[:3])]

        with nc.Fori(0, NG // NS) as i:
            with nc.Block() as block:
                @block.sync
                def _(sp):
                    for G in groups:
                        sp.wait_ge(*done("mm", (G.n, "in", "c")))
                        load_group(sp, G, next_row(i, G.n), stored)
                    for G in groups:
                        sp.wait_ge(*done("rows", G.n))
                        sp.dma_start(out_rows[bass.ds((i * NS + G.n) * T, T), :].rearrange("(t p) d -> p t d", p=128),
                                     G.tmp[:, 0, :].rearrange("p (t d) -> p t d", d=D)).then_inc(stored, 16)
                    sp.wait_ge(stored, 48 * NS)

                @block.tensor
                def _(pe):
                    pe.wait_ge(*done("mod", NS - 1))
                    for stage in order:
                        if stage[0]:
                            stage[0](pe)

                @block.scalar
                def _(act):
                    act_tables(act, 6)
                    for stage in order:
                        if stage[1]:
                            stage[1](act)

                @block.vector
                def _(dve):
                    for G in groups:
                        g = i * NS + G.n
                        dve.tensor_copy(G.mod[:], table[:, :, bass.ds(g * GB, GB)]).then_inc(*tick("dve", ("mod", G.n)))
                        dve.tensor_scalar(G.pen[:], mask8[:, bass.ds(g * (GB // 2), GB // 2), :], -3e38, 1e10, ALU.mult, ALU.mult)\
                            .then_inc(*tick("dve", ("pen", G.n)))
                    dve.wait_ge(*done("pen", NS - 1))
                    for stage in order:
                        if stage[2]:
                            stage[2](dve)

            nc.all_engine_barrier(sems_to_clear=counters)
    return st


def next_row(i, n):
    return ((NS * (i + 1) + n) % NG) * T


_INS = ["x", "cond_1024", "ctx_1024", "mask_BxS2_bf0"] + list(COLS) + [
    "L0_xcond_Wq", "L0_xcond_Wk", "L0_xcond_Wv", "L0_xcond_router_W", "L0_xcond_router_b", "L0_xcond_e_w1", "L0_xcond_e_w2",
    "L0_xcond_gate_w1", "L0_xcond_gate_w2", "L0_xcond_out_w", "L1_xcond_ada_w", "L1_xcond_qkv_w", "L1_xcond_sa_proj_w",
    "L1_xcond_q_w", "L1_xcond_kv_w", "L1_xcond_ca_proj_w", "L1_xcond_fc1_w", "L1_xcond_fc2_w", "L2_xcond_W_mod",
    "L2_xcond_W_qkv", "L2_xcond_W_proj", "L2_xcond_W_qc", "L2_xcond_W_kvc", "L2_xcond_W_cproj", "L2_xcond_W_mlp1",
    "L2_xcond_W_mlp2", "L3_xcond_ln1_w", "L3_xcond_ln2_w", "L3_xcond_ln3_w", "L3_xcond_qkv_w", "L3_xcond_sa_out_w",
    "L3_xcond_q_w", "L3_xcond_k_w", "L3_xcond_v_w", "L3_xcond_ca_out_w", "L3_xcond_ffn_w1", "L3_xcond_ffn_w2"]


def kernel(**inputs):
    import concourse.bacc as bacc
    from concourse.bass_utils import run_bass_kernel_spmd

    arrays = {n: np.ascontiguousarray(inputs[n]) for n in _INS}
    arrays["consts"] = shape_constants()
    found, tiles = {}, {}
    for _ in range(2):
        nc = bacc.Bacc("TRN2", target_bir_lowering=False, num_devices=1)
        io = {n: nc.dram_tensor(f"in_{n}_dram", a.shape, mybir.dt.from_np(a.dtype), kind="ExternalInput").ap()
              for n, a in arrays.items()}
        io["out"] = nc.dram_tensor("out_0_dram", (B, S, D), F32, kind="ExternalOutput").ap()
        steps = build(nc, io, found, tiles)
        found, tiles = steps.found, steps.tiles
    r = run_bass_kernel_spmd(nc, [{f"in_{n}_dram": a for n, a in arrays.items()}], core_ids=[0])
    return r.results[0]["out_0_dram"]
```

```python
from contextlib import ExitStack

import concourse.bass as bass
import numpy as np
from concourse import mybir

F32 = mybir.dt.float32
U8 = mybir.dt.uint8
ALU = mybir.AluOpType
ACT = mybir.ActivationFunctionType
AX_X = mybir.AxisListType.X

D = 128
S = 64
B = 128
GB = 4
T = GB * S
NG = B // GB
NS = 4
ROUNDS = 2
GI = NS * ROUNDS
START = (0, 3.27, 12, 23.1)
PLAN = {"turn in": (0.43, 1.66), "center 0": (1.7, 0.72), "center a": (0.43, 0.55), "center b": (0.37, 0.5),
        "center m": (0.0, 0.5), "center c": (0.43, 0.5), "norm 0": (0.43, 1.8), "norm a": (0.43, 2.2),
        "norm b": (0.43, 1.8), "norm m": (0.43, 1.15), "norm c": (0.43, 0.35), "queries": (0.43, 0.1), "keys": (0.43, 0.2),
        "values": (0.43, 1.0), "projection": (0.43, 1.2), "product": (0.61, 0.86), "first scores": (1.8, 0.1),
        "scores": (1.8, 1.0), "exps": (0, 0), "turn": (0.87, 0.5), "last exps": (0, 0.65), "last turn": (0.87, 1.38),
        "mix": (2.3, 1.6), "mlp in": (1.7, 1.0), "mlp out": (1.7, 0.77), "experts in": (6, 1.05),
        "experts out": (3.4, 0.91), "route": (0.1, 1.5), "scores 0": (0.25, 2.95), "turn 0": (0.25, 1.58),
        "turn out": (0.25, 0.5)}
TT = T // 128
NH = 16
HD = D // NH
RG = 4
JH = NH // RG
HP = NH // 2
PV = 2 * HD
FC = 4
NE = 3
BANKS = 8
SCALE = float(HD) ** -0.5
SCALE0 = float(D) ** -0.5

M1, M2, M3, MA, MGATE, MROUTE = 0, 6, 12, 18, 24, 25
NM = 26

COLS = {}


def _column(name, n):
    COLS[name] = (sum(k for _, k in COLS.values()), n)


for _name, _n in [("L0_xcond_ln_gamma", 1), ("L0_xcond_ln_beta", 1), ("L0_xcond_e_b1", 6), ("L0_xcond_e_b2", 3),
                  ("L0_xcond_gate_b1", 1), ("L0_xcond_gate_b2", 1), ("L0_xcond_out_b", 1),
                  ("L1_xcond_ada_b", 6), ("L1_xcond_qkv_b", 3), ("L1_xcond_sa_proj_b", 1), ("L1_xcond_q_b", 1),
                  ("L1_xcond_kv_b", 2), ("L1_xcond_ca_proj_b", 1), ("L1_xcond_fc1_b", 4), ("L1_xcond_fc2_b", 1),
                  ("L2_xcond_b_mod", 6), ("L2_xcond_b_qkv", 3), ("L2_xcond_b_proj", 1), ("L2_xcond_b_qc", 1),
                  ("L2_xcond_b_kvc", 2), ("L2_xcond_b_cproj", 1), ("L2_xcond_b_mlp1", 4), ("L2_xcond_b_mlp2", 1),
                  ("L3_xcond_ln1_b", 2), ("L3_xcond_ln2_b", 2), ("L3_xcond_ln3_b", 2),
                  ("L3_xcond_ffn_b1", 4), ("L3_xcond_ffn_b2", 1)]:
    _column(_name, _n)
NCOL = sum(k for _, k in COLS.values())

K_ID, K_CEN, K_AVG, K_MASK, K_COS, K_SIN, K_EPS, K_ONE = 0, 128, 256, 384, 388, 452, 516, 518
NK = K_ONE + 3 * PV


def shape_constants():
    k = np.zeros((128, NK), np.float32)
    k[:, K_ID:K_ID + 128] = np.eye(128)
    k[:, K_CEN:K_CEN + 128] = np.eye(128) - 1.0 / 128
    k[:, K_AVG:K_AVG + 128] = 1.0 / 128
    p = np.arange(128)
    for j in range(JH):
        k[:, K_MASK + j] = (p // HD) % JH == j
    half = HD // 2
    inv = (np.float32(1.0) / np.float32(10000.0) ** (np.arange(half, dtype=np.float32) / np.float32(half))).astype(np.float32)
    ang = (np.arange(S, dtype=np.float32)[None, :] * inv[p % half][:, None]).astype(np.float32)
    k[:, K_COS:K_COS + S] = np.cos(ang)
    k[:, K_SIN:K_SIN + S] = np.sin(ang)
    k[:, K_EPS] = 1e-5
    k[:, K_EPS + 1] = 1e-6
    for start in (K_ONE, K_ONE + 2 * PV):
        k[0:64, start:start + HD] = 1
        k[64:128, start + HD:start + PV] = 1
    return k


class Steps:

    def __init__(self, known, banks):
        self.known, self.banks = known, banks
        self.found, self.tiles, self.count, self.sem = {}, {}, {}, {}

    def start(self, sems):
        self.sem = sems
        self.count = {e: 0 for e in sems}

    def tick(self, engine, *names):
        self.count[engine] += 1
        for n in names:
            assert n not in self.found, n
            self.found[n] = (engine, self.count[engine])
        return self.sem[engine], 1

    def done(self, *name):
        engine, value = self.known.get(name, ("pe", 1))
        return self.sem[engine], value


def build(nc, io, known, tiles):
    st = Steps(known, tiles)
    tick, done = st.tick, st.done

    with ExitStack() as ctx:
        def sb(name, shape, dt=F32):
            return ctx.enter_context(nc.sbuf_tensor(name, shape, dt))

        def sem(name):
            return ctx.enter_context(nc.semaphore(name))

        bank = [ctx.enter_context(nc.psum_tensor(f"bank{i}", [128, 512], F32)) for i in range(BANKS)]

        konst = sb("konst", [128, NK])
        cols = sb("cols", [128, NCOL])
        rbias, rbias3 = sb("rbias", [4, 1]), sb("rbias3", [NE, 1])
        w0q, w0k, w0v = sb("w0q", [128, D]), sb("w0k", [128, D]), sb("w0v", [128, D])
        w0r = sb("w0r", [128, 3, 4])
        w0e1 = sb("w0e1", [128, NE, 3, 2 * D])
        w0e2 = sb("w0e2", [128, NE, 2, D])
        w0g1, w0g2, w0o = sb("w0g1", [128, 3, D]), sb("w0g2", [128, D]), sb("w0o", [128, D])
        w1 = {n: sb("w1" + n, [128, k, D]) for n, k in (("qkv", 3), ("proj", 1), ("q", 1), ("kv", 2), ("cproj", 1), ("fc1", 4), ("fc2", 4))}
        w2 = {n: sb("w2" + n, [128, k, D]) for n, k in (("qkv", 3), ("proj", 1), ("q", 1), ("kv", 2), ("cproj", 1), ("fc1", 4), ("fc2", 4))}
        w3 = {n: sb("w3" + n, [128, k, D]) for n, k in (("qkv", 3), ("proj", 1), ("q", 1), ("kv", 2), ("cproj", 1), ("fc1", 4), ("fc2", 4), ("rot", 4))}
        table = sb("table", [128, NM, B])
        mask8 = sb("mask8", [128, B // 2, S], U8)

        buffers = {}

        class Group:

            def __init__(self, n):
                self.n, self.stream = n, n % NS

                def own(name, shape, dt=F32):
                    key = f"{name}{self.stream}"
                    if key not in buffers:
                        buffers[key] = sb(key, shape, dt)
                    return buffers[key]

                self.rows = own("rows", [128, 2, TT, D])
                self.x, self.cT = own("x", [128, T]), own("cT", [128, T])
                self.mod = own("mod", [128, NM, GB])
                self.pen = own("pen", [128, GB // 2, S])
                self.xn = own("xn", [128, T])
                self.qT, self.kT, self.km = own("qT", [128, T]), own("kT", [128, T]), own("km", [128, JH, T])
                self.rot, self.oT = own("rot", [128, T]), own("oT", [128, T])
                self.vb = own("vb", [128, 2, GB // 2, HP // 2, 3 * PV])
                self.small = own("small", [128, 6, TT * 4])
                self.mx = own("mx", [128, 3, RG, 2 * JH])
                self.rec = own("rec", [128, T])
                self.wide = own("wide", [128, 16, T])
                halves = self.wide[:].rearrange("p c t -> p (c t)").rearrange("p (a n) -> p a n", a=2)
                self.ss = halves[:, 0, :].rearrange("q (r n) -> q r n", r=RG)
                self.pT = halves[:, 1, :].rearrange("k (p h q) -> k p h q", p=2, q=128)
                self.hid = self.wide[:, 0:6, :]
                self.v0 = self.wide[0:S, 6:8, :].rearrange("k c t -> k (c t)")
                self.tmp = self.wide[:, 8:12, :]
                self.sq, self.rstd = self.wide[:, 12, :], self.wide[:, 13, :]
                self.prob = self.km[:, 0:NE, :]
                self.lg = self.wide[0:4, 14, :]
                self.cn = self.rot

        visits = [Group(n) for n in range(GI)]
        groups = visits[0:NS]
        G0, G1 = groups[0:2]
        spare = G1.wide[:].rearrange("p c t -> p (c t)").rearrange("p (c n) -> p c n", n=D)
        for i, w in enumerate((w1, w2, w3)):
            w["mod"] = spare[:, 6 * i:6 * i + 6, :]

        ident = konst[:, K_ID:K_ID + 128]
        center = konst[:, K_CEN:K_CEN + 128]
        average = konst[:, K_AVG:K_AVG + 128]

        def col(name, i=0):
            a, _ = COLS[name]
            return cols[:, a + i:a + i + 1]

        def per_seq(G, i):
            return G.mod[:, i, :].unsqueeze(2).broadcast_to((128, GB, S))

        def seqs(ap):
            return ap.rearrange("p (b s) -> p b s", b=GB)

        pe_done, act_done = sem("pe_steps_done"), sem("act_steps_done")
        dve_done = sem("dve_steps_done")
        stored = [sem(f"group_stored_{n}") for n in range(NS)]
        rows_loaded = [sem(f"next_rows_loaded_{n}") for n in range(NS)]
        sems = {"pe": pe_done, "act": act_done, "dve": dve_done}
        loaded = sem("weights_loaded")
        first_in = sem("first_group_loaded")
        nums = [s.num for s in (*sems.values(), *stored, *rows_loaded)]
        assert sorted(nums) == list(range(min(nums), max(nums) + 1))
        counters = range(min(nums), max(nums) + 1)

        x_rows = io["x"].rearrange("b s d -> (b s) d")
        c_rows = io["ctx_1024"].rearrange("b s d -> (b s) d")
        out_rows = io["out"].rearrange("b s d -> (b s) d")

        def load_group(eng, G, first_row, signal):
            for n, rows in enumerate((x_rows, c_rows)):
                eng.dma_start(G.rows[:, n], rows[bass.ds(first_row, T), :].rearrange("(t p) d -> p t d", p=128)).then_inc(signal, 16)

        def vector_in(name):
            a, n = COLS[name]
            v = io[name]
            if len(v.shape) == 2:
                v = v.rearrange("e r -> (e r)")
            return cols[:, a:a + n], v.rearrange("(n p) -> p n", p=128)

        def chunks_in(t, name, rows=1):
            v = io[name]
            dst = t[:, :, :] if len(t.shape) == 3 else t[:, :]
            if rows > 1:
                return dst, v.rearrange("(c p) n -> p c n", p=128)
            return dst, v.rearrange("p (c n) -> p c n", n=128) if len(t.shape) == 3 else v

        straight = [
            (konst[:], io["consts"]),
            (G0.x[:, 0:D], io["cond_1024"]),
            chunks_in(w0q, "L0_xcond_Wq"), chunks_in(w0k, "L0_xcond_Wk"), chunks_in(w0v, "L0_xcond_Wv"),
            (w0e1[:, 0], io["L0_xcond_e_w1"][0].rearrange("(c p) r -> p c r", p=128)),
            (w0e1[:, 1], io["L0_xcond_e_w1"][1].rearrange("(c p) r -> p c r", p=128)),
            (w0e1[:, 2], io["L0_xcond_e_w1"][2].rearrange("(c p) r -> p c r", p=128)),
            (w0e2[:].rearrange("p e c n -> p (e c) n"), io["L0_xcond_e_w2"].rearrange("e (c p) h -> p (e c) h", p=128)),
            (w0g1[:], io["L0_xcond_gate_w1"].rearrange("(c p) h -> p c h", p=128)),
            chunks_in(w0g2, "L0_xcond_gate_w2"), chunks_in(w0o, "L0_xcond_out_w"),
            (w0r[:, :, 0:3], io["L0_xcond_router_W"].rearrange("(c p) e -> p c e", p=128)),
            (rbias3[:], io["L0_xcond_router_b"].rearrange("(e o) -> e o", o=1)),
            chunks_in(w1["mod"], "L1_xcond_ada_w"), chunks_in(w1["qkv"], "L1_xcond_qkv_w"),
            chunks_in(w1["proj"], "L1_xcond_sa_proj_w"), chunks_in(w1["q"], "L1_xcond_q_w"),
            chunks_in(w1["kv"], "L1_xcond_kv_w"), chunks_in(w1["cproj"], "L1_xcond_ca_proj_w"),
            chunks_in(w1["fc1"], "L1_xcond_fc1_w"), chunks_in(w1["fc2"], "L1_xcond_fc2_w", 4),
            chunks_in(w2["mod"], "L2_xcond_W_mod"), chunks_in(w2["qkv"], "L2_xcond_W_qkv"),
            chunks_in(w2["proj"], "L2_xcond_W_proj"), chunks_in(w2["q"], "L2_xcond_W_qc"),
            chunks_in(w2["kv"], "L2_xcond_W_kvc"), chunks_in(w2["cproj"], "L2_xcond_W_cproj"),
            chunks_in(w2["fc1"], "L2_xcond_W_mlp1"), chunks_in(w2["fc2"], "L2_xcond_W_mlp2", 4),
        ]
        turned = [("L3_xcond_ln1_w", "mod", 0, 2), ("L3_xcond_ln2_w", "mod", 2, 2), ("L3_xcond_ln3_w", "mod", 4, 2),
                  ("L3_xcond_qkv_w", "qkv", 0, 3), ("L3_xcond_sa_out_w", "proj", 0, 1), ("L3_xcond_q_w", "q", 0, 1),
                  ("L3_xcond_k_w", "kv", 0, 1), ("L3_xcond_v_w", "kv", 1, 1), ("L3_xcond_ca_out_w", "cproj", 0, 1),
                  ("L3_xcond_ffn_w1", "fc1", 0, 4), ("L3_xcond_ffn_w2", "fc2", 0, 4)]
        blocks = [(w, i) for _, w, a, n in turned for i in range(a, a + n)]
        stage = G0.wide[:].rearrange("p c t -> p (c t)")[:, 0:len(blocks) * D].rearrange("p (c n) -> p c n", n=D)
        at = 0
        for name, w, a, n in turned:
            v = io[name]
            src = v.rearrange("p (c n) -> p c n", n=D) if w == "fc2" else v.rearrange("(c p) n -> p c n", p=128)
            straight.append((stage[:, at:at + n, :], src))
            at += n
        seq_mask = io["mask_BxS2_bf0"].rearrange("(p b) k -> b p k", b=2)
        for b2 in range(2):
            straight.append((mask8[64 * b2:64 * b2 + 64], seq_mask[b2:b2 + 1].broadcast_to((64, B // 2, S))))
        vectors = [vector_in(n) for n in COLS]
        n_sp, n_act = len(straight), len(vectors)

        rot_of = [("qkv", 0), ("qkv", 1), ("q", 0), ("kv", 0)]
        condT, silT = G0.qT[:, 0:B], G0.kT[:, 0:B]
        tables = ([(M1 + i, w1["mod"][:, i, :], silT, col("L1_xcond_ada_b", i), i in (1, 4)) for i in range(6)]
                  + [(M2 + i, w2["mod"][:, i, :], silT, col("L2_xcond_b_mod", i), i in (1, 4)) for i in range(6)]
                  + [(M3 + i, w3["mod"][:, i, :], condT, col(f"L3_xcond_ln{i // 2 + 1}_b", i % 2), i % 2 == 0) for i in range(6)]
                  + [(MA + 2 * e + h, w0e1[:, e, 2, h * D:(h + 1) * D], condT, col("L0_xcond_e_b1", 2 * e + h), False)
                     for e in range(NE) for h in range(2)]
                  + [(MGATE, w0g1[:, 2, :], condT, col("L0_xcond_gate_b1"), False), (MROUTE, w0r[:, 2, :], condT, rbias[:], False)])

        passed = [(w["proj"], col(p + qkv, 2), col(p + b)) for w, p, qkv, b in (
            (w1, "L1_xcond_", "qkv_b", "sa_proj_b"), (w2, "L2_xcond_", "b_qkv", "b_proj"))]
        passed += [(w["cproj"], col(p + kv, 1), col(p + b)) for w, p, kv, b in (
            (w1, "L1_xcond_", "kv_b", "ca_proj_b"), (w2, "L2_xcond_", "b_kvc", "b_cproj"))]

        st.start(sems)
        with nc.Block() as block:
            @block.sync
            def _(sp):
                with nc.allow_non_contiguous_dma("weights in their layouts"):
                    for dst, src in straight:
                        sp.dma_start(dst, src).then_inc(loaded, 16)
                    for G in groups:
                        load_group(sp, G, G.n * T, first_in)
                sp.wait_ge(loaded, 16 * (n_sp + n_act))
                sp.wait_ge(first_in, 32 * NS)

            @block.tensor
            def _(pe):
                pe.wait_ge(loaded, 16 * (n_sp + n_act))
                pe.transpose(bank[7][:, 0:B], G0.x[:, 0:D], ident).then_inc(*tick("pe", ("cond",)))
                for n, (w, i) in enumerate(blocks):
                    if n >= 7:
                        pe.wait_ge(*done("turned", n - 7))
                    pe.transpose(bank[n % 7][:, 0:D], stage[:, n, :], ident).then_inc(*tick("pe", ("turn", n)))
                pe.wait_ge(*done("silu cond"))
                for n, (w, v, _) in enumerate(passed):
                    ins = pe.matmul(bank[7][:, 2 * n:2 * n + 1], w[:, 0, :], v, start=True, stop=True)
                ins.then_inc(*tick("pe", ("passed",)))
                pe.wait_ge(*done("turned", len(blocks) - 1))
                for n, (m, w, rhs, _, _) in enumerate(tables):
                    if n >= 7:
                        pe.wait_ge(*done("table", n - 7))
                    pe.matmul(bank[n % 7][0:w.shape[-1], 0:B], w, rhs, start=True, stop=True).then_inc(*tick("pe", ("table product", n)))

            @block.scalar
            def _(act):
                with nc.allow_non_contiguous_dma("per-feature vectors"):
                    for dst, src in vectors:
                        act.dma_start(dst, src).then_inc(loaded, 16)
                act.wait_ge(*done("condT"))
                act.activation(silT, condT, ACT.Silu).then_inc(*tick("act", ("silu cond",)))
                act.wait_ge(*done("silu cond"))

            @block.vector
            def _(dve):
                for G in groups:
                    dve.memset(G.vb[:], 0.0)
                dve.memset(w0r[:, :, 3:4], 0.0)
                dve.memset(rbias[:], 0.0).then_inc(*tick("dve", ("rbias zero",)))
                dve.wait_ge(loaded, 16 * (n_sp + n_act))
                dve.wait_ge(*done("cond"))
                dve.tensor_copy(condT, bank[7][:, 0:B]).then_inc(*tick("dve", ("condT",)))
                dve.wait_ge(*done("condT"))
                dve.memset(table[:, MROUTE, :], 0.0).then_inc(*tick("dve", ("route zero",)))
                dve.wait_ge(*done("route zero"))
                dve.wait_ge(*done("rbias zero"))
                dve.tensor_copy(rbias[0:NE, :], rbias3[:])
                dve.tensor_scalar(col("L0_xcond_gate_b2"), col("L0_xcond_gate_b2"), 0.5, None, ALU.mult)
                for n, (w, i) in enumerate(blocks):
                    dve.wait_ge(*done("turn", n))
                    dve.tensor_copy(w3[w][:, i, :], bank[n % 7][:, 0:D]).then_inc(*tick("dve", ("turned", n)))
                dve.wait_ge(*done("turned", len(blocks) - 1))
                half = HD // 2
                for n, (w, i) in enumerate(rot_of):
                    src = w3[w][:, i, :].rearrange("p (h t d) -> p h t d", h=NH, t=2)
                    dst = w3["rot"][:, n, :].rearrange("p (h t d) -> p h t d", h=NH, t=2)
                    dve.tensor_scalar(dst[:, :, 0, :], src[:, :, 1, :], -1.0, None, ALU.mult)
                    dve.tensor_copy(dst[:, :, 1, :], src[:, :, 0, :])
                dve.wait_ge(*done("passed"))
                for n, (_, _, b) in enumerate(passed):
                    dve.tensor_tensor(b, b, bank[7][:, 2 * n:2 * n + 1], ALU.add)
                for n, (m, w, rhs, b, one) in enumerate(tables):
                    dve.wait_ge(*done("table product", n))
                    rows = slice(0, w.shape[-1])
                    dve.tensor_scalar(table[rows, m, :], bank[n % 7][rows, 0:B], b, 1.0 if one else 0.0, ALU.add, ALU.add)\
                        .then_inc(*tick("dve", ("table", n)))

        nc.all_engine_barrier(sems_to_clear=counters)

        st.start(sems)

        class Ring:

            def __init__(self):
                self.last, self.turn, self.held = {}, 0, {}

            def claim(self, pe, name, hold=None):
                while self.turn in self.held.values():
                    self.turn = (self.turn + 1) % BANKS
                where = self.turn
                self.turn = (self.turn + 1) % BANKS
                if hold:
                    self.held[hold] = where
                if where in self.last:
                    pe.wait_ge(*done("free", self.last[where]))
                self.last[where] = name
                st.tiles[name] = where
                return bank[where]

            def let_go(self, hold):
                del self.held[hold]

        def tile(name):
            return bank[st.banks.get(name, 0)]

        ring = Ring()

        def pe_turn_in(pe, G):
            if G.n >= NS:
                pe.wait_ge(rows_loaded[G.stream], 32 * (G.n // NS))
            for n, nm in enumerate(("x", "c")):
                b = ring.claim(pe, (G.n, "in", nm))
                for t in range(TT):
                    ins = pe.transpose(b[:, t * 128:(t + 1) * 128], G.rows[:, n, t, :], ident)
                ins.then_inc(*tick("pe", ("mm", (G.n, "in", nm))))

        def pe_product(pe, name, pairs, hold=None):
            b = ring.claim(pe, name, hold)
            for i, (w, m) in enumerate(pairs):
                ins = pe.matmul(b[0:w.shape[-1], 0:T], w, m, start=(i == 0), stop=(i == len(pairs) - 1))
            ins.then_inc(*tick("pe", ("mm", name)))

        def pe_values(pe, G, tag, src, w):
            b = ring.claim(pe, (G.n, tag, "v"))
            for p in range(TT):
                ins = pe.matmul(b[:, p * D:(p + 1) * D], src[:, p * 128:(p + 1) * 128], w, start=True, stop=True)
            ins.then_inc(*tick("pe", ("mm", (G.n, tag, "v"))))

        def pe_scores(pe, G, tag, c):
            if c == 0:
                pe.wait_ge(*done("qT", G.n, tag))
                pe.wait_ge(*done("km", G.n, tag))
            rows2 = (2 * c, 2 * c + 1)
            b2s = [ring.claim(pe, (G.n, tag, "s", r)) for r in rows2]
            for p in range(2):
                for b2 in range(2):
                    tok = (2 * p + b2) * S
                    for r, b in zip(rows2, b2s):
                        rows = slice(32 * r, 32 * r + 32)
                        ins = pe.matmul(b[64 * b2:64 * b2 + 64, p * 256:(p + 1) * 256].rearrange("q (j k) -> q j k", j=JH),
                                        G.qT[rows, tok:tok + S], G.km[rows, :, tok:tok + S], start=True, stop=True)
                        if p == 1 and b2 == 1:
                            ins.then_inc(*tick("pe", ("mm", (G.n, tag, "s", r))))

        def pe_turn_probs(pe, G, tag, c):
            for p in range(2):
                b = ring.claim(pe, (G.n, tag, "pT", p, c))
                for rr in range(2):
                    r = 2 * c + rr
                    pe.wait_ge(*done("exp", G.n, tag, r))
                    for jj in range(2):
                        a = p * 256 + jj * 128
                        ins = pe.transpose(b[:, (2 * rr + jj) * 128:(2 * rr + jj + 1) * 128], G.ss[:, r, a:a + 128], ident)
                ins.then_inc(*tick("pe", ("mm", (G.n, tag, "pT", p, c))))

        def pe_mix(pe, G, tag):
            b = ring.claim(pe, (G.n, tag, "o"))
            pe.wait_ge(*done("vb", G.n, tag))
            for c in range(2):
                for p in range(2):
                    pe.wait_ge(*done("pT", G.n, tag, p, c))
            for p in range(2):
                for b2 in range(2):
                    for odd in range(2):
                        for m in range(HP // 2):
                            a = (2 * p + b2) * S
                            pe.matmul(b[32 * m:32 * m + 32, a:a + S], G.vb[:, b2, p, m, odd * PV:odd * PV + 2 * PV],
                                      G.pT[:, p, 2 * m + odd, 64 * b2:64 * b2 + 64], start=not odd, stop=bool(odd))
            for odd in range(2):
                one = konst[:, K_ONE + odd * PV:K_ONE + odd * PV + 2 * PV]
                for m in range(HP // 2):
                    ins = pe.matmul(b[32 * m:32 * m + 32, T:2 * T].rearrange("f (p q) -> f p q", p=2), one,
                                    G.pT[:, :, 2 * m + odd, :], start=not odd, stop=bool(odd))
            ins.then_inc(*tick("pe", ("mm", (G.n, tag, "o"))))

        def pe_mlp_out(pe, G, tag, w):
            b = ring.claim(pe, (G.n, tag, "y"))
            for c in range(FC):
                pe.wait_ge(*done("h", G.n, tag, c))
                ins = pe.matmul(b[:, 0:T], w[:, c, :], G.hid[:, c, :], start=(c == 0), stop=(c == FC - 1))
            ins.then_inc(*tick("pe", ("mm", (G.n, tag, "y"))))

        def act_tables(act, number):
            act.add_instruction(mybir.InstLoadActFuncSet(name=nc.get_next_instruction_name(), act_func_set_id=number, ins=[], outs=[]))

        def act_out(act, G, name, dst, bias, *names, func=ACT.Identity):
            act.wait_ge(*done("mm", (G.n, *name)))
            act.activation(dst, tile((G.n, *name))[0:dst.shape[0], 0:T], func, bias=bias)\
                .then_inc(*tick("act", ("free", (G.n, *name)), *names))

        def act_square(act, G, tag):
            act.wait_ge(*done("mm", (G.n, tag, "cen")))
            act.activation(G.sq[:], tile((G.n, tag, "cen"))[:, 0:T], ACT.Square).then_inc(*tick("act", ("sq", G.n, tag)))

        def act_rstd(act, G, tag, eps):
            act.wait_ge(*done("mm", (G.n, tag, "var")))
            act.activation(G.rstd[:], tile((G.n, tag, "var"))[:, 0:T], ACT.Ln, bias=konst[:, K_EPS + eps:K_EPS + eps + 1])\
                .then_inc(*tick("act", ("free", (G.n, tag, "var")), ("ln", G.n, tag)))
            act.wait_ge(*done("ln", G.n, tag))
            act.activation(G.rstd[:], G.rstd[:], ACT.Exp, scale=-0.5).then_inc(*tick("act", ("rstd", G.n, tag)))

        def act_values(act, G, tag):
            name = (G.n, tag, "v")
            act.wait_ge(*done("mm", name))
            src = tile(name)[:, 0:T].rearrange("k (h o e d) -> k h o e d", h=TT * HP // 2, o=2, e=2)
            for b2 in range(2):
                dst = G.vb[:, b2].rearrange("k p m (t w) -> k (p m) t w", t=3)
                for e in range(2):
                    end = [("free", name), ("vb", G.n, tag)] if (b2, e) == (1, 1) else []
                    act.activation(dst[64 * e:64 * e + 64, :, 0:3:2, HD * e:HD * e + HD], src[64 * b2:64 * b2 + 64, :, :, e, :],
                                   ACT.Copy).then_inc(*tick("act", *end))

        def act_exp(act, G, tag, c):
            for r in (2 * c, 2 * c + 1):
                act.wait_ge(*done("sub", G.n, tag, r))
                act.activation(G.ss[:, r, :], G.ss[:, r, :], ACT.Exp, scale=SCALE).then_inc(*tick("act", ("exp", G.n, tag, r)))

        def act_turn_probs(act, G, tag, c):
            for p in range(2):
                name = (G.n, tag, "pT", p, c)
                act.wait_ge(*done("mm", name))
                act.activation(G.pT[:, p, 4 * c:4 * c + 4, :].rearrange("k h q -> k (h q)"), tile(name)[:], ACT.Copy)\
                    .then_inc(*tick("act", ("free", name), ("pT", G.n, tag, p, c)))

        def act_mix(act, G, tag):
            name, rec = (G.n, tag, "o"), G.rec[:]
            act.wait_ge(*done("mm", name))
            act.activation(rec, tile(name)[:, T:2 * T], ACT.Ln).then_inc(*tick("act", ("ln sum", G.n, tag)))
            act.wait_ge(*done("ln sum", G.n, tag))
            act.activation(rec, rec, ACT.Exp, scale=-1.0).then_inc(*tick("act", ("rec", G.n, tag)))

        def dve_scale(dve, G, tag, scale, dst):
            cen = (G.n, tag, "cen")
            dve.wait_ge(*done("sq", G.n, tag))
            dve.tensor_tensor(seqs(dst[:]), seqs(tile(cen)[:, 0:T]), per_seq(G, scale), ALU.mult)\
                .then_inc(*tick("dve", ("free", cen), ("scaled", G.n, tag)))

        def dve_norm(dve, G, tag, shift, dst):
            cen = (G.n, tag, "cen")
            dve.wait_ge(*done("rstd", G.n, tag))
            if shift is None:
                dve.tensor_tensor(dst[:], tile(cen)[:, 0:T], G.rstd[:], ALU.mult).then_inc(*tick("dve", ("free", cen), ("xn", G.n, tag)))
                return
            dve.wait_ge(*done("scaled", G.n, tag))
            dve.tensor_tensor(dst[:], dst[:], G.rstd[:], ALU.mult).then_inc(*tick("dve", ("xn 1", G.n, tag)))
            dve.wait_ge(*done("xn 1", G.n, tag))
            dve.tensor_tensor(seqs(dst[:]), seqs(dst[:]), per_seq(G, shift), ALU.add).then_inc(*tick("dve", ("xn", G.n, tag)))

        def dve_rotary(dve, G, tag, n, dst, name):
            wide = lambda a: konst[:, a:a + S].unsqueeze(1).broadcast_to((128, GB, S))
            straight, turned = (G.n, tag, n), (G.n, tag, n + " rot")
            dve.wait_ge(*done("mm", straight))
            dve.tensor_tensor(seqs(dst[:]), seqs(tile(straight)[:, 0:T]), wide(K_COS), ALU.mult)\
                .then_inc(*tick("dve", ("free", straight), ("cos", G.n, tag, n)))
            dve.wait_ge(*done("mm", turned))
            dve.tensor_tensor(seqs(G.rot[:]), seqs(tile(turned)[:, 0:T]), wide(K_SIN), ALU.mult)\
                .then_inc(*tick("dve", ("free", turned), ("sin", G.n, tag, n)))
            dve.wait_ge(*done("sin", G.n, tag, n))
            dve.tensor_tensor(dst[:], dst[:], G.rot[:], ALU.add).then_inc(*tick("dve", (name, G.n, tag)))
            dve.wait_ge(*done(name, G.n, tag))

        def dve_keys(dve, G, tag, bias):
            mask = konst[:, K_MASK:K_MASK + JH].unsqueeze(2).broadcast_to((128, JH, T))
            wide = lambda ap: ap.unsqueeze(1).broadcast_to((128, JH, T))
            if bias is None:
                dve.tensor_tensor(G.km[:], wide(G.kT[:]), mask, ALU.mult).then_inc(*tick("dve", ("km", G.n, tag)))
            else:
                name = (G.n, tag, "k")
                dve.wait_ge(*done("mm", name))
                dve.scalar_tensor_tensor(G.km[:], wide(tile(name)[:, 0:T]), bias, mask, ALU.add, ALU.mult)\
                    .then_inc(*tick("dve", ("free", name), ("km", G.n, tag)))

        def dve_scores(dve, G, tag, c, masked):
            heads = lambda ap: ap.rearrange("q (g k) -> q g k", k=S)
            quads = lambda ap: ap.rearrange("q (p j k) -> q p j k", p=2, j=JH)
            both = (2 * c, 2 * c + 1)
            src = {r: tile((G.n, tag, "s", r))[:] for r in both}
            for r in both:
                name = (G.n, tag, "s", r)
                dve.wait_ge(*done("mm", name))
                if masked:
                    dve.tensor_tensor(quads(G.ss[:, r, :]), quads(src[r]), G.pen[:].unsqueeze(2).broadcast_to((128, 2, JH, S)), ALU.add)\
                        .then_inc(*tick("dve", ("masked", G.n, tag, r), ("free", name)))
                    src[r] = G.ss[:, r, :]
            for r in both:
                if masked:
                    dve.wait_ge(*done("masked", G.n, tag, r))
                dve.tensor_reduce(G.mx[:, 0, r, :], heads(src[r]), AX_X, ALU.max).then_inc(*tick("dve", ("max", G.n, tag, r)))
            for r in both:
                dve.wait_ge(*done("max", G.n, tag, r))
                dve.tensor_tensor(heads(G.ss[:, r, :]), heads(src[r]), G.mx[:, 0, r, :].unsqueeze(2).broadcast_to((128, 2 * JH, S)),
                                  ALU.subtract)\
                    .then_inc(*tick("dve", ("sub", G.n, tag, r), *([] if masked else [("free", (G.n, tag, "s", r))])))

        def dve_mix(dve, G, tag):
            name = (G.n, tag, "o")
            dve.wait_ge(*done("rec", G.n, tag))
            dve.tensor_tensor(G.oT[:], tile(name)[:, 0:T], G.rec[:], ALU.mult)\
                .then_inc(*tick("dve", ("free", name), ("oT", G.n, tag)))

        def dve_residual(dve, G, name, bias, gate, end):
            name, x = (G.n, *name), G.x
            dve.wait_ge(*done("mm", name))
            if gate is None and bias is None:
                dve.tensor_tensor(x[:], tile(name)[:, 0:T], x[:], ALU.add).then_inc(*tick("dve", ("free", name), ("x", G.n, end)))
            elif gate is None:
                dve.scalar_tensor_tensor(x[:], tile(name)[:, 0:T], bias, x[:], ALU.add, ALU.add)\
                    .then_inc(*tick("dve", ("free", name), ("x", G.n, end)))
            else:
                dve.scalar_tensor_tensor(seqs(G.tmp[:, 3, :]), seqs(tile(name)[:, 0:T]), bias, gate, ALU.add, ALU.mult)\
                    .then_inc(*tick("dve", ("free", name), ("gated", G.n, end)))
                dve.wait_ge(*done("gated", G.n, end))
                dve.tensor_tensor(x[:], x[:], G.tmp[:, 3, :], ALU.add).then_inc(*tick("dve", ("x", G.n, end)))

        def pe_keys0(pe, G):
            pe.wait_ge(*done("c", G.n))
            pe_product(pe, (G.n, "0", "k"), [(w0k[:], G.cT[:])])
            for v in range(GB // 4):
                b = ring.claim(pe, (G.n, "0", "v", v))
                for i in range(4):
                    s = (4 * v + i) * S
                    ins = pe.matmul(b[0:S, i * D:(i + 1) * D], G.cT[:, s:s + S], w0v[:], start=True, stop=True)
                ins.then_inc(*tick("pe", ("mm", (G.n, "0", "v", v))))

        def act_keys0(act, G):
            act_out(act, G, ("0", "k"), G.kT[:], 0.0, ("kT", G.n, "0"))
            name = (G.n, "0", "v", 0)
            act.wait_ge(*done("mm", name))
            act.activation(G.v0, tile(name)[0:S, :], ACT.Copy).then_inc(*tick("act", ("free", name), ("v", G.n, 0)))

        def dve_norm0(dve, G):
            cen = (G.n, "0", "cen")
            dve.wait_ge(*done("rstd", G.n, "0"))
            dve.scalar_tensor_tensor(G.xn[:], tile(cen)[:, 0:T], col("L0_xcond_ln_gamma"), G.rstd[:], ALU.mult, ALU.mult)\
                .then_inc(*tick("dve", ("free", cen), ("xn 1", G.n, "0")))
            dve.wait_ge(*done("xn 1", G.n, "0"))
            dve.tensor_scalar(G.xn[:], G.xn[:], col("L0_xcond_ln_beta"), None, ALU.add).then_inc(*tick("dve", ("xn", G.n, "0")))

        def pe_scores0(pe, G):
            pe.wait_ge(*done("qT", G.n, "0"))
            pe.wait_ge(*done("kT", G.n, "0"))
            b = ring.claim(pe, (G.n, "0", "s"))
            for q in range(GB):
                ins = pe.matmul(b[64 * (q % 2):64 * (q % 2) + 64, (q // 2) * S:(q // 2 + 1) * S],
                                G.qT[:, q * S:(q + 1) * S], G.kT[:, q * S:(q + 1) * S], start=True, stop=True)
            ins.then_inc(*tick("pe", ("mm", (G.n, "0", "s"))))

        def dve_scores0(dve, G):
            pairs = lambda ap: ap.rearrange("q (p k) -> q p k", k=S)
            wide = lambda ap: ap.unsqueeze(2).broadcast_to((128, GB // 2, S))
            name = (G.n, "0", "s")
            s, p0 = tile(name)[:, 0:GB // 2 * S], G.ss[:, 0, 0:GB // 2 * S]
            top, total, rec = (G.mx[:, 0, r, 0:GB // 2] for r in range(3))
            dve.wait_ge(*done("mm", name))
            dve.tensor_reduce(top, pairs(s), AX_X, ALU.max).then_inc(*tick("dve", ("max", G.n, "0")))
            dve.wait_ge(*done("max", G.n, "0"))
            dve.tensor_tensor(pairs(p0), pairs(s), wide(top), ALU.subtract).then_inc(*tick("dve", ("sub", G.n, "0"), ("free", name)))
            dve.wait_ge(*done("exp", G.n, "0"))
            dve.tensor_reduce(total, pairs(p0), AX_X, ALU.add).then_inc(*tick("dve", ("sum", G.n, "0")))
            dve.wait_ge(*done("sum", G.n, "0"))
            dve.reciprocal(rec, total).then_inc(*tick("dve", ("rec", G.n, "0")))
            dve.wait_ge(*done("rec", G.n, "0"))
            dve.tensor_tensor(pairs(p0), pairs(p0), wide(rec), ALU.mult).then_inc(*tick("dve", ("p", G.n, "0")))

        def act_scores0(act, G):
            act.wait_ge(*done("sub", G.n, "0"))
            act.activation(G.ss[:, 0, 0:GB // 2 * S], G.ss[:, 0, 0:GB // 2 * S], ACT.Exp, scale=SCALE0).then_inc(*tick("act", ("exp", G.n, "0")))

        def pe_turn_probs0(pe, G):
            pe.wait_ge(*done("p", G.n, "0"))
            b = ring.claim(pe, (G.n, "0", "pT"))
            for p in range(GB // 2):
                ins = pe.transpose(b[0:S, p * 128:(p + 1) * 128], G.ss[:, 0, p * S:(p + 1) * S], ident)
            ins.then_inc(*tick("pe", ("mm", (G.n, "0", "pT"))))

        def pe_evidence(pe, G):
            pe.wait_ge(*done("pT", G.n, "0"))
            pe.wait_ge(*done("v", G.n, 0))
            b = ring.claim(pe, (G.n, "0", "ev"))
            for q in range(GB):
                ins = pe.matmul(b[:, q * S:(q + 1) * S], G.v0[:, q * D:(q + 1) * D],
                                G.oT[0:S, q * S:(q + 1) * S], start=True, stop=True)
            ins.then_inc(*tick("pe", ("mm", (G.n, "0", "ev"))))

        def pe_route(pe, G):
            pe.wait_ge(*done("lg", G.n))
            b = ring.claim(pe, (G.n, "0", "lgT"))
            for t in range(TT):
                ins = pe.transpose(b[:, 4 * t:4 * t + 4], G.lg[:, t * 128:(t + 1) * 128], ident[0:4, 0:4])
            ins.then_inc(*tick("pe", ("mm", (G.n, "0", "lgT"))))

        def dve_route(dve, G):
            three = lambda ap: ap.rearrange("t (n e) -> t n e", e=4)[:, :, 0:NE]
            wide3 = lambda ap: ap.unsqueeze(2).broadcast_to((128, TT, NE))
            small, name = G.small, (G.n, "0", "lgT")
            top, total, rec = (small[:, 0, i * TT:(i + 1) * TT] for i in range(3))
            lgT = three(tile(name)[:, 0:4 * TT])
            dve.wait_ge(*done("mm", name))
            dve.tensor_reduce(top, lgT, AX_X, ALU.max).then_inc(*tick("dve", ("route max", G.n)))
            dve.wait_ge(*done("route max", G.n))
            dve.tensor_tensor(three(small[:, 1, :]), lgT, wide3(top), ALU.subtract).then_inc(*tick("dve", ("free", name), ("route sub", G.n)))
            dve.wait_ge(*done("route exp", G.n))
            dve.tensor_reduce(total, three(small[:, 2, :]), AX_X, ALU.add).then_inc(*tick("dve", ("route sum", G.n)))
            dve.wait_ge(*done("route sum", G.n))
            dve.reciprocal(rec, total).then_inc(*tick("dve", ("route rec", G.n)))
            dve.wait_ge(*done("route rec", G.n))
            dve.tensor_tensor(three(small[:, 5, :]), three(small[:, 2, :]), wide3(rec), ALU.mult).then_inc(*tick("dve", ("route", G.n)))

        def act_route(act, G):
            three = lambda ap: ap.rearrange("t (n e) -> t n e", e=4)[:, :, 0:NE]
            act.wait_ge(*done("route sub", G.n))
            act.activation(three(G.small[:, 2, :]), three(G.small[:, 1, :]), ACT.Exp).then_inc(*tick("act", ("route exp", G.n)))

        hidden_order = (2 * NE, *range(2 * NE))

        def pe_experts_in(pe, G):
            for n in hidden_order:
                e, a = n // 2, n % 2 * D
                w = w0e1[:, e, :, a:a + D] if n < 2 * NE else w0g1[:]
                pe_product(pe, (G.n, "0", "h", n), [(w[:, 0, :], G.xn[:]), (w[:, 1, :], G.rot[:])])
            pe.wait_ge(*done("h", G.n, "0", 2 * NE))
            pe_product(pe, (G.n, "0", "g2"), [(w0g2[:], G.qT[:])])

        def dve_experts_in(dve, G):
            if G.n >= NS:
                dve.wait_ge(stored[G.stream], 16 * (G.n // NS))
            for k, n in enumerate(hidden_order):
                name = (G.n, "0", "h", n)
                dve.wait_ge(*done("mm", name))
                if k >= 3:
                    dve.wait_ge(*done("h", G.n, "0", hidden_order[k - 3]))
                dve.tensor_tensor(seqs(G.tmp[:, k % 3, :]), seqs(tile(name)[:, 0:T]), per_seq(G, MA + n), ALU.add)\
                    .then_inc(*tick("dve", ("free", name), ("h pre", G.n, n)))
            dve.wait_ge(*done("tanh", G.n))
            dve.tensor_scalar(G.sq[:], G.sq[:], 0.5, 0.5, ALU.mult, ALU.add).then_inc(*tick("dve", ("gate", G.n)))

        def act_experts_in(act, G):
            for k, n in enumerate(hidden_order):
                act.wait_ge(*done("h pre", G.n, n))
                dst = G.hid[:, n, :] if n < 2 * NE else G.qT[:]
                act.activation(dst, G.tmp[:, k % 3, :], ACT.Silu).then_inc(*tick("act", ("h", G.n, "0", n)))
            name = (G.n, "0", "g2")
            act.wait_ge(*done("mm", name))
            act.activation(G.sq[:], tile(name)[:, 0:T], ACT.Tanh, bias=col("L0_xcond_gate_b2"), scale=0.5)\
                .then_inc(*tick("act", ("free", name), ("tanh", G.n)))

        def pe_experts_out(pe, G):
            pe.wait_ge(*done("route", G.n))
            for e in range(NE):
                b = ring.claim(pe, (G.n, "0", "pb", e))
                for t in range(TT):
                    ins = pe.matmul(b[:, t * 128:(t + 1) * 128], G.small[:, 5, 4 * t + e:4 * t + e + 1].broadcast_to((128, 128)),
                                    ident, start=True, stop=True)
                ins.then_inc(*tick("pe", ("mm", (G.n, "0", "pb", e))))
            for e in range(NE):
                pe.wait_ge(*done("h", G.n, "0", 2 * e + 1))
                pe_product(pe, (G.n, "0", "e", e), [(w0e2[:, e, h, :], G.hid[:, 2 * e + h, :]) for h in range(2)])

        def act_experts_out(act, G):
            for e in range(NE):
                act_out(act, G, ("0", "pb", e), G.prob[:, e, :], 0.0, ("pb", G.n, e))

        def dve_experts_out(dve, G):
            for e in range(NE):
                name = (G.n, "0", "e", e)
                dve.wait_ge(*done("mm", name))
                dve.wait_ge(*done("pb", G.n, e))
                dst = G.kT[:] if e == 0 else G.tmp[:, 3, :]
                dve.scalar_tensor_tensor(dst, tile(name)[:, 0:T], col("L0_xcond_e_b2", e), G.prob[:, e, :], ALU.add, ALU.mult)\
                    .then_inc(*tick("dve", ("free", name), ("routed", G.n, 0) if e == 0 else ("expert", G.n, e)))
                if e:
                    dve.wait_ge(*done("expert", G.n, e))
                    dve.tensor_tensor(G.kT[:], G.kT[:], G.tmp[:, 3, :], ALU.add).then_inc(*tick("dve", ("routed", G.n, e)))
                    dve.wait_ge(*done("routed", G.n, e))

        def norm_stages(G, tag, before, scale, shift, dst, eps, src, more=(None, None)):
            nothing = (None, None, None)
            one, two = (m or nothing for m in more)

            def pe_a(pe):
                pe.wait_ge(*done(*before))
                pe_product(pe, (G.n, tag, "cen"), [(center, src[:])], hold=(G.n, tag))
                if one[0]:
                    one[0](pe)

            def act_a(act):
                act_square(act, G, tag)
                if one[1]:
                    one[1](act)

            def pe_b(pe):
                pe.wait_ge(*done("sq", G.n, tag))
                pe_product(pe, (G.n, tag, "var"), [(average, G.sq[:])])
                ring.let_go((G.n, tag))
                if two[0]:
                    two[0](pe)

            def act_b(act):
                act_rstd(act, G, tag, eps)
                if two[1]:
                    two[1](act)

            def dve_b(dve):
                if tag == "0":
                    dve_norm0(dve, G)
                else:
                    dve_norm(dve, G, tag, shift, dst)
                if two[2]:
                    two[2](dve)

            def dve_a(dve):
                if scale is not None:
                    dve_scale(dve, G, tag, scale, dst)

            kind = tag[-1]
            return [(pe_a, act_a, dve_a, "center " + kind), (pe_b, act_b, dve_b, "norm " + kind)]

        weights = {1: w1, 2: w2, 3: w3}

        def queries(G, tag, L, cross, ready, bq):
            w = weights[L]

            def pe_q(pe):
                pe.wait_ge(*done(*ready))
                pe_product(pe, (G.n, tag, "q"), [(w["q"][:, 0, :] if cross else w["qkv"][:, 0, :], G.xn[:])])
                if L == 3:
                    pe_product(pe, (G.n, tag, "q rot"), [(w["rot"][:, 2 * cross, :], G.xn[:])])

            def act_q(act):
                if L < 3:
                    act_out(act, G, (tag, "q"), G.qT[:], bq, ("qT", G.n, tag))

            def dve_q(dve):
                if L == 3:
                    dve_rotary(dve, G, tag, "q", G.qT, "qT")
            return pe_q, act_q, dve_q, "queries"

        def keys(G, tag, L, cross, src, ready, bias):
            w = weights[L]

            def pe_k(pe):
                pe.wait_ge(*done(*ready))
                pe_product(pe, (G.n, tag, "k"), [(w["kv"][:, 0, :] if cross else w["qkv"][:, 1, :], src[:])])
                if L == 3:
                    pe_product(pe, (G.n, tag, "k rot"), [(w["rot"][:, 2 * cross + 1, :], src[:])])

            def dve_k(dve):
                if L == 3:
                    dve_rotary(dve, G, tag, "k", G.kT, "kT")
                dve_keys(dve, G, tag, bias)
            return pe_k, None, dve_k, "keys"

        def values(G, tag, L, cross, src):
            w = weights[L]
            return (lambda pe: pe_values(pe, G, tag, src, w["kv"][:, 1, :] if cross else w["qkv"][:, 2, :]),
                    lambda act: act_values(act, G, tag), None, "values")

        def attention_core(G, tag, masked, tail):
            def scores(c):
                return (lambda pe: pe_scores(pe, G, tag, c), None, lambda dve: dve_scores(dve, G, tag, c, masked),
                        "scores" if c else "first scores")

            def exps(c):
                return None, lambda act: act_exp(act, G, tag, c), None, "last exps" if c else "exps"

            def turn(c):
                return lambda pe: pe_turn_probs(pe, G, tag, c), lambda act: act_turn_probs(act, G, tag, c), None, "last turn" if c else "turn"

            mix = lambda pe: pe_mix(pe, G, tag), lambda act: act_mix(act, G, tag), lambda dve: dve_mix(dve, G, tag), "mix"
            return [scores(0), scores(1), exps(0), turn(0), exps(1), *tail, turn(1), mix]

        def projection(G, tag, w, bias, gate):
            def pe_p(pe):
                pe.wait_ge(*done("oT", G.n, tag))
                pe_product(pe, (G.n, tag, "proj"), [(w[:, 0, :], G.oT[:])])
            return pe_p, None, lambda dve: dve_residual(dve, G, (tag, "proj"), bias, gate, tag), "projection"

        def mlp_stages(G, tag, L, func, b1, b2, gate, end, between):
            w = weights[L]

            def pe_h(pe):
                pe.wait_ge(*done("xn", G.n, tag))
                for c in range(FC):
                    pe_product(pe, (G.n, tag, "h", c), [(w["fc1"][:, c, :], G.xn[:])])

            def act_h(act):
                for c in range(FC):
                    act_out(act, G, (tag, "h", c), G.hid[:, c, :], col(b1, c), ("h", G.n, tag, c), func=func)
            return [(pe_h, act_h, None, "mlp in"), *between,
                    (lambda pe: pe_mlp_out(pe, G, tag, w["fc2"]), None,
                     lambda dve: dve_residual(dve, G, (tag, "y"), col(b2), gate, end), "mlp out")]

        def stages_of(G, i):
            n = G.n

            def act_in(act):
                for nm, dst in (("x", G.x), ("c", G.cT)):
                    act_out(act, G, ("in", nm), dst[:], 0.0, ("x", n, "in") if nm == "x" else ("c", n))

            def dve_in(dve):
                g = i * GI + n
                if n >= NS:
                    dve.wait_ge(*done("x", n - NS, "3"))
                dve.tensor_copy(G.mod[:], table[:, :, bass.ds(g * GB, GB)]).then_inc(*tick("dve", ("mod", n)))
                dve.tensor_scalar(G.pen[:], mask8[:, bass.ds(g * (GB // 2), GB // 2), :], -3e38, 1e10, ALU.mult, ALU.mult)\
                    .then_inc(*tick("dve", ("pen", n)))
                dve.wait_ge(*done("pen", n))

            out = [(lambda pe: pe_turn_in(pe, G), act_in, dve_in, "turn in")]
            out += norm_stages(G, "0", ("x", n, "in"), None, None, G.xn, 0, G.x,
                               more=((lambda pe: pe_keys0(pe, G), lambda act: act_keys0(act, G), None), None))

            def pe_q0(pe):
                pe.wait_ge(*done("xn", n, "0"))
                pe_product(pe, (n, "0", "q"), [(w0q[:], G.xn[:])])

            out.append((pe_q0, lambda act: act_out(act, G, ("0", "q"), G.qT[:], 0.0, ("qT", n, "0")), None, "product"))
            out.append((lambda pe: pe_scores0(pe, G), lambda act: act_scores0(act, G), lambda dve: dve_scores0(dve, G), "scores 0"))
            out.append((lambda pe: pe_turn_probs0(pe, G),
                        lambda act: act_out(act, G, ("0", "pT"), G.oT[0:S, :], 0.0, ("pT", n, "0")), None, "turn 0"))
            out.append((lambda pe: pe_evidence(pe, G), lambda act: act_out(act, G, ("0", "ev"), G.rot[:], 0.0, ("ev", n)), None, "product"))

            def pe_logits(pe):
                pe.wait_ge(*done("ev", n))
                pe_product(pe, (n, "0", "lg"), [(w0r[:, 0, :], G.xn[:]), (w0r[:, 1, :], G.rot[:])])

            def dve_logits(dve):
                name = (n, "0", "lg")
                dve.wait_ge(*done("mm", name))
                dve.tensor_tensor(seqs(G.lg), seqs(tile(name)[0:4, 0:T]), per_seq(G, MROUTE)[0:4], ALU.add)\
                    .then_inc(*tick("dve", ("free", name), ("lg", n)))

            out.append((pe_logits, None, dve_logits, "product"))
            out.append((lambda pe: pe_route(pe, G), lambda act: act_route(act, G), lambda dve: dve_route(dve, G), "route"))
            out.append((lambda pe: pe_experts_in(pe, G), lambda act: act_experts_in(act, G), lambda dve: dve_experts_in(dve, G), "experts in"))
            out.append((lambda pe: pe_experts_out(pe, G), lambda act: act_experts_out(act, G), lambda dve: dve_experts_out(dve, G), "experts out"))

            def pe_out0(pe):
                pe.wait_ge(*done("routed", n, NE - 1))
                pe_product(pe, (n, "0", "out"), [(w0o[:], G.kT[:])])

            def dve_out0(dve):
                dve.wait_ge(*done("gate", n))
                dve_residual(dve, G, ("0", "out"), col("L0_xcond_out_b"), seqs(G.sq[:]), "0")

            out.append((pe_out0, None, dve_out0, "product"))

            for L, p in ((1, "L1_xcond_"), (2, "L2_xcond_"), (3, "L3_xcond_")):
                eps = 0 if L == 3 else 1
                s, c, a, b, m = (f"{L}{k}" for k in "sxabm")
                w, last = weights[L], f"{L - 1}"
                base = {1: M1, 2: M2, 3: M3}[L]
                na, nb, nm = {1: ((1, 0), None, (4, 3)), 2: ((1, 0), None, (4, 3)), 3: ((0, 1), (2, 3), (4, 5))}[L]
                na, nb, nm = ((base + i[0], base + i[1]) if i else (None, None) for i in (na, nb, nm))
                ga, gm = (per_seq(G, base + 2), per_seq(G, base + 5)) if L < 3 else (None, None)
                bias = {1: lambda k, i=0: col(p + {"q": "qkv_b", "proj": "sa_proj_b", "cq": "q_b", "ck": "kv_b", 
                                                   "cproj": "ca_proj_b"}[k], i),
                        2: lambda k, i=0: col(p + {"q": "b_qkv", "proj": "b_proj", "cq": "b_qc", "ck": "b_kvc", 
                                                   "cproj": "b_cproj"}[k], i)}.get(L)
                ctx_src, ctx_ready = (G.cn, ("xn", n, "2c")) if L == 2 else (G.cT, ("c", n))

                out += norm_stages(G, a, ("x", n, last), *na, G.xn, eps, G.x)
                out.append(queries(G, s, L, 0, ("xn", n, a), bias("q", 0) if bias else 0.0))
                out.append(keys(G, s, L, 0, G.xn, ("xn", n, a), bias("q", 1) if bias else None))
                out.append(values(G, s, L, 0, G.xn))
                out += attention_core(G, s, False, [keys(G, c, L, 1, ctx_src, ctx_ready, bias("ck") if bias else None)])
                out.append(values(G, c, L, 1, ctx_src))
                out.append(projection(G, s, w["proj"], bias("proj") if bias else None, ga))
                out += norm_stages(G, b, ("x", n, s), *nb, G.xn, eps, G.x)
                out.append(queries(G, c, L, 1, ("xn", n, b), bias("cq") if bias else 0.0))
                out += attention_core(G, c, L == 1, [])
                out.append(projection(G, c, w["cproj"], bias("cproj") if bias else None, None))
                out += norm_stages(G, m, ("x", n, c), *nm, G.xn, eps, G.x)
                b1, b2 = {1: ("fc1_b", "fc2_b"), 2: ("b_mlp1", "b_mlp2"), 3: ("ffn_b1", "ffn_b2")}[L]
                out += mlp_stages(G, m, L, ACT.Gelu_apprx_tanh if L == 2 else ACT.Gelu, p + b1, p + b2, gm, f"{L}",
                                  norm_stages(G, "2c", ("c", n), None, None, G.cn, 1, G.cT) if L == 1 else [])

            def pe_out(pe):
                pe.wait_ge(*done("x", n, "3"))
                b = ring.claim(pe, (n, "out"))
                for t in range(TT):
                    ins = pe.transpose(b[:, t * 128:(t + 1) * 128], G.x[:, t * 128:(t + 1) * 128], ident)
                ins.then_inc(*tick("pe", ("mm", (n, "out"))))

            out.append((pe_out, lambda act: act_out(act, G, ("out",), G.tmp[:, 0, :], 0.0, ("rows", n)), None, "turn out"))
            return out

        def order_of(i):
            left = [[stage for G in visits[g::NS] for stage in stages_of(G, i)] for g in range(NS)]
            ready, free, order = list(START), 0.0, []
            while any(left):
                g = min((g for g in range(NS) if left[g]), key=lambda g: ready[g])
                order.append(left[g].pop(0))
                busy, rest = PLAN[order[-1][3]]
                free = max(free, ready[g]) + busy
                ready[g] = free + rest
            return order

        with nc.Fori(0, NG // GI) as i:
            order = order_of(i)
            with nc.Block() as block:
                @block.sync
                def _(sp):
                    def load_next(G, group):
                        sp.wait_ge(*done("mm", (G.n, "in", "c")))
                        load_group(sp, G, group * T, rows_loaded[G.stream])

                    for G in visits[0:NS]:
                        load_next(G, i * GI + G.n + NS)
                    for G in visits:
                        sp.wait_ge(*done("rows", G.n))
                        sp.dma_start(out_rows[bass.ds((i * GI + G.n) * T, T), :].rearrange("(t p) d -> p t d", p=128),
                                     G.tmp[:, 0, :].rearrange("p (t d) -> p t d", d=D)).then_inc(stored[G.stream], 16)
                        if G.n + NS < GI:
                            load_next(visits[G.n + NS], (i * GI + G.n + 2 * NS) % NG)
                    for n in range(NS):
                        sp.wait_ge(stored[n], 16 * ROUNDS)
                        sp.wait_ge(rows_loaded[n], 32 * ROUNDS)

                @block.tensor
                def _(pe):
                    for stage in order:
                        if stage[0]:
                            stage[0](pe)

                @block.scalar
                def _(act):
                    act_tables(act, 6)
                    stages = [stage for stage in order if stage[1]]
                    for k, stage in enumerate(stages):
                        stage[1](act)
                        if stage[3] in ("experts in", "mlp in") and stages[k + 1][3] != stage[3]:
                            act_tables(act, 6)

                @block.vector
                def _(dve):
                    for stage in order:
                        if stage[2]:
                            stage[2](dve)

            nc.all_engine_barrier(sems_to_clear=counters)
    return st


_INS = ["x", "cond_1024", "ctx_1024", "mask_BxS2_bf0"] + list(COLS) + [
    "L0_xcond_Wq", "L0_xcond_Wk", "L0_xcond_Wv", "L0_xcond_router_W", "L0_xcond_router_b", "L0_xcond_e_w1", "L0_xcond_e_w2",
    "L0_xcond_gate_w1", "L0_xcond_gate_w2", "L0_xcond_out_w", "L1_xcond_ada_w", "L1_xcond_qkv_w", "L1_xcond_sa_proj_w",
    "L1_xcond_q_w", "L1_xcond_kv_w", "L1_xcond_ca_proj_w", "L1_xcond_fc1_w", "L1_xcond_fc2_w", "L2_xcond_W_mod",
    "L2_xcond_W_qkv", "L2_xcond_W_proj", "L2_xcond_W_qc", "L2_xcond_W_kvc", "L2_xcond_W_cproj", "L2_xcond_W_mlp1",
    "L2_xcond_W_mlp2", "L3_xcond_ln1_w", "L3_xcond_ln2_w", "L3_xcond_ln3_w", "L3_xcond_qkv_w", "L3_xcond_sa_out_w",
    "L3_xcond_q_w", "L3_xcond_k_w", "L3_xcond_v_w", "L3_xcond_ca_out_w", "L3_xcond_ffn_w1", "L3_xcond_ffn_w2"]


def kernel(**inputs):
    import concourse.bacc as bacc
    from concourse.bass_utils import run_bass_kernel_spmd

    arrays = {n: np.ascontiguousarray(inputs[n]) for n in _INS}
    arrays["consts"] = shape_constants()
    found, tiles = {}, {}
    for _ in range(2):
        nc = bacc.Bacc("TRN2", target_bir_lowering=False, num_devices=1)
        io = {n: nc.dram_tensor(f"in_{n}_dram", a.shape, mybir.dt.from_np(a.dtype), kind="ExternalInput").ap()
              for n, a in arrays.items()}
        io["out"] = nc.dram_tensor("out_0_dram", (B, S, D), F32, kind="ExternalOutput").ap()
        steps = build(nc, io, found, tiles)
        found, tiles = steps.found, steps.tiles
    r = run_bass_kernel_spmd(nc, [{f"in_{n}_dram": a for n, a in arrays.items()}], core_ids=[0])
    return r.results[0]["out_0_dram"]
```
